# Optimizing a Trainium2 kernel written in Bass

```python
import numpy as np
import jax
import jax.numpy as jnp

def _softmax(x, axis=-1):
    return jax.nn.softmax(x, axis=axis)

def _gelu(x):
    return jax.nn.gelu(x, approximate=True)

def _silu(x):
    return jax.nn.silu(x)

def _sigmoid(x):
    return jax.nn.sigmoid(x)

def _layernorm(x, axis=-1, eps=1e-05):
    m = jnp.mean(x, axis=axis, keepdims=True)
    v = jnp.var(x, axis=axis, keepdims=True)
    return (x - m) / jnp.sqrt(v + eps)

def _scatter_add(tgt, idx, src, axis=0):
    return tgt.at[idx].add(src)

def _segment_sum(src, seg, n):
    return jax.ops.segment_sum(src, seg, n)
kernel_name = 'mk_gnn_preln_d2_gnn_r8_e60010'

def setup_inputs(seed: int=0):
    np.random.seed(seed)
    _w = jnp.asarray

    def _rec_inputs():
        import jax
        import jax.numpy as jnp
        _gk = jax.random.key(seed)
        x = -0.0003713 + 1 * jax.random.normal(jax.random.fold_in(_gk, 1), (12500, 256), jnp.float32)
        src = jax.random.randint(jax.random.fold_in(_gk, 2), (200000,), 0, 12500, jnp.int32)
        dst = jax.random.randint(jax.random.fold_in(_gk, 3), (200000,), 0, 12500, jnp.int32)
        _o = jnp.argsort(dst, stable=True)
        src = src[_o]
        dst = dst[_o]
        edge_attr_3 = -1.09012e-05 + 0.99985 * jax.random.normal(jax.random.fold_in(_gk, 11), (200000, 3), jnp.float32)
        return (x, src, dst, edge_attr_3)
    x, src, dst, edge_attr_3 = _rec_inputs()

    def _L0_gnn_setup():
        import jax, jax.numpy as jnp
        import numpy as np
        N = 6250
        E = 50000
        IN = 256
        H = 8
        D = 32
        EF = 3
        key = jax.random.key(seed)
        ks = jax.random.split(key, 8)
        x = jax.random.normal(ks[0], (N, IN), dtype=jnp.float32)
        edge_index = jax.random.randint(ks[1], (2, E), 0, N, dtype=jnp.int64)
        edge_attr = jax.random.normal(ks[2], (E, EF), dtype=jnp.float32)
        W = jax.random.normal(ks[3], (H * D, IN), dtype=jnp.float32) * np.float32(np.sqrt(2.0 / (IN + H * D)))
        a_src = jax.random.normal(ks[4], (H, D), dtype=jnp.float32) * np.float32(np.sqrt(2.0 / (H + D)))
        a_dst = jax.random.normal(ks[5], (H, D), dtype=jnp.float32) * np.float32(np.sqrt(2.0 / (H + D)))
        edge_W = jax.random.normal(ks[6], (H * D, EF), dtype=jnp.float32) * np.float32(np.sqrt(2.0 / (EF + H * D)))
        edge_b = jnp.zeros((H * D,), dtype=jnp.float32)
        bias = jnp.zeros((H * D,), dtype=jnp.float32)
        return {'x': x, 'W': W, 'a_src': a_src, 'a_dst': a_dst, 'edge_W': edge_W, 'edge_b': edge_b, 'bias': bias, 'edge_attr': edge_attr, 'edge_index': edge_index}
    _L0_gnn_all = _L0_gnn_setup()
    _L0_gnn_in = {k: v for k, v in _L0_gnn_all.items() if k in ('W', 'a_src', 'a_dst', 'edge_W', 'edge_b', 'bias')}
    del _L0_gnn_all

    def _L1_gnn_setup():
        import jax, jax.numpy as jnp
        import numpy as np
        N_NODES = 12500
        BN_EPS = 1e-05

        def gcn_conv(x, src, dst, W, b, n):
            h = x @ W
            loop = jnp.arange(n, dtype=src.dtype)
            s = jnp.concatenate([src, loop])
            d = jnp.concatenate([dst, loop])
            deg = jax.ops.segment_sum(jnp.ones(s.shape, h.dtype), d, num_segments=n)
            dinv = jnp.where(deg > 0, jax.lax.rsqrt(jnp.maximum(deg, 1.0)), 0.0)
            norm = dinv[s] * dinv[d]
            msg = h[s] * norm[:, None]
            out = jax.ops.segment_sum(msg, d, num_segments=n)
            return out + b

        def batch_norm(x, gamma, beta):
            mean = jnp.mean(x, axis=0)
            var = jnp.mean(jnp.square(x - mean), axis=0)
            return (x - mean) * jax.lax.rsqrt(var + BN_EPS) * gamma + beta
        key = jax.random.key(seed)
        ks = jax.random.split(key, 10)
        d0, d1, d2 = (256, 128, 64)
        d_cat = d0 + d1 + d2
        inp = {'node_features': jax.random.normal(ks[0], (N_NODES, d0), jnp.float32), 'edge_idx': jax.random.randint(ks[1], (2, 200000), 0, N_NODES, jnp.int64), 'W1': jax.random.normal(ks[2], (d0, d1), jnp.float32) * (1.0 / np.sqrt(d0)), 'b1': jnp.zeros((d1,), jnp.float32), 'g1': jnp.ones((d1,), jnp.float32), 'be1': jnp.zeros((d1,), jnp.float32), 'W2': jax.random.normal(ks[3], (d1, d2), jnp.float32) * (1.0 / np.sqrt(d1)), 'b2': jnp.zeros((d2,), jnp.float32), 'g2': jnp.ones((d2,), jnp.float32), 'be2': jnp.zeros((d2,), jnp.float32), 'Wfc': jax.random.normal(ks[4], (d_cat, d0), jnp.float32) * (1.0 / np.sqrt(d_cat)), 'bfc': jnp.zeros((d0,), jnp.float32)}
        return inp
    _L1_gnn_all = _L1_gnn_setup()
    _L1_gnn_in = {k: v for k, v in _L1_gnn_all.items() if k in ('W1', 'b1', 'g1', 'be1', 'W2', 'b2', 'g2', 'be2', 'Wfc', 'bfc')}
    del _L1_gnn_all
    return {'x': x, 'src': src, 'dst': dst, 'edge_attr_3': edge_attr_3, 'L0_gnn_W': _L0_gnn_in['W'], 'L0_gnn_a_src': _L0_gnn_in['a_src'], 'L0_gnn_a_dst': _L0_gnn_in['a_dst'], 'L0_gnn_edge_W': _L0_gnn_in['edge_W'], 'L0_gnn_edge_b': _L0_gnn_in['edge_b'], 'L0_gnn_bias': _L0_gnn_in['bias'], 'L1_gnn_W1': _L1_gnn_in['W1'], 'L1_gnn_b1': _L1_gnn_in['b1'], 'L1_gnn_g1': _L1_gnn_in['g1'], 'L1_gnn_be1': _L1_gnn_in['be1'], 'L1_gnn_W2': _L1_gnn_in['W2'], 'L1_gnn_b2': _L1_gnn_in['b2'], 'L1_gnn_g2': _L1_gnn_in['g2'], 'L1_gnn_be2': _L1_gnn_in['be2'], 'L1_gnn_Wfc': _L1_gnn_in['Wfc'], 'L1_gnn_bfc': _L1_gnn_in['bfc']}

def reference(x, src, dst, edge_attr_3, L0_gnn_W, L0_gnn_a_src, L0_gnn_a_dst, L0_gnn_edge_W, L0_gnn_edge_b, L0_gnn_bias, L1_gnn_W1, L1_gnn_b1, L1_gnn_g1, L1_gnn_be1, L1_gnn_W2, L1_gnn_b2, L1_gnn_g2, L1_gnn_be2, L1_gnn_Wfc, L1_gnn_bfc):
    import jax
    import jax.numpy as jnp

    def _L0_gnn_ref(x, W, a_src, a_dst, edge_W, edge_b, bias, edge_attr, edge_index):
        import jax, jax.numpy as jnp
        import numpy as np
        N = 6250
        E = 50000
        IN = 256
        H = 8
        D = 32
        EF = 3
        n = x.shape[0]
        h = (x @ W.T).reshape(n, H, D)
        src, dst = (edge_index[0], edge_index[1])
        h_src = h[src]
        h_dst = h[dst]
        alpha = jnp.einsum('ehd,hd->eh', h_src, a_src) + jnp.einsum('ehd,hd->eh', h_dst, a_dst)
        enc = jax.nn.relu(edge_attr @ edge_W.T + edge_b).reshape(-1, H, D)
        alpha = alpha + jnp.sum(enc * h_dst, axis=-1)
        alpha = jnp.where(alpha >= 0, alpha, 0.2 * alpha)
        amax = jax.ops.segment_max(alpha, dst, num_segments=n)
        ex = jnp.exp(alpha - amax[dst])
        denom = jax.ops.segment_sum(ex, dst, num_segments=n)
        attn = ex / jnp.maximum(denom[dst], 1e-10)
        out = jax.ops.segment_sum(h_src * attn[..., None], dst, num_segments=n)
        return out.reshape(n, H * D) + bias

    def _L1_gnn_ref(node_features, edge_idx, W1, b1, g1, be1, W2, b2, g2, be2, Wfc, bfc):
        import jax, jax.numpy as jnp
        import numpy as np
        N_NODES = 12500
        BN_EPS = 1e-05

        def gcn_conv(x, src, dst, W, b, n):
            h = x @ W
            loop = jnp.arange(n, dtype=src.dtype)
            s = jnp.concatenate([src, loop])
            d = jnp.concatenate([dst, loop])
            deg = jax.ops.segment_sum(jnp.ones(s.shape, h.dtype), d, num_segments=n)
            dinv = jnp.where(deg > 0, jax.lax.rsqrt(jnp.maximum(deg, 1.0)), 0.0)
            norm = dinv[s] * dinv[d]
            msg = h[s] * norm[:, None]
            out = jax.ops.segment_sum(msg, d, num_segments=n)
            return out + b

        def batch_norm(x, gamma, beta):
            mean = jnp.mean(x, axis=0)
            var = jnp.mean(jnp.square(x - mean), axis=0)
            return (x - mean) * jax.lax.rsqrt(var + BN_EPS) * gamma + beta
        n = node_features.shape[0]
        src, dst = (edge_idx[0], edge_idx[1])
        feats = [node_features]
        x = node_features
        x = gcn_conv(x, src, dst, W1, b1, n)
        x = jax.nn.relu(batch_norm(x, g1, be1))
        feats.append(x)
        x = gcn_conv(x, src, dst, W2, b2, n)
        x = jax.nn.relu(batch_norm(x, g2, be2))
        feats.append(x)
        cat = jnp.concatenate(feats, axis=1)
        return jax.nn.relu(cat @ Wfc + bfc)
    edge_index = jnp.stack([src, dst])
    h = jnp.maximum(_layernorm(x, axis=-1), 0.0)
    x = x + _L0_gnn_ref(h, L0_gnn_W, L0_gnn_a_src, L0_gnn_a_dst, L0_gnn_edge_W, L0_gnn_edge_b, L0_gnn_bias, edge_attr_3, edge_index)
    h = jnp.maximum(_layernorm(x, axis=-1), 0.0)
    x = x + _L1_gnn_ref(h, edge_index, L1_gnn_W1, L1_gnn_b1, L1_gnn_g1, L1_gnn_be1, L1_gnn_W2, L1_gnn_b2, L1_gnn_g2, L1_gnn_be2, L1_gnn_Wfc, L1_gnn_bfc)
    return x

_drawn_inputs = setup_inputs


def setup_inputs(seed=0):
    import zlib

    import numpy as np

    out = dict(_drawn_inputs(seed))
    spreads = {'L0_gnn_edge_b': (0.0, 0.376),
     'L0_gnn_bias': (0.0, 0.1),
     'L1_gnn_b1': (0.0, 0.8),
     'L1_gnn_g1': (1.0, 0.2),
     'L1_gnn_be1': (0.0, 0.314),
     'L1_gnn_b2': (0.0, 0.8),
     'L1_gnn_g2': (1.0, 0.2),
     'L1_gnn_be2': (0.0, 0.474),
     'L1_gnn_bfc': (0.0, 0.1)}
    factors = {}
    for name, (base, spread) in spreads.items():
        noise = np.random.default_rng([zlib.crc32(name.encode()), seed]).standard_normal(out[name].shape)
        drawn = base * np.exp(spread * noise) if base else spread * noise
        out[name] = jnp.asarray(drawn.astype(out[name].dtype))
    for name, factor in factors.items():
        out[name] = (out[name] * factor).astype(out[name].dtype)
    return out
```

```python
from contextlib import ExitStack, contextmanager

import numpy as np

import concourse.bass as bass
from concourse import mybir
from concourse.bass import AP

F32 = mybir.dt.float32
BF16 = mybir.dt.bfloat16
I32 = mybir.dt.int32
ALU = mybir.AluOpType
ACT = mybir.ActivationFunctionType
AXX = mybir.AxisListType.X

P = 128
NODES, FEAT, EDGES = 12500, 256, 200000
HEADS, HDIM = 8, 32
F1, F2 = 128, 64
CHUNKS = -(-EDGES // P)
TILES = -(-NODES // P)
LAST = NODES - (TILES - 1) * P
Q = -(-(CHUNKS + TILES - 1) // P)
STEPS = Q * P
LANES = 16
ITERS = STEPS // LANES
PL = P // LANES
EROW = 6 * P
HROW = HEADS + FEAT + 1
HCOL = HROW + HEADS
DROW = HCOL - HEADS
H0, H1 = HEADS, HEADS + FEAT
GT = 7
GROUPS = TILES // GT
BIG = 1.0e30
EPS = 1.0e-5
PAD_DST = 20000
EPP = Q * P
FULL_P = EDGES // EPP
REST = EDGES - FULL_P * EPP


class Link:

    def __init__(self, eng, sem):
        self.eng, self.sem, self.base, self.n = eng, sem, 0, 0

    def __call__(self, ins):
        self.n += 1
        ins.then_inc(self.sem, 1)
        self.eng.wait_ge(self.sem, self.base + self.n)

    @contextmanager
    def loop(self, trips, links):
        start = self.base + self.n
        with self.eng.Fori(0, trips) as i:
            self.base, self.n = i * links + start, 0
            yield i
            assert self.n == links, (self.n, links)
        self.base, self.n = start + trips * links, 0


def take_waits(eng, held):
    eng.sem_inc(held, 1)


def spread(ap, dims):
    return AP(ap.tensor, ap.offset, [list(ap.ap[0])] + [list(d) for d in dims])


def gnn(nc, A, out):
    held = nc.alloc_semaphore(name="held")
    top = ExitStack()
    in_phase = []

    def sem(name):
        in_phase.append(nc.alloc_semaphore(name=name))
        return in_phase[-1]

    def end_phase():
        nc.clear_and_free_semaphores(in_phase)
        nc.all_engine_barrier()
        in_phase.clear()

    def pair(name):
        return [sem(name + "0"), sem(name + "1")]

    def dram(name, shape, dt=F32):
        return nc.dram_tensor(name, shape, dt, kind="Internal").ap()

    edge_rows = dram("edge_rows", (STEPS, EROW))
    chunk_end = dram("chunk_end", (STEPS,))
    tile_of = dram("tile_of", (STEPS,), I32)
    dloc_rows = dram("dloc_rows", (ITERS, LANES, P), BF16)
    attr_rows = dram("attr_rows", (ITERS, 3, LANES, P))
    start_rows = dram("start_rows", (STEPS, P))
    mask_rows = dram("mask_rows", (STEPS, P))
    gat_table = dram("gat_table", (TILES * P, HROW))
    gathered = dram("gathered", (ITERS, P, LANES * HROW))
    score_rows = dram("score_rows", (ITERS, P, LANES * HEADS))
    weight_rows = dram("weight_rows", (ITERS, P, LANES * HEADS))
    x1_rows = dram("x1_rows", (TILES * P, FEAT))
    conv1_table = dram("conv1_table", (TILES * P, F1))
    conv2_table = dram("conv2_table", (TILES * P, F2))

    def sb(ctx, name, shape, dt=F32):
        return ctx.enter_context(nc.sbuf_tensor(name, shape, dt))

    def ps(ctx, name, shape, dt=F32):
        return ctx.enter_context(nc.psum_tensor(name, shape, dt))

    with top:
        src_col = sb(top, "src_col", [P, STEPS], I32)
        dloc_col = sb(top, "dloc_col", [P, STEPS])
        tiles_row = sb(top, "tiles_row", [1, STEPS], I32)
        iota_row = sb(top, "iota_row", [P, P])
        part_id = sb(top, "part_id", [P, 1])
        ident = sb(top, "ident", [P, P])
        const = (src_col, dloc_col, tiles_row, iota_row, part_id, ident)

        steps_phase(nc, sb, ps, sem, A, const, edge_rows, chunk_end, tile_of, dloc_rows, attr_rows,
                    start_rows, mask_rows)
        end_phase()
        with ExitStack() as ctx:
            h_all = sb(ctx, "h_all", [P, TILES, HCOL])
            node_phase(nc, sb, ps, sem, pair, held, A, const, h_all, gat_table)
            end_phase()
            score_phase(nc, sb, ps, sem, pair, held, A, const, h_all, gat_table, gathered, dloc_rows,
                        attr_rows, score_rows)
            end_phase()
        softmax_phase(nc, sb, ps, sem, pair, held, const, start_rows, mask_rows, score_rows, weight_rows)
        end_phase()
        with ExitStack() as ctx:
            acc1 = sb(ctx, "acc1", [P, TILES, F1])
            dinv = sb(ctx, "dinv", [P, TILES])
            with ExitStack() as ctx2:
                acc = sb(ctx2, "acc", [P, TILES, HROW])
                gat_sum_phase(nc, sb, ps, sem, pair, held, const, acc, acc1[:, 0:LANES, :], gathered, weight_rows)
                end_phase()
                mid_phase(nc, sb, ps, sem, pair, held, A, const, acc, acc1, dinv, x1_rows, conv1_table)
                end_phase()
            conv_phase(nc, sb, ps, sem, pair, held, const, "c1", F1, acc1, conv1_table)
            end_phase()
            acc2 = sb(ctx, "acc2", [P, TILES, F2])
            norm_phase(nc, sb, ps, sem, A, const, "n1", F1, acc1, dinv,
                       A["L1_gnn_b1"], A["L1_gnn_g1"], A["L1_gnn_be1"])
            end_phase()
            project_phase(nc, sb, ps, sem, pair, A, const, acc1, acc2, dinv, conv2_table)
            end_phase()
            conv_phase(nc, sb, ps, sem, pair, held, const, "c2", F2, acc2, conv2_table)
            end_phase()
            norm_phase(nc, sb, ps, sem, A, const, "n2", F2, acc2, dinv,
                       A["L1_gnn_b2"], A["L1_gnn_g2"], A["L1_gnn_be2"])
            end_phase()
            final_phase(nc, sb, ps, sem, pair, held, A, const, acc1, acc2, x1_rows, out)
            end_phase()


def steps_phase(nc, sb, ps, sem, A, const, edge_rows, chunk_end, tile_of, dloc_rows, attr_rows,
                start_rows, mask_rows):
    src_col, dloc_col, tiles_row, iota_row, part_id, ident = const
    with ExitStack() as ctx:
        dst_i = sb(ctx, "dst_i", [P, EPP], I32)
        prev_i = sb(ctx, "prev_i", [P, EPP], I32)
        src_i = sb(ctx, "src_i", [P, EPP], I32)
        attr = sb(ctx, "attr", [P, EPP * 3])
        rows = sb(ctx, "rows", [P, Q, EROW])
        ends = sb(ctx, "ends", [P, STEPS])
        below = sb(ctx, "below", [P, STEPS])
        order_i = sb(ctx, "order_i", [P, Q], I32)
        order = sb(ctx, "order", [P, Q])
        last_i = sb(ctx, "last_i", [P, Q], I32)
        last = sb(ctx, "last", [P, Q])
        chunk = sb(ctx, "chunk", [P, Q])
        chunk_i = sb(ctx, "chunk_i", [P, Q], I32)
        tile = sb(ctx, "tile", [P, Q])
        tile_i = sb(ctx, "tile_i", [P, Q], I32)
        base = sb(ctx, "base", [P, Q])
        valid = sb(ctx, "valid", [P, Q, P])
        dclip = sb(ctx, "dclip", [P, Q, P])
        dclip16 = sb(ctx, "dclip16", [P, Q, P], BF16)
        iota_i = sb(ctx, "iota_i", [P, P], I32)
        part_i = sb(ctx, "part_i", [P, 1], I32)
        turn = ps(ctx, "turn_s", [P, 4, 512])
        s_pads, s_loads, s_rows, s_rows_out = sem("st_pads"), sem("st_loads"), sem("st_rows"), sem("st_rows_out")
        s_end, s_end_out, s_end_in = sem("st_end"), sem("st_end_out"), sem("st_end_in")
        s_chunk, s_step_rows, s_iota, s_ident = sem("st_chunk"), sem("st_step_rows"), sem("st_iota"), sem("st_ident")
        s_tile, s_tile_out, s_tile_in = sem("st_tile"), sem("st_tile_out"), sem("st_tile_in")
        s_clip = sem("st_clip")
        s_ready, s_out, s_turned, s_taken = sem("st_ready"), sem("st_out"), sem("st_turned"), sem("st_taken")
        s_dve = sem("st_dve")
        with nc.Block() as block:
            @block.sync
            def _(sp):
                sp.wait_ge(s_pads, 4)
                a3 = A["edge_attr_3"].rearrange("e f -> (e f)")
                for t, a, w in ((dst_i, A["dst"], 1), (src_i, A["src"], 1), (attr, a3, 3)):
                    sp.dma_start(t[0:FULL_P, :], a[0:FULL_P * EPP * w].rearrange("(p e) -> p e", e=EPP * w)).then_inc(s_loads, 16)
                    sp.dma_start(t[FULL_P:FULL_P + 1, 0:REST * w], a[FULL_P * EPP * w:].rearrange("(p e) -> p e", p=1)).then_inc(s_loads, 16)
                d = A["dst"]
                sp.dma_start(prev_i[0:1, 1:EPP], d[0:EPP - 1].rearrange("(p e) -> p e", p=1)).then_inc(s_loads, 16)
                sp.dma_start(prev_i[1:FULL_P, :], d[EPP - 1:FULL_P * EPP - 1].rearrange("(p e) -> p e", e=EPP)).then_inc(s_loads, 16)
                sp.dma_start(prev_i[FULL_P:FULL_P + 1, 0:REST], d[FULL_P * EPP - 1:EDGES - 1].rearrange("(p e) -> p e", p=1)).then_inc(s_loads, 16)
                sp.wait_ge(s_rows, 1)
                sp.dma_start(edge_rows.rearrange("(p q) e -> p q e", q=Q), rows[:, :, :]).then_inc(s_rows_out, 16)
                sp.wait_ge(s_end, 1)
                sp.dma_start(chunk_end.rearrange("(p q) -> p q", q=Q), last[:, :]).then_inc(s_end_out, 16)
                sp.wait_ge(s_end_out, 16)
                sp.dma_start(ends[:, :], AP(chunk_end.tensor, 0, [[0, P], [1, STEPS]])).then_inc(s_end_in, 16)
                sp.wait_ge(s_tile, 1)
                with nc.allow_non_contiguous_dma(reason="one small table"):
                    for b in range(LANES):
                        sp.dma_start(AP(tile_of.tensor, b, [[Q * LANES, PL], [LANES, Q], [1, 1]]),
                                     tile_i[b * PL:(b + 1) * PL, :].rearrange("p (q o) -> p q o", o=1)).then_inc(s_tile_out, 16)
                sp.wait_ge(s_tile_out, 16 * LANES)
                sp.dma_start(tiles_row[:, :], tile_of.rearrange("(o k) -> o k", o=1)).then_inc(s_tile_in, 16)
                sp.wait_ge(s_ready, 1)
                sp.dma_start(start_rows.rearrange("(p q) e -> p q e", q=Q), rows[:, :, 2 * P:3 * P]).then_inc(s_out, 16)
                sp.dma_start(mask_rows.rearrange("(p q) e -> p q e", q=Q), valid[:, :, :]).then_inc(s_out, 16)
                for b in range(LANES):
                    p = slice(b * PL, (b + 1) * PL)
                    sp.dma_start(AP(dloc_rows.tensor, b * P, [[Q * LANES * P, PL], [LANES * P, Q], [1, P]]),
                                 dclip16[p, :, :]).then_inc(s_out, 16)
                    for f in range(3):
                        sp.dma_start(AP(attr_rows.tensor, (f * LANES + b) * P, [[Q * 3 * LANES * P, PL], [3 * LANES * P, Q], [1, P]]),
                                     rows[p, :, (3 + f) * P:(4 + f) * P]).then_inc(s_out, 16)
                sp.wait_ge(s_tile_in, 16)
                sp.wait_ge(s_out, 16 * (2 + 4 * LANES))

            @block.gpsimd
            def _(pool):
                nc.gpsimd.memset(dst_i[:, :], PAD_DST).then_inc(s_pads, 1)
                nc.gpsimd.memset(src_i[:, :], 0).then_inc(s_pads, 1)
                nc.gpsimd.memset(attr[:, :], 0.0).then_inc(s_pads, 1)
                nc.gpsimd.memset(prev_i[:, :], -1).then_inc(s_pads, 1)
                nc.gpsimd.iota(order_i[:, :], pattern=[[1, Q]], base=0, channel_multiplier=Q).then_inc(s_iota, 1)
                nc.gpsimd.iota(iota_i[:, :], pattern=[[1, P]], base=0, channel_multiplier=0).then_inc(s_iota, 1)
                nc.gpsimd.iota(part_i[:, :], pattern=[[0, 1]], base=0, channel_multiplier=1).then_inc(s_iota, 1)
                nc.gpsimd.memset(ident[:, :], 0.0).then_inc(s_ident, 1)
                pool.wait_ge(s_ident, 1)
                nc.gpsimd.affine_select(out=ident[:, :], in_=ident[:, :], compare_op=ALU.not_equal, fill=1.0,
                                        base=0, pattern=[[-1, P]], channel_multiplier=1).then_inc(s_ident, 1)
                pool.wait_ge(s_rows_out, 16)
                pool.wait_ge(s_chunk, 1)
                for q in range(Q):
                    pool.indirect_dma_start(rows[:, q, :], None, edge_rows,
                                            bass.IndirectOffsetOnAxis(chunk_i[:, q:q + 1], 0)).then_inc(s_step_rows, 16)

            @block.vector
            def _(dve):
                link = Link(dve, s_dve)
                dve.wait_ge(s_iota, 3)
                nc.vector.tensor_copy(iota_row[:, :], iota_i[:, :])
                nc.vector.tensor_copy(part_id[:, :], part_i[:, :])
                nc.vector.tensor_copy(order[:, :], order_i[:, :])
                dve.wait_ge(s_loads, 16 * 9)
                link(nc.vector.tensor_scalar(last_i[:, :], dst_i[:, :].rearrange("p (q e) -> p q e", e=P)[:, :, P - 1],
                                             7, None, ALU.arith_shift_right))
                link(nc.vector.tensor_scalar(last[:, :], last_i[:, :], float(TILES - 1), None, ALU.min))
                nc.vector.tensor_tensor(last[:, :], last[:, :], order[:, :], ALU.add).then_inc(s_end, 1)
                for n, t in enumerate((src_i, dst_i, prev_i)):
                    nc.vector.tensor_copy(rows[:, :, n * P:(n + 1) * P], t[:, :].rearrange("p (q e) -> p q e", e=P))
                for f in range(3):
                    i = nc.vector.tensor_copy(rows[:, :, (3 + f) * P:(4 + f) * P],
                                              attr[:, :].rearrange("p (q e f) -> p q e f", e=P, f=3)[:, :, :, f])
                i.then_inc(s_rows, 1)
                dve.wait_ge(s_end_in, 16)
                for q in range(Q):
                    link(nc.vector.tensor_scalar(below[:, :], ends[:, :], order[:, q:q + 1], None, ALU.is_lt))
                    link(nc.vector.reduce_sum(chunk[:, q:q + 1], below[:, :], AXX))
                nc.vector.tensor_copy(chunk_i[:, :], chunk[:, :]).then_inc(s_chunk, 1)
                link(nc.vector.tensor_tensor(tile[:, :], order[:, :], chunk[:, :], ALU.subtract))
                nc.vector.tensor_copy(tile_i[:, :], tile[:, :]).then_inc(s_tile, 1)
                link(nc.vector.tensor_scalar(base[:, :], tile[:, :], float(P), None, ALU.mult))
                dve.wait_ge(s_step_rows, 16 * Q)
                link(nc.vector.tensor_tensor(rows[:, :, P:2 * P], rows[:, :, P:2 * P], spread(base[:, :], [[1, Q], [0, P]]), ALU.subtract))
                link(nc.vector.tensor_tensor(rows[:, :, 2 * P:3 * P], rows[:, :, 2 * P:3 * P], spread(base[:, :], [[1, Q], [0, P]]), ALU.subtract))
                link(nc.vector.tensor_scalar(valid[:, :, :], rows[:, :, P:2 * P], float(P - 1), None, ALU.is_le))
                link(nc.vector.scalar_tensor_tensor(valid[:, :, :], rows[:, :, P:2 * P], 0.0, valid[:, :, :], ALU.is_ge, ALU.mult))
                link(nc.vector.tensor_scalar(dclip[:, :, :], rows[:, :, P:2 * P], -1.0, float(P), ALU.max, ALU.min))
                dve.sem_inc(s_clip, 1)
                link(nc.vector.tensor_copy(dclip16[:, :, :], dclip[:, :, :]))
                link(nc.vector.tensor_tensor(rows[:, :, 2 * P:3 * P], rows[:, :, P:2 * P], rows[:, :, 2 * P:3 * P], ALU.not_equal))
                link(nc.vector.scalar_tensor_tensor(rows[:, :, 2 * P:3 * P], rows[:, :, 2 * P:3 * P], -BIG, valid[:, :, :], ALU.mult, ALU.mult))
                nc.vector.tensor_scalar(valid[:, :, :], valid[:, :, :], BIG, -BIG, ALU.mult, ALU.add).then_inc(s_ready, 1)

            @block.tensor
            def _(pe):
                pe.wait_ge(s_ident, 2)
                pe.wait_ge(s_step_rows, 16 * Q)
                for n in range(2 * Q):
                    if n == Q:
                        pe.wait_ge(s_clip, 1)
                    if n >= 4:
                        pe.wait_ge(s_taken, n - 3)
                    rows_n = rows[:, n, 0:P] if n < Q else dclip[:, n - Q, :]
                    nc.tensor.transpose(turn[:, n % 4, 0:P], rows_n, ident[:, :]).then_inc(s_turned, 1)

            @block.scalar
            def _(act):
                views = [t[:, :].rearrange("e (pl q b) -> e q b pl", q=Q, b=LANES) for t in (src_col, dloc_col)]
                for n in range(2 * Q):
                    act.wait_ge(s_turned, n + 1)
                    nc.scalar.copy(views[n // Q][:, n % Q, :, :],
                                   turn[:, n % 4, 0:P].rearrange("e (b pl) -> e b pl", pl=PL)).then_inc(s_taken, 1)


def load_groups(sp, src, xg, s_in, waits, rows, stores=None):
    def load(g, u):
        r = g * (GT * P)
        full = GT - 1
        sp.dma_start(xg[u][:, 0:full, :], src[bass.ds(r, full * P), :].rearrange("(a p) c -> p a c", p=P)).then_inc(s_in[u], 16)
        n = P if not isinstance(g, int) else min(P, rows - g * GT * P - full * P)
        sp.dma_start(xg[u][0:n, full, :], src[bass.ds(r + full * P, n), :]).then_inc(s_in[u], 16)

    load(0, 0)
    load(1, 1)
    half = GROUPS // 2
    with sp.Fori(0, half - 2) as i:
        for u in range(2):
            waits(2 * i + u, u, i)
            load(2 * i + u + 2, u)
    for g in range(GROUPS - 4, GROUPS):
        waits(g, g % 2, g // 2)
        if g + 2 < GROUPS:
            load(g + 2, g % 2)


def dense_phase(nc, sb, ps, sem, pair, held, const, name, ctx, src, rows, weights, nout, w_ready,
                pre=None, pre_links=0, extra=(), finish_act=None, act_store=None, finish_dve=None,
                hold=None, act_first=None, pool=None, tensor_before=None, dve_before=None, sync_before=None):
    ident = const[5]
    xg = [sb(ctx, f"{name}_x{u}", [P, GT, FEAT]) for u in range(2)]
    hn = sb(ctx, f"{name}_hn", [P, GT, FEAT])
    ys = [[sb(ctx, f"{name}_y{n}{r}", [P, w]) for n, (_, w) in enumerate(extra)] for r in range(2)]
    nk = 2 + len(extra)
    hT = [sb(ctx, f"{name}_hT{r}", [P, nk, P]) for r in range(2)]
    stats = sb(ctx, f"{name}_stats", [P, GT, 6])
    mv = sb(ctx, f"{name}_mv", [P, GT, 2])
    var = sb(ctx, f"{name}_var", [P, GT])
    sd = sb(ctx, f"{name}_sd", [P, GT])
    rstd = [sb(ctx, f"{name}_rstd{u}", [P, GT]) for u in range(2)]
    shift = [sb(ctx, f"{name}_shift{u}", [P, GT]) for u in range(2)]
    tp = [ps(ctx, f"{name}_tp{r}", [P, 4, P]) for r in range(2)]
    op = [ps(ctx, f"{name}_op{r}", [P, 512]) for r in range(2)]
    x_in = pair(f"{name}_x_in")
    s_var, s_sd, s_norm = sem(f"{name}_var_ready"), sem(f"{name}_sd_ready"), sem(f"{name}_norm_ready")
    relu_done, turn_done = sem(f"{name}_relu_done"), sem(f"{name}_turn_done")
    copy_done, product_done = sem(f"{name}_copy_done"), sem(f"{name}_product_done")
    finish_done = sem(f"{name}_finish_done")
    s_dve = sem(f"{name}_dve")
    stored = pair(f"{name}_stored")
    half = GROUPS // 2
    with nc.Block() as block:
        @block.sync
        def _(sp):
            if sync_before:
                sync_before(sp)

            def waits(g, u, i):
                sp.wait_ge(relu_done, GT * (g + 1) + 2 * GT)
                take_waits(sp, held)
                if hold:
                    hold(sp, g, u, i, xg, finish_done, stored)
            load_groups(sp, src, xg, x_in, waits, rows)

        if pool:
            @block.gpsimd
            def _(p):
                pool(p)

        @block.vector
        def _(dve):
            link = Link(dve, s_dve)
            dve.sem_inc(relu_done, 2 * GT)
            dve.sem_inc(turn_done, GT)
            dve.sem_inc(copy_done, 2)
            dve.sem_inc(product_done, 2)
            dve.sem_inc(finish_done, 2)
            if dve_before:
                dve_before(dve, link)
            with link.loop(half, 2 * (4 + pre_links + (GT if finish_dve else 0))) as i:
                for u in range(2):
                    g = 2 * i + u
                    dve.wait_ge(x_in[u], 32 * (i + 1))
                    if pre:
                        pre(dve, link, g, u, i, xg)
                    for a in range(GT):
                        last = nc.vector.bn_stats(stats[:, a, :], xg[u][:, a, :])
                    link(last)
                    take_waits(dve, held)
                    for a in range(GT):
                        last = nc.vector.bn_aggr(mv[:, a, :], stats[:, a, :])
                    link(last)
                    dve.wait_ge(s_sd, g)
                    nc.vector.tensor_scalar(var[:, :], mv[:, :, 1], EPS, None, ALU.add).then_inc(s_var, 1)
                    dve.wait_ge(s_sd, g + 1)
                    dve.wait_ge(relu_done, GT * (g + 1))
                    link(nc.vector.reciprocal(rstd[u][:, :], sd[:, :]))
                    link(nc.vector.scalar_tensor_tensor(shift[u][:, :], mv[:, :, 0], -1.0, rstd[u][:, :], ALU.mult, ALU.mult))
                    dve.sem_inc(s_norm, 1)

                    def finish(a):
                        n = g * GT + a
                        dve.wait_ge(product_done, n + 3)
                        finish_dve(dve, link, i, u, a, op[(u * GT + a) % 2], xg, finish_done)

                    for a in range(GT):
                        n, r = g * GT + a, (u * GT + a) % 2
                        dve.wait_ge(turn_done, n + 1 + GT)
                        dve.wait_ge(product_done, n + 1)
                        w = min(nk, 3)
                        last = nc.vector.tensor_copy(hT[r][:, 0:w, :], tp[r][:, 0:w, :])
                        if nk == 4:
                            last = nc.vector.tensor_copy(hT[r][0:F2, 3, :], tp[r][0:F2, 3, :])
                        last.then_inc(copy_done, 1)
                        if finish_dve and a:
                            finish(a - 1)
                    if finish_dve:
                        finish(GT - 1)

        @block.scalar
        def _(act):
            with act.Fori(0, half) as i:
                for u in range(2):
                    g = 2 * i + u
                    if act_first:
                        act_first(act, g, u)
                    act.wait_ge(s_var, g + 1)
                    act.wait_ge(s_norm, g)
                    nc.scalar.activation(sd[:, :], var[:, :], ACT.Sqrt).then_inc(s_sd, 1)
                    act.wait_ge(s_norm, g + 1)
                    for a in range(GT):
                        n, r = g * GT + a, (u * GT + a) % 2
                        act.wait_ge(turn_done, n + (GT - 1 if extra else 1))
                        for y, (s, w) in zip(ys[r], extra):
                            nc.scalar.activation(y[:, :], s[:, :, :].rearrange("p t c -> p (t c)")[:, bass.ds(n * w, w)], ACT.Relu)
                        nc.scalar.activation(hn[:, a, :], xg[u][:, a, :], ACT.Relu, bias=shift[u][:, a:a + 1],
                                             scale=rstd[u][:, a:a + 1]).then_inc(relu_done, 1)
                    if finish_act:
                        for a in range(GT):
                            act.wait_ge(product_done, g * GT + a + 3)
                            finish_act(act, g, u, a, op[(u * GT + a) % 2], finish_done)
                        act.wait_ge(finish_done, (g + 1) * GT + 2)
                        act_store(act, g, u, stored)
            if finish_act:
                for u in range(2):
                    act.wait_ge(stored[u], 16 * half)

        @block.tensor
        def _(pe):
            if tensor_before:
                tensor_before(pe)
            w_ready(pe)
            with pe.Fori(0, half) as i:
                for u in range(2):
                    for a in range(GT):
                        n, r = (2 * i + u) * GT + a, (u * GT + a) % 2
                        pe.wait_ge(relu_done, n + 1 + 2 * GT)
                        pe.wait_ge(copy_done, n + 1)
                        pieces = [hn[:, a, 0:P], hn[:, a, P:2 * P]] + [y[:, :] for y in ys[r]]
                        for c, piece in enumerate(pieces):
                            w = piece.shape[1]
                            last = nc.tensor.transpose(tp[r][0:w, c, :], piece, ident[:, :])
                        last.then_inc(turn_done, 1)
                        pe.wait_ge(copy_done, n + 3)
                        pe.wait_ge(finish_done, n + 1)
                        for c in range(nk):
                            k = weights[c].shape[0]
                            last = nc.tensor.matmul(op[r][:, 0:nout], hT[r][0:k, c, :], weights[c],
                                                    start=c == 0, stop=c == nk - 1)
                        last.then_inc(product_done, 1)


def node_phase(nc, sb, ps, sem, pair, held, A, const, h_all, gat_table):
    ident = const[5]
    with ExitStack() as ctx:
        w_sb = sb(ctx, "w_sb", [P, 2, FEAT])
        score = sb(ctx, "score", [P, 2, 2])
        heads = sb(ctx, "heads", [P, 2, 2 * HEADS])
        w_t = sb(ctx, "w_t", [P, 2, HCOL])
        wp = ps(ctx, "wp", [P, 4, 512])
        s_w, s_heads, s_zero = sem("nd_w"), sem("nd_heads"), sem("nd_zero")
        s_wturn, s_wcopy = sem("nd_wturn"), sem("nd_wcopy")

        def sync_before(sp):
            sp.dma_start(w_sb[:, :, :], A["L0_gnn_W"].rearrange("(c p) k -> p c k", p=P)).then_inc(s_w, 16)
            with nc.allow_non_contiguous_dma(reason="two vectors"):
                for n, a in enumerate((A["L0_gnn_a_src"], A["L0_gnn_a_dst"])):
                    sp.dma_start(score[:, n, :], a.rearrange("h d -> (h d)").rearrange("(c p) -> p c", p=P)).then_inc(s_w, 16)

        def dve_before(dve, link):
            nc.vector.memset(h_all[:, :, H1:H1 + 1], 1.0)
            nc.vector.memset(w_t[:, :, H1:H1 + 1], 0.0)
            link(nc.vector.memset(heads[:, :, :], 0.0))
            dve.wait_ge(s_w, 48)
            for n in range(2):
                for c in range(2):
                    for q in range(4):
                        col = n * HEADS + c * 4 + q
                        last = nc.vector.tensor_copy(heads[q * HDIM:(q + 1) * HDIM, c, col:col + 1],
                                                     score[q * HDIM:(q + 1) * HDIM, n, c:c + 1])
            last.then_inc(s_heads, 1)
            for n in range(4):
                dve.wait_ge(s_wturn, n + 1)
                last = nc.vector.tensor_copy(w_t[:, n % 2, H0 + n // 2 * P:H0 + (n // 2 + 1) * P], wp[:, n, 0:P])
            last.then_inc(s_wcopy, 1)
            for c in range(2):
                dve.wait_ge(s_wturn, 5 + c)
                nc.vector.tensor_copy(w_t[:, c, 0:HEADS], wp[:, c, P:P + HEADS])
                last = nc.vector.tensor_copy(w_t[:, c, HROW:HCOL], wp[:, c, P + HEADS:P + 2 * HEADS])
            last.then_inc(s_wcopy, 1)

        def tensor_before(pe):
            pe.wait_ge(s_w, 48)
            for n in range(4):
                nc.tensor.transpose(wp[:, n, 0:P], w_sb[:, n // 2, n % 2 * P:(n % 2 + 1) * P], ident[:, :]).then_inc(s_wturn, 1)
            pe.wait_ge(s_heads, 1)
            pe.wait_ge(s_wcopy, 1)
            for c in range(2):
                for k in range(2):
                    last = nc.tensor.matmul(wp[:, c, P:P + 2 * HEADS], w_sb[:, k, c * P:(c + 1) * P], heads[:, k, :],
                                            start=k == 0, stop=k == 1)
                last.then_inc(s_wturn, 1)

        def finish_act(act, g, u, a, op, done):
            nc.scalar.copy(h_all[:, :, :].rearrange("p t c -> p (t c)")[:, bass.ds((g * GT + a) * HCOL, H1)], op[:, 0:H1])
            nc.scalar.copy(h_all[:, :, :].rearrange("p t c -> p (t c)")[:, bass.ds((g * GT + a) * HCOL + HROW, HEADS)],
                           op[:, HROW:HCOL]).then_inc(done, 1)

        def act_store(act, g, u, stored):
            act.dma_start(gat_table[bass.ds(g * (GT * P), GT * P), :].rearrange("(a p) c -> p a c", p=P),
                          h_all[:, bass.ds(g * GT, GT), 0:HROW]).then_inc(stored[u], 16)

        dense_phase(nc, sb, ps, sem, pair, held, const, "nd", ctx, A["x"], NODES, [w_t[:, 0, :], w_t[:, 1, :]], HCOL,
                    lambda pe: pe.wait_ge(s_wcopy, 2), finish_act=finish_act, act_store=act_store,
                    tensor_before=tensor_before, dve_before=dve_before, sync_before=sync_before)


def score_phase(nc, sb, ps, sem, pair, held, A, const, h_all, gat_table, gathered, dloc_rows, attr_rows, score_rows):
    src_col, dloc_col, tiles_row, iota_row, part_id, ident = const
    PAIRS = LANES // 2
    with ExitStack() as ctx:
        idx = [sb(ctx, f"sc_idx{u}", [P, LANES], I32) for u in range(2)]
        G = [sb(ctx, f"sc_g{u}", [P, LANES, HROW]) for u in range(2)]
        dl = [sb(ctx, f"sc_dl{u}", [P, LANES * P], BF16) for u in range(2)]
        att = [sb(ctx, f"sc_att{u}", [4, LANES * P]) for u in range(2)]
        ew = sb(ctx, "sc_ew", [4, FEAT])
        onehot = [sb(ctx, f"sc_onehot{r}", [P, 2 * P]) for r in range(2)]
        enc = [sb(ctx, f"sc_enc{r}", [P, 2, FEAT]) for r in range(2)]
        prod = [sb(ctx, f"sc_prod{r}", [P, 2, FEAT]) for r in range(2)]
        dots = sb(ctx, "sc_dots", [P, LANES * HEADS])
        dsts = sb(ctx, "sc_dsts", [P, LANES * HEADS])
        score = [sb(ctx, f"sc_score{u}", [P, LANES * HEADS]) for u in range(2)]
        enc_p = [ps(ctx, f"sc_encp{r}", [P, 2, FEAT]) for r in range(2)]
        dst_p = [ps(ctx, f"sc_dstp{r}", [P, 2, 512]) for r in range(2)]
        s_w, s_ones = sem("sc_w"), sem("sc_ones")
        idx_ready, rows_in, rows_out, score_out = pair("sc_idx_ready"), pair("sc_rows_in"), pair("sc_rows_out"), pair("sc_score_out")
        dl_in, att_in = pair("sc_dl_in"), pair("sc_att_in")
        onehot_done = sem("sc_onehot_done")
        enc_done = sem("sc_enc_done")
        relu_done, dst_done = sem("sc_relu_done"), sem("sc_dst_done")
        prod_done, read_done = sem("sc_prod_done"), sem("sc_read_done")
        score_done = sem("sc_score_done")
        s_dve = sem("sc_dve")
        half = ITERS // 2
        with nc.Block() as block:
            @block.sync
            def _(sp):
                with nc.allow_non_contiguous_dma(reason="a small matrix"):
                    sp.dma_start(ew[0:3, :], A["L0_gnn_edge_W"].rearrange("k f -> f k")).then_inc(s_w, 16)
                sp.dma_start(ew[3:4, :], A["L0_gnn_edge_b"].rearrange("(o k) -> o k", o=1)).then_inc(s_w, 16)
                sp.wait_ge(s_ones, 2)

                def load(m, u):
                    sp.dma_start(dl[u][:, :], AP(dloc_rows.tensor, m * (LANES * P), [[0, P], [1, LANES * P]])).then_inc(dl_in[u], 16)
                    sp.dma_start(att[u][0:3, :], attr_rows[bass.ds(m, 1), :, :, :].rearrange("o f b l -> (o f) (b l)")).then_inc(att_in[u], 16)

                def store(m, u, i):
                    sp.wait_ge(rows_in[u], 16 * LANES * (i + 1))
                    take_waits(sp, held)
                    sp.dma_start(gathered[bass.ds(m, 1), :, :].rearrange("o p c -> (o p) c"),
                                 G[u][:, :, :].rearrange("p b c -> p (b c)")).then_inc(rows_out[u], 16)
                    sp.wait_ge(score_done, m + 3)
                    take_waits(sp, held)
                    sp.dma_start(score_rows[bass.ds(m, 1), :, :].rearrange("o p c -> (o p) c"), score[u][:, :]).then_inc(score_out[u], 16)

                load(0, 0)
                load(1, 1)
                with sp.Fori(0, half - 1) as i:
                    for u in range(2):
                        m = 2 * i + u
                        store(m, u, i)
                        sp.wait_ge(onehot_done, PAIRS * (m + 1))
                        take_waits(sp, held)
                        sp.wait_ge(dst_done, PAIRS * (m + 1) + 2)
                        take_waits(sp, held)
                        load(m + 2, u)
                for u in range(2):
                    store(ITERS - 2 + u, u, half - 1)
                for u in range(2):
                    sp.wait_ge(rows_out[u], 16 * half)
                    sp.wait_ge(score_out[u], 16 * half)

            @block.gpsimd
            def _(pool):
                for u in range(2):
                    nc.gpsimd.memset(att[u][:, :], 1.0).then_inc(s_ones, 1)
                with pool.Fori(0, half) as i:
                    for u in range(2):
                        pool.wait_ge(idx_ready[u], i + 1)
                        pool.wait_ge(rows_out[u], 16 * i)
                        pool.wait_ge(score_done, 2 * i + u + 1)
                        take_waits(pool, held)
                        for b in range(LANES):
                            pool.indirect_dma_start(G[u][:, b, :], None, gat_table,
                                                    bass.IndirectOffsetOnAxis(idx[u][:, b:b + 1], 0)).then_inc(rows_in[u], 16)

            @block.scalar
            def _(act):
                act.sem_inc(prod_done, 2)
                act.sem_inc(relu_done, 2)
                with act.Fori(0, half) as i:
                    for u in range(2):
                        m = 2 * i + u
                        act.wait_ge(rows_in[u], 16 * LANES * i)
                        nc.scalar.copy(idx[u][:, :], src_col[:, bass.ds(m * LANES, LANES)]).then_inc(idx_ready[u], 1)
                        for q in range(PAIRS):
                            n, r = m * PAIRS + q, q % 2
                            act.wait_ge(enc_done, n + 1)
                            act.wait_ge(prod_done, n + 1)
                            nc.scalar.activation(enc[r][:, :, :], enc_p[r][:, :, :], ACT.Relu).then_inc(relu_done, 1)

            @block.vector
            def _(dve):
                link = Link(dve, s_dve)
                dve.sem_inc(dst_done, 2)
                dve.sem_inc(read_done, 2)
                dve.sem_inc(score_done, 2)
                with link.loop(half, 2 * (PAIRS + 3)) as i:
                    for u in range(2):
                        m = 2 * i + u

                        def product(q):
                            n, r = m * PAIRS + q, q % 2
                            dve.wait_ge(relu_done, n + 3)
                            dve.wait_ge(dst_done, n + 3)
                            nc.vector.tensor_tensor(prod[r][:, :, :], enc[r][:, :, :], dst_p[r][:, :, 0:FEAT], ALU.mult).then_inc(prod_done, 1)
                            nc.vector.tensor_copy(dsts[:, 2 * q * HEADS:2 * (q + 1) * HEADS].rearrange("p (s h) -> p s h", s=2),
                                                  dst_p[r][:, :, FEAT + 1:DROW]).then_inc(read_done, 1)
                            dve.wait_ge(prod_done, n + 3)
                            link(nc.vector.reduce_sum(dots[:, 2 * q * HEADS:2 * (q + 1) * HEADS],
                                                      prod[r][:, :, :].rearrange("p s (h d) -> p (s h) d", d=HDIM), AXX))

                        dve.wait_ge(dl_in[u], 16 * (i + 1))
                        for q in range(PAIRS):
                            n, r = m * PAIRS + q, q % 2
                            dve.wait_ge(dst_done, n + 1)
                            nc.vector.tensor_scalar(onehot[r][:, :], dl[u][:, 2 * q * P:2 * (q + 1) * P], part_id[:, 0:1], None,
                                                    ALU.is_equal).then_inc(onehot_done, 1)
                            if q:
                                product(q - 1)
                        product(PAIRS - 1)
                        dve.wait_ge(read_done, PAIRS * (m + 1) + 2)
                        link(nc.vector.tensor_tensor(dots[:, :], dots[:, :], dsts[:, :], ALU.add))
                        dve.wait_ge(rows_in[u], 16 * LANES * (i + 1))
                        dve.wait_ge(score_out[u], 16 * i)
                        link(nc.vector.tensor_tensor(dots[:, :].rearrange("p (b h) -> p b h", h=HEADS),
                                                     dots[:, :].rearrange("p (b h) -> p b h", h=HEADS), G[u][:, :, 0:HEADS], ALU.add))
                        link(nc.vector.scalar_tensor_tensor(score[u][:, :], dots[:, :], 0.2, dots[:, :], ALU.mult, ALU.max))
                        dve.sem_inc(score_done, 1)

            @block.tensor
            def _(pe):
                pe.wait_ge(s_w, 32)
                flat = h_all[:, :, :].rearrange("p t c -> p (t c)")
                with pe.Fori(0, half) as i:
                    for u in range(2):
                        m = 2 * i + u
                        _, tiles = nc.values_load_multi_w_load_instructions(
                            tiles_row[0:1, bass.ds(m * LANES, LANES)], engines=[mybir.EngineType.PE], min_val=0, max_val=TILES - 1,
                            skip_runtime_bounds_check_because="tile numbers are clamped where they are worked out")
                        pe.wait_ge(att_in[u], 16 * (i + 1))
                        for q in range(PAIRS):
                            n, r = m * PAIRS + q, q % 2
                            pe.wait_ge(relu_done, n + 1)
                            for s in range(2):
                                b = 2 * q + s
                                last = nc.tensor.matmul(enc_p[r][:, s, :], att[u][:, b * P:(b + 1) * P], ew[:, :], start=True, stop=True)
                            last.then_inc(enc_done, 1)
                            pe.wait_ge(onehot_done, n + 1)
                            pe.wait_ge(read_done, n + 1)
                            for s in range(2):
                                last = nc.tensor.matmul(dst_p[r][:, s, 0:DROW], onehot[r][:, s * P:(s + 1) * P],
                                                        flat[:, bass.ds(tiles[2 * q + s] * HCOL + HEADS, DROW)], start=True, stop=True)
                            last.then_inc(dst_done, 1)


def softmax_phase(nc, sb, ps, sem, pair, held, const, start_rows, mask_rows, score_rows, weight_rows):
    ident = const[5]
    COLS = ITERS * P
    J = 4
    TURNS = ITERS // J
    PIECE = 1024


    def backwards(t, hi, lo):
        return t[:, hi - 1:lo - 1:-1] if lo else t[:, hi - 1::-1]

    with ExitStack() as ctx:
        alpha = sb(ctx, "alpha", [P, COLS])
        start = sb(ctx, "start", [P, COLS + 1])
        top = sb(ctx, "top", [P, COLS])
        buf = [sb(ctx, f"sm_buf{u}", [P, J, P]) for u in range(2)]
        dump = [sb(ctx, f"sm_dump{u}", [P, PIECE]) for u in range(2)]
        weight = [sb(ctx, f"sm_weight{u}", [P, J * P]) for u in range(2)]
        any_start = sb(ctx, "any_start", [P, 1])
        carry = sb(ctx, "carry", [P, 1])
        line = sb(ctx, "line", [1, 3, P])
        turn = [ps(ctx, f"sm_turn{u}", [P, 512]) for u in range(2)]
        small = ps(ctx, "sm_small", [P, 3, P])
        s_flags, s_edge = sem("sm_flags"), sem("sm_edge")
        buf_in, buf_out = pair("sm_buf_in"), pair("sm_buf_out")
        turned, added = sem("sm_turned"), sem("sm_added")
        back, copied = sem("sm_back"), sem("sm_copied")
        s_dve, s_line, s_diff, s_exp = sem("sm_dve"), sem("sm_line"), sem("sm_diff"), sem("sm_exp")
        s_sum, s_pe = sem("sm_sum"), sem("sm_pe")
        half = TURNS // 2
        with nc.Block() as block:
            @block.sync
            def _(sp):
                for b in range(LANES):
                    o = b * COLS
                    p = slice(b * HEADS, (b + 1) * HEADS)
                    sp.dma_start(top[p, :], AP(mask_rows.tensor, o, [[0, HEADS], [1, COLS]])).then_inc(s_flags, 16)
                for u in range(2):
                    sp.dma_start(buf[u][:, :, :], score_rows[u * J:(u + 1) * J, :, :].rearrange("j e c -> e j c")).then_inc(buf_in[u], 16)
                with sp.Fori(0, half - 1) as i:
                    for u in range(2):
                        g = 2 * i + u
                        sp.wait_ge(turned, g + 1)
                        take_waits(sp, held)
                        sp.dma_start(buf[u][:, :, :], score_rows[bass.ds((g + 2) * J, J), :, :].rearrange("j e c -> e j c")).then_inc(buf_in[u], 16)
                with sp.Fori(0, half) as i:
                    for u in range(2):
                        g = 2 * i + u
                        sp.wait_ge(copied, g + 3)
                        take_waits(sp, held)
                        sp.dma_start(weight_rows[bass.ds(g * J, J), :, :].rearrange("j e c -> e j c"), buf[u][:, :, :]).then_inc(buf_out[u], 16)
                for u in range(2):
                    sp.wait_ge(buf_out[u], 16 * half)

            @block.scalar
            def _(act):
                act.wait_ge(s_edge, 1)
                for b in range(LANES):
                    w = COLS + (b < LANES - 1)
                    act.dma_start(start[b * HEADS:(b + 1) * HEADS, 0:w],
                                  AP(start_rows.tensor, b * COLS, [[0, HEADS], [1, w]])).then_inc(s_flags, 16)
                act.sem_inc(back, 2)
                act.wait_ge(s_diff, 1)
                with act.Fori(0, half) as i:
                    for u in range(2):
                        g = 2 * i + u
                        act.wait_ge(back, g + 1)
                        nc.scalar.activation(weight[u][:, :], alpha[:, bass.ds(g * (J * P), J * P)], ACT.Exp).then_inc(s_exp, 1)

            @block.gpsimd
            def _(pool):
                nc.gpsimd.memset(start[96:P, COLS:COLS + 1], -BIG).then_inc(s_edge, 1)

            @block.vector
            def _(dve):
                link = Link(dve, s_dve)
                dve.sem_inc(added, 2)
                dve.sem_inc(copied, 2)
                dve.wait_ge(s_flags, 16 * 2 * LANES)
                with dve.Fori(0, half) as i:
                    for u in range(2):
                        g = 2 * i + u
                        dve.wait_ge(turned, g + 1)
                        c = bass.ds(g * (J * P), J * P)
                        nc.vector.tensor_tensor(alpha[:, c], turn[u][:, :], top[:, c], ALU.add).then_inc(added, 1)
                dve.wait_ge(added, TURNS + 2)

                def across(first_in, first_out, step, lo):
                    link(nc.vector.tensor_reduce(any_start[:, :], start[:, lo:lo + COLS], AXX, ALU.min))
                    dve.sem_inc(s_sum, 1)
                    k = 0 if lo == 0 else 1
                    dve.wait_ge(s_pe, 2 * k + 1)
                    link(nc.vector.tensor_copy(line[0:1, 0:2, :], small[0:1, 0:2, :]))
                    link(nc.vector.memset(line[0:1, 2, :], -BIG))
                    def at(row, first, h):
                        one = line[0:1, row, first + h:first + h + 1]
                        return AP(one.tensor, one.offset, [list(one.ap[0]), [step, LANES - 1]])

                    for h in range(HEADS):
                        last = nc.vector.tensor_tensor_scan(out=at(2, first_out, h), data0=at(1, first_in, h), data1=at(0, first_in, h),
                                                            initial=-BIG, op0=ALU.add, op1=ALU.max)
                    link(last)
                    dve.sem_inc(s_line, 1)
                    dve.wait_ge(s_pe, 2 * k + 2)
                    link(nc.vector.tensor_copy(carry[:, :], small[:, 2, 0:1]))

                link(nc.vector.tensor_tensor_scan(out=top[:, :], data0=start[:, 0:COLS], data1=alpha[:, :], initial=-BIG, op0=ALU.add, op1=ALU.max))
                link(nc.vector.tensor_copy(dump[0][:, 0:1], top[:, COLS - 1:COLS]))
                across(0, HEADS, HEADS, 0)
                link(nc.vector.tensor_tensor_scan(out=top[:, :], data0=start[:, 0:COLS], data1=alpha[:, :], initial=carry[:, 0:1], op0=ALU.add, op1=ALU.max))
                prev = -BIG
                for k in range(COLS // PIECE):
                    hi = COLS - k * PIECE
                    lo = hi - PIECE
                    link(nc.vector.tensor_tensor_scan(out=dump[k % 2][:, :], data0=start[:, hi:lo:-1], data1=backwards(top, hi, lo),
                                                      initial=prev, op0=ALU.add, op1=ALU.max))
                    prev = dump[k % 2][:, PIECE - 1:PIECE]
                link(nc.vector.tensor_copy(dump[1][:, 0:1], prev))
                across(HEADS * (LANES - 1), HEADS * (LANES - 2), -HEADS, 1)
                link(nc.vector.tensor_tensor_scan(out=backwards(top, COLS, 0), data0=start[:, COLS:0:-1], data1=backwards(top, COLS, 0),
                                                  initial=carry[:, 0:1], op0=ALU.add, op1=ALU.max))
                nc.vector.tensor_tensor(alpha[:, :], alpha[:, :], top[:, :], ALU.subtract).then_inc(s_diff, 1)
                with dve.Fori(0, half) as i:
                    for u in range(2):
                        g = 2 * i + u
                        dve.wait_ge(back, g + 3)
                        dve.wait_ge(buf_out[u], 16 * i)
                        nc.vector.tensor_copy(buf[u][:, :, :], turn[u][:, :].rearrange("p (j c) -> p j c", c=P)).then_inc(copied, 1)

            @block.tensor
            def _(pe):
                with pe.Fori(0, half) as i:
                    for u in range(2):
                        g = 2 * i + u
                        pe.wait_ge(buf_in[u], 16 * (i + 1))
                        pe.wait_ge(added, g + 1)
                        for j in range(J):
                            last = nc.tensor.transpose(turn[u][:, j * P:(j + 1) * P], buf[u][:, j, :], ident[:, :])
                        last.then_inc(turned, 1)
                for k in range(2):
                    pe.wait_ge(s_sum, k + 1)
                    nc.tensor.transpose(small[0:1, 0, :], dump[k][:, 0:1], ident[:, :])
                    nc.tensor.transpose(small[0:1, 1, :], any_start[:, 0:1], ident[:, :]).then_inc(s_pe, 1)
                    pe.wait_ge(s_line, k + 1)
                    nc.tensor.transpose(small[:, 2, 0:1], line[0:1, 2, :], ident[0:1, 0:1]).then_inc(s_pe, 1)
                with pe.Fori(0, half) as i:
                    for u in range(2):
                        g = 2 * i + u
                        pe.wait_ge(s_exp, g + 1)
                        pe.wait_ge(copied, g + 1)
                        for j in range(J):
                            last = nc.tensor.transpose(turn[u][:, j * P:(j + 1) * P], weight[u][:, j * P:(j + 1) * P], ident[:, :])
                        last.then_inc(back, 1)


def gat_sum_phase(nc, sb, ps, sem, pair, held, const, acc, S, gathered, weight_rows):
    src_col, dloc_col, tiles_row, iota_row, part_id, ident = const
    QUART = LANES // 4
    ON_DVE = 1
    R = 4
    with ExitStack() as ctx:
        G = [sb(ctx, f"gs_g{u}", [P, LANES, HROW]) for u in range(2)]
        wt = [sb(ctx, f"gs_wt{u}", [P, LANES * HEADS]) for u in range(2)]
        dcol = [sb(ctx, f"gs_dcol{u}", [P, LANES]) for u in range(2)]
        sums = ps(ctx, "gs_sums", [P, R, 512])
        rows_in, wt_in, dcol_ready = pair("gs_rows_in"), pair("gs_wt_in"), pair("gs_dcol_ready")
        zeroed, onehot_done = sem("gs_zeroed"), sem("gs_onehot_done")
        dve_mul, pool_mul = sem("gs_dve_mul"), sem("gs_pool_mul")
        sum_done = sem("gs_sum_done")
        add_done = sem("gs_add_done")
        half = ITERS // 2

        def multiply(eng, u, q):
            b = slice(q * QUART, (q + 1) * QUART)
            w = wt[u][:, q * QUART * HEADS:(q + 1) * QUART * HEADS]
            eng.tensor_copy(G[u][:, b, 0:HEADS], w.rearrange("p (b h) -> p b h", h=HEADS))
            h = G[u][:, b, H0:H1].rearrange("p b (h d) -> p b h d", d=HDIM)
            return eng.tensor_tensor(h, h, spread(w, [[HEADS, QUART], [1, HEADS], [0, HDIM]]), ALU.mult)

        with nc.Block() as block:
            @block.sync
            def _(sp):
                with sp.Fori(0, half) as i:
                    for u in range(2):
                        m = 2 * i + u
                        sp.wait_ge(sum_done, LANES * m)
                        take_waits(sp, held)
                        sp.wait_ge(dve_mul, ON_DVE * m)
                        take_waits(sp, held)
                        sp.wait_ge(pool_mul, (4 - ON_DVE) * m)
                        take_waits(sp, held)
                        sp.dma_start(G[u][:, :, :].rearrange("p b c -> p (b c)"),
                                     gathered[bass.ds(m, 1), :, :].rearrange("o p c -> (o p) c")).then_inc(rows_in[u], 16)
                        sp.dma_start(wt[u][:, :], weight_rows[bass.ds(m, 1), :, :].rearrange("o p c -> (o p) c")).then_inc(wt_in[u], 16)

            @block.scalar
            def _(act):
                with act.Fori(0, half) as i:
                    for u in range(2):
                        m = 2 * i + u
                        act.wait_ge(onehot_done, LANES * m)
                        nc.scalar.copy(dcol[u][:, :], dloc_col[:, bass.ds(m * LANES, LANES)]).then_inc(dcol_ready[u], 1)

            @block.gpsimd
            def _(pool):
                nc.gpsimd.memset(acc[:, :, :], 0.0).then_inc(zeroed, 1)
                with pool.Fori(0, half) as i:
                    for u in range(2):
                        pool.wait_ge(rows_in[u], 16 * (i + 1))
                        pool.wait_ge(wt_in[u], 16 * (i + 1))
                        take_waits(pool, held)
                        for q in range(ON_DVE, 4):
                            multiply(nc.gpsimd, u, q).then_inc(pool_mul, 1)

            @block.vector
            def _(dve):
                dve.sem_inc(add_done, R)
                dve.sem_inc(dve_mul, ON_DVE)
                dve.wait_ge(zeroed, 1)
                flat = acc[:, :, :].rearrange("p t c -> p (t c)")
                with dve.Fori(0, half) as i:
                    for u in range(2):
                        m = 2 * i + u
                        _, tiles = nc.values_load_multi_w_load_instructions(
                            tiles_row[0:1, bass.ds(m * LANES, LANES)], engines=[mybir.EngineType.DVE], min_val=0, max_val=TILES - 1,
                            skip_runtime_bounds_check_because="tile numbers are clamped where they are worked out")
                        dve.wait_ge(dcol_ready[u], i + 1)
                        for b in range(LANES):
                            dve.wait_ge(sum_done, m * LANES + b + 1)
                            nc.vector.tensor_scalar(S[:, b, :], iota_row[:, :], dcol[u][:, b:b + 1], None, ALU.is_equal).then_inc(onehot_done, 1)
                        dve.wait_ge(rows_in[u], 16 * (i + 1))
                        dve.wait_ge(wt_in[u], 16 * (i + 1))
                        for q in range(ON_DVE):
                            multiply(nc.vector, u, q).then_inc(dve_mul, 1)
                        for b in range(LANES):
                            n = m * LANES + b
                            dve.wait_ge(sum_done, n + 1 + LANES)
                            dve.wait_ge(add_done, n + R)
                            t = flat[:, bass.ds(tiles[b] * HROW, HROW)]
                            nc.vector.tensor_tensor(t, t, sums[:, b % R, 0:HROW], ALU.add).then_inc(add_done, 1)

            @block.tensor
            def _(pe):
                pe.sem_inc(sum_done, LANES)
                with pe.Fori(0, half) as i:
                    for u in range(2):
                        m = 2 * i + u
                        for b in range(LANES):
                            n = m * LANES + b
                            if b == 0:
                                pe.wait_ge(dve_mul, ON_DVE * (m + 2))
                            if b >= ON_DVE * QUART and b % QUART == 0:
                                pe.wait_ge(pool_mul, (4 - ON_DVE) * m + b // QUART - ON_DVE + 1)
                            pe.wait_ge(onehot_done, n + 1)
                            pe.wait_ge(add_done, n + 1)
                            nc.tensor.matmul(sums[:, b % R, 0:HROW], S[:, b, :], G[u][:, b, :], start=True, stop=True).then_inc(sum_done, 1)


def mid_phase(nc, sb, ps, sem, pair, held, A, const, acc, acc1, dinv, x1_rows, conv1_table):
    with ExitStack() as ctx:
        w1 = sb(ctx, "w1", [P, 2, F1])
        bias = sb(ctx, "gat_bias", [P, FEAT])
        den = sb(ctx, "den", [P, GT, HEADS])
        deg = [sb(ctx, f"deg{u}", [P, GT]) for u in range(2)]
        s_w, deg_ready, root_ready = sem("md_w"), sem("md_deg_ready"), sem("md_root_ready")
        x1_ready, x1_out = sem("md_x1_ready"), pair("md_x1_out")

        def sync_before(sp):
            sp.dma_start(w1[:, :, :], A["L1_gnn_W1"].rearrange("(c p) k -> p c k", p=P)).then_inc(s_w, 16)
            sp.dma_start(bias[:, :], A["L0_gnn_bias"].partition_broadcast(P)).then_inc(s_w, 16)

        def pre(dve, link, g, u, i, xg):
            a = acc[:, bass.ds(g * GT, GT), :]
            nc.vector.tensor_scalar(deg[u][:, :], acc[:, bass.ds(g * GT, GT), H1:HROW].rearrange("p t o -> p (t o)"), 1.0, None, ALU.add).then_inc(deg_ready, 1)
            link(nc.vector.tensor_scalar(den[:, :, :], acc[:, bass.ds(g * GT, GT), 0:HEADS], 1e-10, None, ALU.max))
            link(nc.vector.reciprocal(den[:, :, :], den[:, :, :]))
            h = acc[:, bass.ds(g * GT, GT), H0:H1].rearrange("p t (h d) -> p t h d", d=HDIM)
            link(nc.vector.tensor_tensor(h, h, spread(den[:, :, :], [[HEADS, GT], [1, HEADS], [0, HDIM]]), ALU.mult))
            link(nc.vector.tensor_tensor(xg[u][:, :, :], xg[u][:, :, :], acc[:, bass.ds(g * GT, GT), H0:H1], ALU.add))
            link(nc.vector.tensor_tensor(xg[u][:, :, :], xg[u][:, :, :], spread(bias[:, :], [[0, GT], [1, FEAT]]), ALU.add))
            dve.sem_inc(x1_ready, 1)
            dve.wait_ge(root_ready, g + 1)
            link(nc.vector.reciprocal(deg[u][:, :], deg[u][:, :]))
            nc.vector.tensor_copy(dinv[:, bass.ds(g * GT, GT)], deg[u][:, :])

        def act_root(act, g, u):
            act.wait_ge(deg_ready, g + 1)
            nc.scalar.activation(deg[u][:, :], deg[u][:, :], ACT.Sqrt).then_inc(root_ready, 1)

        def hold(sp, g, u, i, xg, finish_done, stored):
            sp.dma_start(x1_rows[bass.ds(g * (GT * P), GT * P), :].rearrange("(a p) c -> p a c", p=P), xg[u][:, :, :]).then_inc(x1_out[u], 16)
            sp.wait_ge(x1_out[u], 16 * (i + 1))
            take_waits(sp, held)

        def finish_act(act, g, u, a, op, done):
            nc.scalar.activation(acc1[:, bass.ds(g * GT + a, 1), :].rearrange("p o c -> p (o c)"), op[:, 0:F1], ACT.Copy, scale=deg[u][:, a:a + 1]).then_inc(done, 1)

        def act_store(act, g, u, stored):
            act.dma_start(conv1_table[bass.ds(g * (GT * P), GT * P), :].rearrange("(a p) c -> p a c", p=P),
                          acc1[:, bass.ds(g * GT, GT), :]).then_inc(stored[u], 16)

        dense_phase(nc, sb, ps, sem, pair, held, const, "md", ctx, A["x"], NODES, [w1[:, 0, :], w1[:, 1, :]], F1,
                    lambda pe: pe.wait_ge(s_w, 32), pre=pre, pre_links=6, finish_act=finish_act, act_store=act_store,
                    hold=hold, act_first=act_root, sync_before=sync_before, dve_before=lambda dve, link: dve.wait_ge(s_w, 32))


def conv_phase(nc, sb, ps, sem, pair, held, const, name, width, acc, table):
    src_col, dloc_col, tiles_row, iota_row, part_id, ident = const
    R = 4
    with ExitStack() as ctx:
        idx = [sb(ctx, f"{name}_idx{u}", [P, LANES], I32) for u in range(2)]
        dcol = [sb(ctx, f"{name}_dcol{u}", [P, LANES]) for u in range(2)]
        G = [sb(ctx, f"{name}_g{u}", [P, LANES, width]) for u in range(2)]
        S = sb(ctx, f"{name}_S", [P, LANES, P])
        sums = ps(ctx, f"{name}_sums", [P, R, 512])
        idx_ready, dcol_ready, rows_in = pair(f"{name}_idx_ready"), pair(f"{name}_dcol_ready"), pair(f"{name}_rows_in")
        onehot_done = sem(f"{name}_onehot_done")
        sum_done, add_done = sem(f"{name}_sum_done"), sem(f"{name}_add_done")
        half = ITERS // 2
        with nc.Block() as block:
            @block.scalar
            def _(act):
                with act.Fori(0, half) as i:
                    for u in range(2):
                        m = 2 * i + u
                        act.wait_ge(rows_in[u], 16 * LANES * i)
                        nc.scalar.copy(idx[u][:, :], src_col[:, bass.ds(m * LANES, LANES)]).then_inc(idx_ready[u], 1)
                        act.wait_ge(onehot_done, LANES * m)
                        nc.scalar.copy(dcol[u][:, :], dloc_col[:, bass.ds(m * LANES, LANES)]).then_inc(dcol_ready[u], 1)

            @block.gpsimd
            def _(pool):
                with pool.Fori(0, half) as i:
                    for u in range(2):
                        pool.wait_ge(idx_ready[u], i + 1)
                        pool.wait_ge(sum_done, (2 * i + u) * LANES)
                        take_waits(pool, held)
                        for b in range(LANES):
                            pool.indirect_dma_start(G[u][:, b, :], None, table,
                                                    bass.IndirectOffsetOnAxis(idx[u][:, b:b + 1], 0)).then_inc(rows_in[u], 16)

            @block.vector
            def _(dve):
                dve.sem_inc(add_done, R)
                flat = acc[:, :, :].rearrange("p t c -> p (t c)")
                with dve.Fori(0, half) as i:
                    for u in range(2):
                        m = 2 * i + u
                        _, tiles = nc.values_load_multi_w_load_instructions(
                            tiles_row[0:1, bass.ds(m * LANES, LANES)], engines=[mybir.EngineType.DVE], min_val=0, max_val=TILES - 1,
                            skip_runtime_bounds_check_because="tile numbers are clamped where they are worked out")
                        dve.wait_ge(dcol_ready[u], i + 1)
                        for b in range(LANES):
                            dve.wait_ge(sum_done, m * LANES + b + 1)
                            nc.vector.tensor_scalar(S[:, b, :], iota_row[:, :], dcol[u][:, b:b + 1], None, ALU.is_equal).then_inc(onehot_done, 1)
                        for b in range(LANES):
                            n = m * LANES + b
                            dve.wait_ge(sum_done, n + 1 + LANES)
                            dve.wait_ge(add_done, n + R)
                            t = flat[:, bass.ds(tiles[b] * width, width)]
                            nc.vector.tensor_tensor(t, t, sums[:, b % R, 0:width], ALU.add).then_inc(add_done, 1)

            @block.tensor
            def _(pe):
                pe.sem_inc(sum_done, LANES)
                with pe.Fori(0, half) as i:
                    for u in range(2):
                        m = 2 * i + u
                        pe.wait_ge(rows_in[u], 16 * LANES * (i + 1))
                        for b in range(LANES):
                            n = m * LANES + b
                            pe.wait_ge(onehot_done, n + 1)
                            pe.wait_ge(add_done, n + 1)
                            nc.tensor.matmul(sums[:, b % R, 0:width], S[:, b, :], G[u][:, b, :], start=True, stop=True).then_inc(sum_done, 1)


def norm_phase(nc, sb, ps, sem, A, const, name, width, acc, dinv, bias, gamma, beta):
    with ExitStack() as ctx:
        square = sb(ctx, f"{name}_square", [P, TILES, width])
        rows = sb(ctx, f"{name}_rows", [P, 3, width])
        ones = sb(ctx, f"{name}_ones", [P, 2, P])
        part_ok = sb(ctx, f"{name}_part_ok", [P, 1])
        mean = sb(ctx, f"{name}_mean", [P, width])
        var = sb(ctx, f"{name}_var", [P, width])
        root = sb(ctx, f"{name}_root", [P, width])
        total = [ps(ctx, f"{name}_total{k}", [P, 512]) for k in range(2)]
        s_rows, s_ones, s_dve = sem(f"{name}_rows_in"), sem(f"{name}_ones_ready"), sem(f"{name}_dve")
        s_vals, s_total, s_var, s_root, s_dev = (sem(f"{name}_{x}") for x in ("vals", "totals", "var_ready", "root_ready", "dev"))
        per = 512 // width
        whole = (TILES - 1) // per
        flat = acc[:, :, :].rearrange("p t c -> p (t c)")
        with nc.Block() as block:
            @block.sync
            def _(sp):
                for n, a in enumerate((bias, gamma, beta)):
                    sp.dma_start(rows[:, n, :], a.partition_broadcast(P)).then_inc(s_rows, 16)

            @block.vector
            def _(dve):
                link = Link(dve, s_dve)
                part_id = const[4]
                link(nc.vector.tensor_scalar(part_ok[:, :], part_id[:, :], float(LAST), None, ALU.is_lt))
                nc.vector.memset(ones[:, 0, :], 1.0)
                nc.vector.tensor_copy(ones[:, 1, :], spread(part_ok[:, :], [[0, P]])).then_inc(s_ones, 1)
                dve.wait_ge(s_rows, 48)

                def each(row):
                    return spread(row, [[0, TILES], [1, width]])

                link(nc.vector.tensor_tensor(acc[:, :, :], acc[:, :, :], spread(dinv[:, :], [[1, TILES], [0, width]]), ALU.mult))
                nc.vector.tensor_tensor(acc[:, :, :], acc[:, :, :], each(rows[:, 0, :]), ALU.add).then_inc(s_vals, 1)
                dve.wait_ge(s_total, 1)
                link(nc.vector.reduce_sum(mean[:, :], total[0][:, :].rearrange("p (a c) -> p c a", c=width), AXX))
                link(nc.vector.tensor_scalar(mean[:, :], mean[:, :], 1.0 / NODES, None, ALU.mult))
                nc.vector.tensor_tensor(acc[:, :, :], acc[:, :, :], each(mean[:, :]), ALU.subtract).then_inc(s_dev, 1)
                dve.wait_ge(s_total, 2)
                link(nc.vector.reduce_sum(var[:, :], total[1][:, :].rearrange("p (a c) -> p c a", c=width), AXX))
                nc.vector.tensor_scalar(var[:, :], var[:, :], 1.0 / NODES, EPS, ALU.mult, ALU.add).then_inc(s_var, 1)
                dve.wait_ge(s_root, 1)
                link(nc.vector.reciprocal(root[:, :], root[:, :]))
                link(nc.vector.tensor_tensor(root[:, :], root[:, :], rows[:, 1, :], ALU.mult))
                link(nc.vector.tensor_tensor(acc[:, :, :], acc[:, :, :], each(root[:, :]), ALU.mult))
                link(nc.vector.tensor_tensor(acc[:, :, :], acc[:, :, :], each(rows[:, 2, :]), ALU.add))

            @block.scalar
            def _(act):
                act.wait_ge(s_dev, 1)
                nc.scalar.activation(square[:, :, :], acc[:, :, :], ACT.Square).then_inc(s_dev, 1)
                act.wait_ge(s_var, 1)
                nc.scalar.activation(root[:, :], var[:, :], ACT.Sqrt).then_inc(s_root, 1)

            @block.tensor
            def _(pe):
                pe.wait_ge(s_ones, 1)
                for k, (src, ready, count) in enumerate(((flat, s_vals, 1), (square[:, :, :].rearrange("p t c -> p (t c)"), s_dev, 2))):
                    pe.wait_ge(ready, count)
                    for n in range(whole):
                        nc.tensor.matmul(total[k][:, :], ones[:, 0, :], src[:, n * 512:(n + 1) * 512], start=n == 0, stop=False)
                    for t in range(whole * per, TILES):
                        last = nc.tensor.matmul(total[k][:, 0:width], ones[:, int(t == TILES - 1), :], src[:, t * width:(t + 1) * width],
                                                start=False, stop=t == TILES - 1)
                    last.then_inc(s_total, 1)


def project_phase(nc, sb, ps, sem, pair, A, const, acc1, acc2, dinv, conv2_table):
    ident = const[5]
    with ExitStack() as ctx:
        w2 = sb(ctx, "w2", [P, F2])
        y = [sb(ctx, f"pj_y{r}", [P, F1]) for r in range(2)]
        yT = [sb(ctx, f"pj_yT{r}", [P, P]) for r in range(2)]
        tp = [ps(ctx, f"pj_tp{r}", [P, P]) for r in range(2)]
        op = [ps(ctx, f"pj_op{r}", [P, F2]) for r in range(2)]
        s_w, s_out = sem("pj_w"), sem("pj_out")
        relu_done, turn_done, copy_done = sem("pj_relu_done"), sem("pj_turn_done"), sem("pj_copy_done")
        product_done, finish_done = sem("pj_product_done"), sem("pj_finish_done")
        with nc.Block() as block:
            @block.sync
            def _(sp):
                sp.dma_start(w2[:, :], A["L1_gnn_W2"]).then_inc(s_w, 16)
                sp.wait_ge(finish_done, TILES + 2)
                sp.dma_start(conv2_table.rearrange("(t p) c -> p t c", p=P), acc2[:, :, :]).then_inc(s_out, 16)
                sp.wait_ge(s_out, 16)

            @block.scalar
            def _(act):
                for s in (turn_done, copy_done, product_done, finish_done):
                    act.sem_inc(s, 2)
                flat = acc1[:, :, :].rearrange("p t c -> p (t c)")
                with act.Fori(0, TILES // 2) as i:
                    for r in range(2):
                        t = 2 * i + r
                        act.wait_ge(turn_done, t + 1)
                        nc.scalar.activation(y[r][:, :], flat[:, bass.ds(t * F1, F1)], ACT.Relu).then_inc(relu_done, 1)

            @block.vector
            def _(dve):
                flat = acc2[:, :, :].rearrange("p t c -> p (t c)")
                with dve.Fori(0, TILES // 2) as i:
                    for r in range(2):
                        t = 2 * i + r
                        dve.wait_ge(turn_done, t + 3)
                        dve.wait_ge(product_done, t + 1)
                        nc.vector.tensor_copy(yT[r][:, :], tp[r][:, :]).then_inc(copy_done, 1)
                        dve.wait_ge(product_done, t + 3)
                        nc.vector.tensor_scalar(flat[:, bass.ds(t * F2, F2)], op[r][:, :], dinv[:, bass.ds(t, 1)], None, ALU.mult).then_inc(finish_done, 1)

            @block.tensor
            def _(pe):
                pe.wait_ge(s_w, 16)
                with pe.Fori(0, TILES // 2) as i:
                    for r in range(2):
                        t = 2 * i + r
                        pe.wait_ge(relu_done, t + 1)
                        pe.wait_ge(copy_done, t + 1)
                        nc.tensor.transpose(tp[r][:, :], y[r][:, :], ident[:, :]).then_inc(turn_done, 1)
                        pe.wait_ge(copy_done, t + 3)
                        pe.wait_ge(finish_done, t + 1)
                        nc.tensor.matmul(op[r][:, :], yT[r][:, :], w2[:, :], start=True, stop=True).then_inc(product_done, 1)


def final_phase(nc, sb, ps, sem, pair, held, A, const, acc1, acc2, x1_rows, out):
    with ExitStack() as ctx:
        wfc = sb(ctx, "wfc", [P, 4, FEAT])
        bias = sb(ctx, "fc_bias", [P, FEAT])
        res = [sb(ctx, f"fc_res{u}", [P, GT, FEAT]) for u in range(2)]
        s_w, out_done = sem("fn_w"), pair("fn_out_done")

        def sync_before(sp):
            w = A["L1_gnn_Wfc"]
            sp.dma_start(wfc[:, 0:3, :], w[0:3 * P, :].rearrange("(c p) k -> p c k", p=P)).then_inc(s_w, 16)
            sp.dma_start(wfc[0:F2, 3, :], w[3 * P:3 * P + F2, :]).then_inc(s_w, 16)
            sp.dma_start(bias[:, :], A["L1_gnn_bfc"].partition_broadcast(P)).then_inc(s_w, 16)

        def finish_dve(dve, link, i, u, a, op, xg, done):
            if a == 0:
                dve.wait_ge(out_done[u], 32 * i)
            link(nc.vector.tensor_tensor(res[u][:, a, :], op[:, 0:FEAT], bias[:, :], ALU.add))
            nc.vector.scalar_tensor_tensor(res[u][:, a, :], res[u][:, a, :], 0.0, xg[u][:, a, :], ALU.max, ALU.add).then_inc(done, 1)

        def hold(sp, g, u, i, xg, finish_done, stored):
            sp.wait_ge(finish_done, GT * (g + 1) + 2)
            take_waits(sp, held)
            r = g * (GT * P)
            full = GT - 1
            n = P if not isinstance(g, int) else min(P, NODES - g * GT * P - full * P)
            sp.dma_start(out[bass.ds(r, full * P), :].rearrange("(a p) c -> p a c", p=P), res[u][:, 0:full, :]).then_inc(out_done[u], 16)
            sp.dma_start(out[bass.ds(r + full * P, n), :], res[u][0:n, full, :]).then_inc(out_done[u], 16)
            if isinstance(g, int) and g >= GROUPS - 2:
                sp.wait_ge(out_done[u], 32 * (GROUPS // 2))

        dense_phase(nc, sb, ps, sem, pair, held, const, "fn", ctx, x1_rows, TILES * P,
                    [wfc[:, 0, :], wfc[:, 1, :], wfc[:, 2, :], wfc[0:F2, 3, :]], FEAT,
                    lambda pe: pe.wait_ge(s_w, 48), extra=((acc1, F1), (acc2, F2)), finish_dve=finish_dve, hold=hold,
                    sync_before=sync_before, dve_before=lambda dve, link: dve.wait_ge(s_w, 48))


_INS = ["x", "src", "dst", "edge_attr_3", "L0_gnn_W", "L0_gnn_a_src", "L0_gnn_a_dst", "L0_gnn_edge_W",
        "L0_gnn_edge_b", "L0_gnn_bias", "L1_gnn_W1", "L1_gnn_b1", "L1_gnn_g1", "L1_gnn_be1", "L1_gnn_W2",
        "L1_gnn_b2", "L1_gnn_g2", "L1_gnn_be2", "L1_gnn_Wfc", "L1_gnn_bfc"]


def kernel(**inputs):
    import concourse.bacc as _bacc
    from concourse.bass_utils import run_bass_kernel_spmd as _run

    nc = _bacc.Bacc("TRN2", target_bir_lowering=False, num_devices=1)
    arrays, A = {}, {}
    for name in _INS:
        a = np.ascontiguousarray(inputs[name])
        arrays[f"in_{name}"] = a
        A[name] = nc.dram_tensor(f"in_{name}", a.shape, mybir.dt.from_np(a.dtype), kind="ExternalInput").ap()
    out = nc.dram_tensor("out", (NODES, FEAT), F32, kind="ExternalOutput").ap()
    gnn(nc, A, out)
    return _run(nc, [arrays], core_ids=[0]).results[0]["out"]
```

```python
from contextlib import ExitStack, contextmanager

import numpy as np

import concourse.bass as bass
from concourse import mybir
from concourse.bass import AP

F32 = mybir.dt.float32
BF16 = mybir.dt.bfloat16
I32 = mybir.dt.int32
ALU = mybir.AluOpType
ACT = mybir.ActivationFunctionType
AXX = mybir.AxisListType.X

P = 128
NODES, FEAT, EDGES = 12500, 256, 200000
HEADS, HDIM = 8, 32
F1, F2 = 128, 64
CHUNKS = -(-EDGES // P)
TILES = -(-NODES // P)
LAST = NODES - (TILES - 1) * P
Q = -(-(CHUNKS + TILES - 1) // P)
STEPS = Q * P
LANES = 16
ITERS = STEPS // LANES
PL = P // LANES
PARTS = 3
AROW = PARTS * 3 * P
EROW = 3 * P + AROW // 2
ENC = PARTS * PARTS * 3 + PARTS
HROW = HEADS + FEAT + 1
HCOL = HROW + HEADS
DROW = HCOL - HEADS
H0, H1 = HEADS, HEADS + FEAT
GT = 7
GROUPS = TILES // GT
BIG = 1.0e30
EPS = 1.0e-5
PAD_DST = 20000
EPP = Q * P
FULL_P = EDGES // EPP
REST = EDGES - FULL_P * EPP


class Link:

    def __init__(self, eng, sem):
        self.eng, self.sem, self.base, self.n = eng, sem, 0, 0

    def __call__(self, ins):
        self.n += 1
        ins.then_inc(self.sem, 1)
        self.eng.wait_ge(self.sem, self.base + self.n)

    @contextmanager
    def loop(self, trips, links):
        start = self.base + self.n
        with self.eng.Fori(0, trips) as i:
            self.base, self.n = i * links + start, 0
            yield i
            assert self.n == links, (self.n, links)
        self.base, self.n = start + trips * links, 0


def take_waits(eng, held):
    eng.sem_inc(held, 1)


def spread(ap, dims):
    return AP(ap.tensor, ap.offset, [list(ap.ap[0])] + [list(d) for d in dims])


def gnn(nc, A, out):
    held = nc.alloc_semaphore(name="held")
    top = ExitStack()
    in_phase = []

    def sem(name):
        in_phase.append(nc.alloc_semaphore(name=name))
        return in_phase[-1]

    def end_phase():
        nc.clear_and_free_semaphores(in_phase)
        nc.all_engine_barrier()
        in_phase.clear()

    def pair(name):
        return [sem(name + "0"), sem(name + "1")]

    def dram(name, shape, dt=F32):
        return nc.dram_tensor(name, shape, dt, kind="Internal").ap()

    edge_rows = dram("edge_rows", (STEPS, EROW))
    chunk_end = dram("chunk_end", (STEPS,))
    tile_of = dram("tile_of", (STEPS,), I32)
    dloc_rows = dram("dloc_rows", (ITERS, LANES, P), BF16)
    attr_rows = dram("attr_rows", (ITERS, LANES, AROW), BF16)
    enc_parts = dram("enc_parts", (PARTS, 4, FEAT), BF16)
    start_rows = dram("start_rows", (STEPS, P))
    gat_table = dram("gat_table", (TILES * P, HROW))
    gathered = dram("gathered", (ITERS, P, LANES * HROW))
    score_rows = dram("score_rows", (ITERS, P, LANES * HEADS))
    weight_rows = dram("weight_rows", (ITERS, P, LANES * HEADS))
    x1_rows = dram("x1_rows", (TILES * P, FEAT))
    conv1_table = dram("conv1_table", (TILES * P, F1))
    conv2_table = dram("conv2_table", (TILES * P, F2))

    def sb(ctx, name, shape, dt=F32):
        return ctx.enter_context(nc.sbuf_tensor(name, shape, dt))

    def ps(ctx, name, shape, dt=F32):
        return ctx.enter_context(nc.psum_tensor(name, shape, dt))

    with top:
        src_col = sb(top, "src_col", [P, STEPS], I32)
        dloc_col = sb(top, "dloc_col", [P, STEPS])
        tiles_row = sb(top, "tiles_row", [1, STEPS], I32)
        iota_row = sb(top, "iota_row", [P, P])
        part_id = sb(top, "part_id", [P, 1])
        ident = sb(top, "ident", [P, P])
        const = (src_col, dloc_col, tiles_row, iota_row, part_id, ident)

        steps_phase(nc, sb, ps, sem, A, const, edge_rows, chunk_end, tile_of, dloc_rows, attr_rows,
                    start_rows)
        end_phase()
        with ExitStack() as ctx:
            h_all = sb(ctx, "h_all", [P, TILES, HCOL])
            node_phase(nc, sb, ps, sem, pair, held, A, const, h_all, gat_table)
            end_phase()
            score_phase(nc, sb, ps, sem, pair, held, A, const, h_all, gat_table, gathered, dloc_rows,
                        attr_rows, enc_parts, score_rows)
            end_phase()
        softmax_phase(nc, sb, ps, sem, pair, held, const, start_rows, score_rows, weight_rows)
        end_phase()
        with ExitStack() as ctx:
            acc1 = sb(ctx, "acc1", [P, TILES, F1])
            dinv = sb(ctx, "dinv", [P, TILES])
            with ExitStack() as ctx2:
                acc = sb(ctx2, "acc", [P, TILES, HROW])
                gat_sum_phase(nc, sb, ps, sem, pair, held, const, acc, acc1[:, 0:2 * LANES, :], gathered, weight_rows)
                end_phase()
                mid_phase(nc, sb, ps, sem, pair, held, A, const, acc, acc1, dinv, x1_rows, conv1_table)
                end_phase()
            conv_phase(nc, sb, ps, sem, pair, held, const, "c1", F1, acc1, conv1_table)
            end_phase()
            acc2 = sb(ctx, "acc2", [P, TILES, F2])
            norm_phase(nc, sb, ps, sem, A, const, "n1", F1, acc1, dinv,
                       A["L1_gnn_b1"], A["L1_gnn_g1"], A["L1_gnn_be1"])
            end_phase()
            project_phase(nc, sb, ps, sem, pair, A, const, acc1, acc2, dinv, conv2_table)
            end_phase()
            conv_phase(nc, sb, ps, sem, pair, held, const, "c2", F2, acc2, conv2_table)
            end_phase()
            norm_phase(nc, sb, ps, sem, A, const, "n2", F2, acc2, dinv,
                       A["L1_gnn_b2"], A["L1_gnn_g2"], A["L1_gnn_be2"])
            end_phase()
            final_phase(nc, sb, ps, sem, pair, held, A, const, acc1, acc2, x1_rows, out)
            end_phase()


def steps_phase(nc, sb, ps, sem, A, const, edge_rows, chunk_end, tile_of, dloc_rows, attr_rows,
                start_rows):
    src_col, dloc_col, tiles_row, iota_row, part_id, ident = const
    with ExitStack() as ctx:
        dst_i = sb(ctx, "dst_i", [P, EPP], I32)
        prev_i = sb(ctx, "prev_i", [P, EPP], I32)
        src_i = sb(ctx, "src_i", [P, EPP], I32)
        attr = sb(ctx, "attr", [P, EPP * 3])
        rows = sb(ctx, "rows", [P, Q, EROW])
        parts = rows[:, :, 3 * P:EROW].bitcast(BF16)
        left = sb(ctx, "left", [P, Q, 3, P])
        ends = sb(ctx, "ends", [P, STEPS])
        below = sb(ctx, "below", [P, STEPS])
        order_i = sb(ctx, "order_i", [P, Q], I32)
        order = sb(ctx, "order", [P, Q])
        last_i = sb(ctx, "last_i", [P, Q], I32)
        last = sb(ctx, "last", [P, Q])
        chunk = sb(ctx, "chunk", [P, Q])
        chunk_i = sb(ctx, "chunk_i", [P, Q], I32)
        tile = sb(ctx, "tile", [P, Q])
        tile_i = sb(ctx, "tile_i", [P, Q], I32)
        base = sb(ctx, "base", [P, Q])
        valid = sb(ctx, "valid", [P, Q, P])
        dclip = sb(ctx, "dclip", [P, Q, P])
        dclip16 = sb(ctx, "dclip16", [P, Q, P], BF16)
        iota_i = sb(ctx, "iota_i", [P, P], I32)
        part_i = sb(ctx, "part_i", [P, 1], I32)
        turn = ps(ctx, "turn_s", [P, 4, 512])
        s_pads, s_loads, s_rows, s_rows_out = sem("st_pads"), sem("st_loads"), sem("st_rows"), sem("st_rows_out")
        s_end, s_end_out, s_end_in = sem("st_end"), sem("st_end_out"), sem("st_end_in")
        s_chunk, s_step_rows, s_iota, s_ident = sem("st_chunk"), sem("st_step_rows"), sem("st_iota"), sem("st_ident")
        s_tile, s_tile_out, s_tile_in = sem("st_tile"), sem("st_tile_out"), sem("st_tile_in")
        s_clip, s_left = sem("st_clip"), sem("st_left")
        s_ready, s_out, s_turned, s_taken = sem("st_ready"), sem("st_out"), sem("st_turned"), sem("st_taken")
        s_dve = sem("st_dve")
        with nc.Block() as block:
            @block.sync
            def _(sp):
                sp.wait_ge(s_pads, 4)
                a3 = A["edge_attr_3"].rearrange("e f -> (e f)")
                for t, a, w in ((dst_i, A["dst"], 1), (src_i, A["src"], 1), (attr, a3, 3)):
                    sp.dma_start(t[0:FULL_P, :], a[0:FULL_P * EPP * w].rearrange("(p e) -> p e", e=EPP * w)).then_inc(s_loads, 16)
                    sp.dma_start(t[FULL_P:FULL_P + 1, 0:REST * w], a[FULL_P * EPP * w:].rearrange("(p e) -> p e", p=1)).then_inc(s_loads, 16)
                d = A["dst"]
                sp.dma_start(prev_i[0:1, 1:EPP], d[0:EPP - 1].rearrange("(p e) -> p e", p=1)).then_inc(s_loads, 16)
                sp.dma_start(prev_i[1:FULL_P, :], d[EPP - 1:FULL_P * EPP - 1].rearrange("(p e) -> p e", e=EPP)).then_inc(s_loads, 16)
                sp.dma_start(prev_i[FULL_P:FULL_P + 1, 0:REST], d[FULL_P * EPP - 1:EDGES - 1].rearrange("(p e) -> p e", p=1)).then_inc(s_loads, 16)
                sp.wait_ge(s_rows, 2)
                sp.dma_start(edge_rows.rearrange("(p q) e -> p q e", q=Q), rows[:, :, :]).then_inc(s_rows_out, 16)
                sp.wait_ge(s_end, 1)
                sp.dma_start(chunk_end.rearrange("(p q) -> p q", q=Q), last[:, :]).then_inc(s_end_out, 16)
                sp.wait_ge(s_end_out, 16)
                sp.dma_start(ends[:, :], AP(chunk_end.tensor, 0, [[0, P], [1, STEPS]])).then_inc(s_end_in, 16)
                sp.wait_ge(s_tile, 1)
                with nc.allow_non_contiguous_dma(reason="one small table"):
                    for b in range(LANES):
                        sp.dma_start(AP(tile_of.tensor, b, [[Q * LANES, PL], [LANES, Q], [1, 1]]),
                                     tile_i[b * PL:(b + 1) * PL, :].rearrange("p (q o) -> p q o", o=1)).then_inc(s_tile_out, 16)
                sp.wait_ge(s_tile_out, 16 * LANES)
                sp.dma_start(tiles_row[:, :], tile_of.rearrange("(o k) -> o k", o=1)).then_inc(s_tile_in, 16)
                sp.wait_ge(s_ready, 1)
                sp.dma_start(start_rows.rearrange("(p q) e -> p q e", q=Q), rows[:, :, 2 * P:3 * P]).then_inc(s_out, 16)
                for b in range(LANES):
                    p = slice(b * PL, (b + 1) * PL)
                    sp.dma_start(AP(dloc_rows.tensor, b * P, [[Q * LANES * P, PL], [LANES * P, Q], [1, P]]),
                                 dclip16[p, :, :]).then_inc(s_out, 16)
                    sp.dma_start(AP(attr_rows.tensor, b * AROW, [[Q * LANES * AROW, PL], [LANES * AROW, Q], [1, AROW]]),
                                 parts[p, :, :]).then_inc(s_out, 16)
                sp.wait_ge(s_tile_in, 16)
                sp.wait_ge(s_out, 16 * (1 + 2 * LANES))

            @block.gpsimd
            def _(pool):
                nc.gpsimd.memset(dst_i[:, :], PAD_DST).then_inc(s_pads, 1)
                nc.gpsimd.memset(src_i[:, :], 0).then_inc(s_pads, 1)
                nc.gpsimd.memset(attr[:, :], 0.0).then_inc(s_pads, 1)
                nc.gpsimd.memset(prev_i[:, :], -1).then_inc(s_pads, 1)
                nc.gpsimd.iota(order_i[:, :], pattern=[[1, Q]], base=0, channel_multiplier=Q).then_inc(s_iota, 1)
                nc.gpsimd.iota(iota_i[:, :], pattern=[[1, P]], base=0, channel_multiplier=0).then_inc(s_iota, 1)
                nc.gpsimd.iota(part_i[:, :], pattern=[[0, 1]], base=0, channel_multiplier=1).then_inc(s_iota, 1)
                nc.gpsimd.memset(ident[:, :], 0.0).then_inc(s_ident, 1)
                pool.wait_ge(s_ident, 1)
                nc.gpsimd.affine_select(out=ident[:, :], in_=ident[:, :], compare_op=ALU.not_equal, fill=1.0,
                                        base=0, pattern=[[-1, P]], channel_multiplier=1).then_inc(s_ident, 1)
                pool.wait_ge(s_loads, 16 * 9)
                nc.gpsimd.tensor_copy(left[:, :, :, :], attr[:, :].rearrange("p (q e f) -> p q f e", e=P, f=3)).then_inc(s_left, 1)
                for n in range(PARTS):
                    part = parts[:, :, n * 3 * P:(n + 1) * 3 * P].rearrange("p q (f e) -> p q f e", e=P)
                    pool.wait_ge(s_left, 2 * n + 1)
                    i = nc.gpsimd.tensor_copy(part, left[:, :, :, :])
                    if n < PARTS - 1:
                        i.then_inc(s_left, 1)
                        pool.wait_ge(s_left, 2 * n + 2)
                        nc.gpsimd.tensor_tensor(left[:, :, :, :], left[:, :, :, :], part, ALU.subtract).then_inc(s_left, 1)
                i.then_inc(s_rows, 1)
                pool.wait_ge(s_rows_out, 16)
                pool.wait_ge(s_chunk, 1)
                for q in range(Q):
                    pool.indirect_dma_start(rows[:, q, :], None, edge_rows,
                                            bass.IndirectOffsetOnAxis(chunk_i[:, q:q + 1], 0)).then_inc(s_step_rows, 16)

            @block.vector
            def _(dve):
                link = Link(dve, s_dve)
                dve.wait_ge(s_iota, 3)
                nc.vector.tensor_copy(iota_row[:, :], iota_i[:, :])
                nc.vector.tensor_copy(part_id[:, :], part_i[:, :])
                nc.vector.tensor_copy(order[:, :], order_i[:, :])
                dve.wait_ge(s_loads, 16 * 9)
                link(nc.vector.tensor_scalar(last_i[:, :], dst_i[:, :].rearrange("p (q e) -> p q e", e=P)[:, :, P - 1],
                                             7, None, ALU.arith_shift_right))
                link(nc.vector.tensor_scalar(last[:, :], last_i[:, :], float(TILES - 1), None, ALU.min))
                nc.vector.tensor_tensor(last[:, :], last[:, :], order[:, :], ALU.add).then_inc(s_end, 1)
                for n, t in enumerate((src_i, dst_i, prev_i)):
                    i = nc.vector.tensor_copy(rows[:, :, n * P:(n + 1) * P], t[:, :].rearrange("p (q e) -> p q e", e=P))
                    if n == 2:
                        i.then_inc(s_rows, 1)
                dve.wait_ge(s_end_in, 16)
                for q in range(Q):
                    link(nc.vector.tensor_scalar(below[:, :], ends[:, :], order[:, q:q + 1], None, ALU.is_lt))
                    link(nc.vector.reduce_sum(chunk[:, q:q + 1], below[:, :], AXX))
                nc.vector.tensor_copy(chunk_i[:, :], chunk[:, :]).then_inc(s_chunk, 1)
                link(nc.vector.tensor_tensor(tile[:, :], order[:, :], chunk[:, :], ALU.subtract))
                nc.vector.tensor_copy(tile_i[:, :], tile[:, :]).then_inc(s_tile, 1)
                link(nc.vector.tensor_scalar(base[:, :], tile[:, :], float(P), None, ALU.mult))
                dve.wait_ge(s_step_rows, 16 * Q)
                link(nc.vector.tensor_tensor(rows[:, :, P:2 * P], rows[:, :, P:2 * P], spread(base[:, :], [[1, Q], [0, P]]), ALU.subtract))
                link(nc.vector.tensor_tensor(rows[:, :, 2 * P:3 * P], rows[:, :, 2 * P:3 * P], spread(base[:, :], [[1, Q], [0, P]]), ALU.subtract))
                link(nc.vector.tensor_scalar(valid[:, :, :], rows[:, :, P:2 * P], float(P - 1), None, ALU.is_le))
                link(nc.vector.scalar_tensor_tensor(valid[:, :, :], rows[:, :, P:2 * P], 0.0, valid[:, :, :], ALU.is_ge, ALU.mult))
                link(nc.vector.tensor_scalar(dclip[:, :, :], rows[:, :, P:2 * P], -1.0, float(P), ALU.max, ALU.min))
                dve.sem_inc(s_clip, 1)
                link(nc.vector.tensor_copy(dclip16[:, :, :], dclip[:, :, :]))
                link(nc.vector.tensor_tensor(rows[:, :, 2 * P:3 * P], rows[:, :, P:2 * P], rows[:, :, 2 * P:3 * P], ALU.not_equal))
                nc.vector.scalar_tensor_tensor(rows[:, :, 2 * P:3 * P], rows[:, :, 2 * P:3 * P], -BIG, valid[:, :, :], ALU.mult, ALU.mult).then_inc(s_ready, 1)

            @block.tensor
            def _(pe):
                pe.wait_ge(s_ident, 2)
                pe.wait_ge(s_step_rows, 16 * Q)
                for n in range(2 * Q):
                    if n == Q:
                        pe.wait_ge(s_clip, 1)
                    if n >= 4:
                        pe.wait_ge(s_taken, n - 3)
                    rows_n = rows[:, n, 0:P] if n < Q else dclip[:, n - Q, :]
                    nc.tensor.transpose(turn[:, n % 4, 0:P], rows_n, ident[:, :]).then_inc(s_turned, 1)

            @block.scalar
            def _(act):
                views = [t[:, :].rearrange("e (pl q b) -> e q b pl", q=Q, b=LANES) for t in (src_col, dloc_col)]
                for n in range(2 * Q):
                    act.wait_ge(s_turned, n + 1)
                    nc.scalar.copy(views[n // Q][:, n % Q, :, :],
                                   turn[:, n % 4, 0:P].rearrange("e (b pl) -> e b pl", pl=PL)).then_inc(s_taken, 1)


def load_groups(sp, src, xg, s_in, waits, rows, after=None):
    def load(g, u):
        r = g * (GT * P)
        full = GT - 1
        sp.dma_start(xg[u][:, 0:full, :], src[bass.ds(r, full * P), :].rearrange("(a p) c -> p a c", p=P)).then_inc(s_in[u], 16)
        n = P if not isinstance(g, int) else min(P, rows - g * GT * P - full * P)
        sp.dma_start(xg[u][0:n, full, :], src[bass.ds(r + full * P, n), :]).then_inc(s_in[u], 16)

    load(0, 0)
    load(1, 1)
    half = GROUPS // 2
    with sp.Fori(0, half - 2) as i:
        for u in range(2):
            waits(2 * i + u, u, i)
            load(2 * i + u + 2, u)
            if after:
                after(2 * i + u, u, i)
    for g in range(GROUPS - 4, GROUPS):
        waits(g, g % 2, g // 2)
        if g + 2 < GROUPS:
            load(g + 2, g % 2)
        if after:
            after(g, g % 2, g // 2)


def dense_phase(nc, sb, ps, sem, pair, held, const, name, ctx, src, rows, weights, nout, w_ready,
                pre=None, pre_late=None, pre_links=0, extra=(), finish_act=None, act_store=None, finish_dve=None,
                hold=None, after=None, act_first=None, pool=None, tensor_before=None, dve_before=None, sync_before=None):
    ident = const[5]
    xg = [sb(ctx, f"{name}_x{u}", [P, GT, FEAT]) for u in range(2)]
    hn = sb(ctx, f"{name}_hn", [P, GT, FEAT])
    ys = [[sb(ctx, f"{name}_y{n}{r}", [P, w]) for n, (_, w) in enumerate(extra)] for r in range(2)]
    nk = 2 + len(extra)
    hT = [sb(ctx, f"{name}_hT{r}", [P, nk, P]) for r in range(2)]
    stats = sb(ctx, f"{name}_stats", [P, GT, 6])
    mv = sb(ctx, f"{name}_mv", [P, GT, 2])
    var = sb(ctx, f"{name}_var", [P, GT])
    sd = sb(ctx, f"{name}_sd", [P, GT])
    rstd = [sb(ctx, f"{name}_rstd{u}", [P, GT]) for u in range(2)]
    shift = [sb(ctx, f"{name}_shift{u}", [P, GT]) for u in range(2)]
    tp = [ps(ctx, f"{name}_tp{r}", [P, 4, P]) for r in range(2)]
    op = [ps(ctx, f"{name}_op{r}", [P, 512]) for r in range(2)]
    x_in = pair(f"{name}_x_in")
    s_var, s_sd, s_norm = sem(f"{name}_var_ready"), sem(f"{name}_sd_ready"), sem(f"{name}_norm_ready")
    relu_done, turn_done = sem(f"{name}_relu_done"), sem(f"{name}_turn_done")
    copy_done, product_done = sem(f"{name}_copy_done"), sem(f"{name}_product_done")
    finish_done = sem(f"{name}_finish_done")
    s_dve = sem(f"{name}_dve")
    stored = pair(f"{name}_stored")
    half = GROUPS // 2
    with nc.Block() as block:
        @block.sync
        def _(sp):
            if sync_before:
                sync_before(sp)

            def waits(g, u, i):
                sp.wait_ge(relu_done, GT * (g + 1) + 2 * GT)
                take_waits(sp, held)
                if hold:
                    hold(sp, g, u, i, xg, finish_done, stored)
            load_groups(sp, src, xg, x_in, waits, rows, after and (lambda g, u, i: after(sp, g, u, i)))

        if pool:
            @block.gpsimd
            def _(p):
                pool(p)

        @block.vector
        def _(dve):
            link = Link(dve, s_dve)
            dve.sem_inc(relu_done, 2 * GT)
            dve.sem_inc(turn_done, GT)
            for s in (copy_done, product_done, finish_done):
                dve.sem_inc(s, 2)
            for s in (s_sd, s_norm):
                dve.sem_inc(s, 1)
            if dve_before:
                dve_before(dve, link)

            def begin(g, u, i):
                dve.wait_ge(x_in[u], 32 * (i + 1))
                if pre:
                    pre(dve, link, g, u, xg, finish_done)

            def statistics(g, u):
                take_waits(dve, held)
                for a in range(GT):
                    last = nc.vector.bn_aggr(mv[:, a, :], stats[:, a, :])
                link(last)
                dve.wait_ge(s_sd, g + 1)
                nc.vector.tensor_scalar(var[:, :], mv[:, :, 1], EPS, None, ALU.add).then_inc(s_var, 1)
                dve.wait_ge(s_sd, g + 2)
                dve.wait_ge(relu_done, GT * (g + 1))
                link(nc.vector.reciprocal(rstd[u][:, :], sd[:, :]))
                link(nc.vector.scalar_tensor_tensor(shift[u][:, :], mv[:, :, 0], -1.0, rstd[u][:, :], ALU.mult, ALU.mult))
                dve.sem_inc(s_norm, 1)

            def sums(u, tiles):
                for a in tiles:
                    last = nc.vector.bn_stats(stats[:, a, :], xg[u][:, a, :])
                if GT - 1 in tiles:
                    link(last)

            def group(g, u, i, more):
                def finish(a):
                    dve.wait_ge(product_done, g * GT + a + 3)
                    finish_dve(dve, link, g, u, a, op[(u * GT + a) % 2], xg, finish_done)

                for a in range(GT):
                    n, r = g * GT + a, (u * GT + a) % 2
                    dve.wait_ge(turn_done, n + 1 + GT)
                    dve.wait_ge(product_done, n + 1)
                    w = min(nk, 3)
                    last = nc.vector.tensor_copy(hT[r][:, 0:w, :], tp[r][:, 0:w, :])
                    if nk == 4:
                        last = nc.vector.tensor_copy(hT[r][0:F2, 3, :], tp[r][0:F2, 3, :])
                    last.then_inc(copy_done, 1)
                    if finish_dve and a:
                        finish(a - 1)
                    if more and a == 0:
                        begin(g + 1, 1 - u, i + u)
                        sums(1 - u, [0])
                    if more and a in (1, 2, 3):
                        sums(1 - u, [2 * a - 1, 2 * a])
                    if more and a == 4:
                        if pre_late:
                            pre_late(dve, link, g + 1, 1 - u)
                        statistics(g + 1, 1 - u)
                if finish_dve:
                    finish(GT - 1)

            begin(0, 0, 0)
            sums(0, range(GT))
            if pre_late:
                pre_late(dve, link, 0, 0)
            statistics(0, 0)
            with link.loop(half - 1, 2 * (4 + pre_links + (GT if finish_dve else 0))) as i:
                for u in range(2):
                    group(2 * i + u, u, i, True)
            group(GROUPS - 2, 0, half - 1, True)
            group(GROUPS - 1, 1, half - 1, False)

        @block.scalar
        def _(act):
            def root(g, u):
                act.wait_ge(s_var, g + 1)
                act.wait_ge(s_norm, g + 1)
                nc.scalar.activation(sd[:, :], var[:, :], ACT.Sqrt).then_inc(s_sd, 1)

            def relu(g, u, tiles):
                for a in tiles:
                    n, r = g * GT + a, (u * GT + a) % 2
                    if a == 0:
                        act.wait_ge(s_norm, g + 2)
                    act.wait_ge(turn_done, n + (GT - 1 if extra else 1))
                    for y, (s, w) in zip(ys[r], extra):
                        nc.scalar.activation(y[:, :], s[:, :, :].rearrange("p t c -> p (t c)")[:, bass.ds(n * w, w)], ACT.Relu)
                    nc.scalar.activation(hn[:, a, :], xg[u][:, a, :], ACT.Relu, bias=shift[u][:, a:a + 1],
                                         scale=rstd[u][:, a:a + 1]).then_inc(relu_done, 1)

            def group(g, u, more):
                for a in range(GT):
                    if finish_act:
                        act.wait_ge(product_done, g * GT + a + 3)
                        finish_act(act, g, u, a, op[(u * GT + a) % 2], finish_done)
                    if more and act_first and a == 1:
                        act_first(act, g + 1, 1 - u)
                    if more and a == 4:
                        root(g + 1, 1 - u)
                    if more and a == 5:
                        relu(g + 1, 1 - u, range(3))
                if more:
                    relu(g + 1, 1 - u, range(3, GT))
                if finish_act:
                    act.wait_ge(finish_done, (g + 1) * GT + 2)
                    act_store(act, g, u, stored)

            if act_first:
                act_first(act, 0, 0)
            root(0, 0)
            relu(0, 0, range(GT))
            with act.Fori(0, half - 1) as i:
                for u in range(2):
                    group(2 * i + u, u, True)
            group(GROUPS - 2, 0, True)
            group(GROUPS - 1, 1, False)
            if finish_act:
                for u in range(2):
                    act.wait_ge(stored[u], 16 * half)

        @block.tensor
        def _(pe):
            if tensor_before:
                tensor_before(pe)
            w_ready(pe)

            def turn(g, u, a):
                n, r = g * GT + a, (u * GT + a) % 2
                pe.wait_ge(relu_done, n + 1 + 2 * GT)
                pe.wait_ge(copy_done, n + 1)
                pieces = [hn[:, a, 0:P], hn[:, a, P:2 * P]] + [y[:, :] for y in ys[r]]
                for c, piece in enumerate(pieces):
                    w = piece.shape[1]
                    last = nc.tensor.transpose(tp[r][0:w, c, :], piece, ident[:, :])
                last.then_inc(turn_done, 1)

            def product(g, u, a):
                n, r = g * GT + a, (u * GT + a) % 2
                pe.wait_ge(copy_done, n + 3)
                pe.wait_ge(finish_done, n + 1)
                for c in range(nk):
                    k = weights[c].shape[0]
                    last = nc.tensor.matmul(op[r][:, 0:nout], hT[r][0:k, c, :], weights[c],
                                            start=c == 0, stop=c == nk - 1)
                last.then_inc(product_done, 1)

            with pe.Fori(0, half) as i:
                for u in range(2):
                    g = 2 * i + u
                    turn(g, u, 0)
                    for a in range(GT):
                        if a < GT - 1:
                            turn(g, u, a + 1)
                        product(g, u, a)


def node_phase(nc, sb, ps, sem, pair, held, A, const, h_all, gat_table):
    ident = const[5]
    with ExitStack() as ctx:
        w_sb = sb(ctx, "w_sb", [P, 2, FEAT])
        score = sb(ctx, "score", [P, 2, 2])
        heads = sb(ctx, "heads", [P, 2, 2 * HEADS])
        w_t = sb(ctx, "w_t", [P, 2, HCOL])
        wp = ps(ctx, "wp", [P, 4, 512])
        s_w, s_heads, s_zero = sem("nd_w"), sem("nd_heads"), sem("nd_zero")
        s_wturn, s_wcopy = sem("nd_wturn"), sem("nd_wcopy")

        def sync_before(sp):
            sp.dma_start(w_sb[:, :, :], A["L0_gnn_W"].rearrange("(c p) k -> p c k", p=P)).then_inc(s_w, 16)
            with nc.allow_non_contiguous_dma(reason="two vectors"):
                for n, a in enumerate((A["L0_gnn_a_src"], A["L0_gnn_a_dst"])):
                    sp.dma_start(score[:, n, :], a.rearrange("h d -> (h d)").rearrange("(c p) -> p c", p=P)).then_inc(s_w, 16)

        def dve_before(dve, link):
            nc.vector.memset(h_all[:, :, H1:H1 + 1], 1.0)
            nc.vector.memset(w_t[:, :, H1:H1 + 1], 0.0)
            link(nc.vector.memset(heads[:, :, :], 0.0))
            dve.wait_ge(s_w, 48)
            for n in range(2):
                for c in range(2):
                    for q in range(4):
                        col = n * HEADS + c * 4 + q
                        last = nc.vector.tensor_copy(heads[q * HDIM:(q + 1) * HDIM, c, col:col + 1],
                                                     score[q * HDIM:(q + 1) * HDIM, n, c:c + 1])
            last.then_inc(s_heads, 1)
            for n in range(4):
                dve.wait_ge(s_wturn, n + 1)
                last = nc.vector.tensor_copy(w_t[:, n % 2, H0 + n // 2 * P:H0 + (n // 2 + 1) * P], wp[:, n, 0:P])
            last.then_inc(s_wcopy, 1)
            for c in range(2):
                dve.wait_ge(s_wturn, 5 + c)
                nc.vector.tensor_copy(w_t[:, c, 0:HEADS], wp[:, c, P:P + HEADS])
                last = nc.vector.tensor_copy(w_t[:, c, HROW:HCOL], wp[:, c, P + HEADS:P + 2 * HEADS])
            last.then_inc(s_wcopy, 1)

        def tensor_before(pe):
            pe.wait_ge(s_w, 48)
            for n in range(4):
                nc.tensor.transpose(wp[:, n, 0:P], w_sb[:, n // 2, n % 2 * P:(n % 2 + 1) * P], ident[:, :]).then_inc(s_wturn, 1)
            pe.wait_ge(s_heads, 1)
            pe.wait_ge(s_wcopy, 1)
            for c in range(2):
                for k in range(2):
                    last = nc.tensor.matmul(wp[:, c, P:P + 2 * HEADS], w_sb[:, k, c * P:(c + 1) * P], heads[:, k, :],
                                            start=k == 0, stop=k == 1)
                last.then_inc(s_wturn, 1)

        def finish_act(act, g, u, a, op, done):
            nc.scalar.copy(h_all[:, :, :].rearrange("p t c -> p (t c)")[:, bass.ds((g * GT + a) * HCOL, H1)], op[:, 0:H1])
            nc.scalar.copy(h_all[:, :, :].rearrange("p t c -> p (t c)")[:, bass.ds((g * GT + a) * HCOL + HROW, HEADS)],
                           op[:, HROW:HCOL]).then_inc(done, 1)

        def act_store(act, g, u, stored):
            act.dma_start(gat_table[bass.ds(g * (GT * P), GT * P), :].rearrange("(a p) c -> p a c", p=P),
                          h_all[:, bass.ds(g * GT, GT), 0:HROW]).then_inc(stored[u], 16)

        dense_phase(nc, sb, ps, sem, pair, held, const, "nd", ctx, A["x"], NODES, [w_t[:, 0, :], w_t[:, 1, :]], HCOL,
                    lambda pe: pe.wait_ge(s_wcopy, 2), finish_act=finish_act, act_store=act_store,
                    tensor_before=tensor_before, dve_before=dve_before, sync_before=sync_before)


def score_phase(nc, sb, ps, sem, pair, held, A, const, h_all, gat_table, gathered, dloc_rows, attr_rows, enc_parts,
                score_rows):
    src_col, dloc_col, tiles_row, iota_row, part_id, ident = const
    PAIRS, HALF = LANES // 2, LANES // 2
    DEPTH = 4
    with ExitStack() as ctx:
        idx = [sb(ctx, f"sc_idx{v}", [P, LANES], I32) for v in range(4)]
        G = [sb(ctx, f"sc_g{u}", [P, LANES, HROW]) for u in range(2)]
        dl = [sb(ctx, f"sc_dl{u}", [P, LANES * P], BF16) for u in range(2)]
        att = [sb(ctx, f"sc_att{u}", [ENC, LANES * P], BF16) for u in range(2)]
        ew_left = sb(ctx, "sc_ew_left", [4, FEAT])
        ew_parts = sb(ctx, "sc_ew_parts", [4, PARTS, FEAT], BF16)
        ew = sb(ctx, "sc_ew", [ENC, FEAT], BF16)
        onehot = [sb(ctx, f"sc_onehot{r}", [P, 2 * P]) for r in range(DEPTH)]
        enc = [sb(ctx, f"sc_enc{r}", [P, 2, FEAT]) for r in range(2)]
        prod = [sb(ctx, f"sc_prod{r}", [P, 2, FEAT]) for r in range(2)]
        dots = sb(ctx, "sc_dots", [P, LANES * HEADS])
        dsts = sb(ctx, "sc_dsts", [P, LANES, 1 + HEADS])
        score = [sb(ctx, f"sc_score{u}", [P, LANES * HEADS]) for u in range(2)]
        enc_p = [ps(ctx, f"sc_encp{r}", [P, 2, FEAT]) for r in range(2)]
        dst_p = [ps(ctx, f"sc_dstp{r}", [P, 2, 512]) for r in range(2)]
        s_w, s_ones, s_parts, s_parts_out, s_ew = (sem("sc_" + x) for x in ("w", "ones", "parts", "parts_out", "ew"))
        rows_in, rows_out = ([pair(f"sc_{x}{u}_") for u in range(2)] for x in ("rows_in", "rows_out"))
        score_out = pair("sc_score_out")
        dl_in, att_in = pair("sc_dl_in"), pair("sc_att_in")
        idx_ready, onehot_done = sem("sc_idx_ready"), sem("sc_onehot_done")
        enc_done = sem("sc_enc_done")
        relu_done, dst_done = sem("sc_relu_done"), sem("sc_dst_done")
        prod_done, read_done = sem("sc_prod_done"), sem("sc_read_done")
        dots_done, s_part = sem("sc_dots_done"), sem("sc_part")
        added_done = sem("sc_added_done")
        score_done = sem("sc_score_done")
        s_dve = sem("sc_dve")
        half = ITERS // 2
        with nc.Block() as block:
            @block.sync
            def _(sp):
                with nc.allow_non_contiguous_dma(reason="a small matrix"):
                    sp.dma_start(ew_left[0:3, :], A["L0_gnn_edge_W"].rearrange("k f -> f k")).then_inc(s_w, 16)
                sp.dma_start(ew_left[3:4, :], A["L0_gnn_edge_b"].rearrange("(o k) -> o k", o=1)).then_inc(s_w, 16)
                for u in range(2):
                    sp.sem_inc(score_out[u], 16)
                    for k in range(2):
                        sp.sem_inc(rows_out[u][k], 16)

                def load(m, u):
                    sp.dma_start(dl[u][:, :], AP(dloc_rows.tensor, m * (LANES * P), [[0, P], [1, LANES * P]])).then_inc(dl_in[u], 16)
                    n = PARTS * 3
                    for r in range(PARTS):
                        sp.dma_start(att[u][r * n:(r + 1) * n, :].rearrange("n (b l) -> n b l", l=P),
                                     AP(attr_rows.tensor, m * (LANES * AROW), [[P, n], [AROW, LANES], [1, P]])).then_inc(att_in[u], 16)

                def store(m, u, i):
                    for k in range(2):
                        sp.wait_ge(rows_in[u][k], 16 * HALF * (i + 1))
                        take_waits(sp, held)
                        sp.dma_start(gathered[bass.ds(m, 1), :, k * HALF * HROW:(k + 1) * HALF * HROW].rearrange("o p c -> (o p) c"),
                                     G[u][:, k * HALF:(k + 1) * HALF, :].rearrange("p b c -> p (b c)")).then_inc(rows_out[u][k], 16)
                    sp.wait_ge(score_done, m + 1)
                    take_waits(sp, held)
                    sp.dma_start(score_rows[bass.ds(m, 1), :, :].rearrange("o p c -> (o p) c"), score[u][:, :]).then_inc(score_out[u], 16)

                sp.wait_ge(s_ones, 2)
                load(0, 0)
                load(1, 1)
                sp.wait_ge(s_parts, 3 * PARTS - 2)
                sp.dma_start(enc_parts.rearrange("r f k -> f r k"), ew_parts[:, :, :]).then_inc(s_parts_out, 16)
                sp.wait_ge(s_parts_out, 16)
                for r in range(PARTS):
                    for n in range(PARTS):
                        k = (r * PARTS + n) * 3
                        sp.dma_start(ew[k:k + 3, :], enc_parts[r, 0:3, :]).then_inc(s_ew, 16)
                    sp.dma_start(ew[ENC - PARTS + r:ENC - PARTS + r + 1, :], enc_parts[r, 3:4, :]).then_inc(s_ew, 16)
                with sp.Fori(0, half - 1) as i:
                    for u in range(2):
                        m = 2 * i + u
                        store(m, u, i)
                        sp.wait_ge(onehot_done, PAIRS * (m + 1))
                        take_waits(sp, held)
                        sp.wait_ge(dst_done, PAIRS * (m + 1) + DEPTH)
                        take_waits(sp, held)
                        load(m + 2, u)
                for u in range(2):
                    store(ITERS - 2 + u, u, half - 1)
                for u in range(2):
                    for k in range(2):
                        sp.wait_ge(rows_out[u][k], 16 * (half + 1))
                    sp.wait_ge(score_out[u], 16 * (half + 1))

            @block.gpsimd
            def _(pool):
                for u in range(2):
                    nc.gpsimd.memset(att[u][:, :], 1.0).then_inc(s_ones, 1)
                with pool.Fori(0, half // 2) as i:
                    for v in range(4):
                        m, u = 4 * i + v, v % 2
                        pool.wait_ge(idx_ready, m + 1)
                        take_waits(pool, held)
                        pool.wait_ge(added_done, m + 1)
                        take_waits(pool, held)
                        for k in range(2):
                            pool.wait_ge(rows_out[u][k], 16 * (2 * i + v // 2 + 1))
                            take_waits(pool, held)
                            for b in range(k * HALF, (k + 1) * HALF):
                                pool.indirect_dma_start(G[u][:, b, :], None, gat_table,
                                                        bass.IndirectOffsetOnAxis(idx[v][:, b:b + 1], 0)).then_inc(rows_in[u][k], 16)

            @block.scalar
            def _(act):
                act.sem_inc(prod_done, 2)
                act.sem_inc(relu_done, 2)
                def indices(m, v):
                    nc.scalar.copy(idx[v][:, :], src_col[:, bass.ds(m * LANES, LANES)]).then_inc(idx_ready, 1)

                def relus(m):
                    for q in range(PAIRS):
                        n, r = m * PAIRS + q, q % 2
                        act.wait_ge(enc_done, n + 1)
                        act.wait_ge(prod_done, n + 1)
                        nc.scalar.activation(enc[r][:, :, :], enc_p[r][:, :, :], ACT.Relu).then_inc(relu_done, 1)

                def four(i, steps_ahead):
                    for v in range(4):
                        m = 4 * i + v
                        if v < steps_ahead:
                            act.wait_ge(added_done, m + 1)
                            indices(m + 2, (v + 2) % 4)
                        relus(m)

                indices(0, 0)
                indices(1, 1)
                with act.Fori(0, half // 2 - 1) as i:
                    four(i, 4)
                four(half // 2 - 1, 2)

            @block.vector
            def _(dve):
                link = Link(dve, s_dve)
                dve.sem_inc(dst_done, DEPTH)
                dve.sem_inc(read_done, 2)
                dve.sem_inc(added_done, 2)
                dve.wait_ge(s_w, 32)
                for r in range(PARTS):
                    nc.vector.tensor_copy(ew_parts[:, r, :], ew_left[:, :]).then_inc(s_parts, 1)
                    dve.wait_ge(s_parts, 3 * r + 1)
                    if r < PARTS - 1:
                        nc.vector.tensor_tensor(ew_left[:, :], ew_left[:, :], ew_parts[:, r, :], ALU.subtract).then_inc(s_parts, 2)
                        dve.wait_ge(s_parts, 3 * r + 3)

                def onehots(m, u, q, i):
                    if q == 0:
                        dve.wait_ge(dl_in[u], 16 * (i + 1))
                    dve.wait_ge(dst_done, m * PAIRS + q + 1)
                    nc.vector.tensor_scalar(onehot[q % DEPTH][:, :], dl[u][:, 2 * q * P:2 * (q + 1) * P], part_id[:, 0:1], None,
                                            ALU.is_equal).then_inc(onehot_done, 1)

                def iteration(m, u, i, more):
                    def product(q):
                        n, r = m * PAIRS + q, q % 2
                        dve.wait_ge(relu_done, n + 3)
                        dve.wait_ge(dst_done, n + 3 + DEPTH - 2)
                        if q >= 2:
                            dve.wait_ge(dots_done, n - 1)
                        nc.vector.tensor_tensor(prod[r][:, :, :], enc[r][:, :, :], dst_p[r][:, :, 0:FEAT], ALU.mult).then_inc(prod_done, 1)
                        nc.vector.tensor_copy(dsts[:, 2 * q:2 * q + 2, :], dst_p[r][:, :, FEAT:DROW]).then_inc(read_done, 1)
                        dve.wait_ge(prod_done, n + 3)
                        nc.vector.reduce_sum(dots[:, 2 * q * HEADS:2 * (q + 1) * HEADS],
                                             prod[r][:, :, :].rearrange("p s (h d) -> p (s h) d", d=HDIM), AXX).then_inc(dots_done, 1)

                    for q in range(PAIRS):
                        ahead = q + DEPTH - 2
                        if ahead < PAIRS:
                            onehots(m, u, ahead, i)
                        elif more:
                            onehots(m + 1, 1 - u, ahead - PAIRS, i + u)
                        product(q)
                    by_head = dots[:, :].rearrange("p (b h) -> p b h", h=HEADS)
                    dve.wait_ge(read_done, PAIRS * (m + 1) + 2)
                    dve.wait_ge(dots_done, PAIRS * (m + 1))
                    nc.vector.tensor_tensor(by_head, by_head, dsts[:, :, 1:1 + HEADS], ALU.add).then_inc(s_part, 1)
                    nc.vector.tensor_scalar(dsts[:, :, 0], dsts[:, :, 0], BIG, -BIG, ALU.mult, ALU.add).then_inc(s_part, 1)
                    dve.wait_ge(s_part, 2 * m + 2)
                    link(nc.vector.tensor_tensor(by_head, by_head, spread(dsts[:, :, :], [[1 + HEADS, LANES], [0, HEADS]]), ALU.add))
                    for k in range(2):
                        dve.wait_ge(rows_in[u][k], 16 * HALF * (i + 1))
                    link(nc.vector.tensor_tensor(by_head, by_head, G[u][:, :, 0:HEADS], ALU.add))
                    dve.sem_inc(added_done, 1)
                    dve.wait_ge(score_out[u], 16 * (i + 1))
                    link(nc.vector.scalar_tensor_tensor(score[u][:, :], dots[:, :], 0.2, dots[:, :], ALU.mult, ALU.max))
                    dve.sem_inc(score_done, 1)

                for q in range(DEPTH - 2):
                    onehots(0, 0, q, 0)
                with link.loop(half - 1, 2 * 3) as i:
                    for u in range(2):
                        iteration(2 * i + u, u, i, True)
                for u in range(2):
                    iteration(ITERS - 2 + u, u, half - 1, u == 0)

            @block.tensor
            def _(pe):
                pe.wait_ge(s_ew, 16 * (PARTS * PARTS + PARTS))
                flat = h_all[:, :, :].rearrange("p t c -> p (t c)")
                with pe.Fori(0, half) as i:
                    for u in range(2):
                        m = 2 * i + u
                        _, tiles = nc.values_load_multi_w_load_instructions(
                            tiles_row[0:1, bass.ds(m * LANES, LANES)], engines=[mybir.EngineType.PE], min_val=0, max_val=TILES - 1,
                            skip_runtime_bounds_check_because="tile numbers are clamped where they are worked out")
                        pe.wait_ge(att_in[u], 16 * PARTS * (i + 1))
                        for q in range(PAIRS):
                            n, r = m * PAIRS + q, q % 2
                            pe.wait_ge(relu_done, n + 1)
                            for s in range(2):
                                b = 2 * q + s
                                last = nc.tensor.matmul(enc_p[r][:, s, :], att[u][:, b * P:(b + 1) * P], ew[:, :], start=True, stop=True)
                            last.then_inc(enc_done, 1)
                            pe.wait_ge(onehot_done, n + 1)
                            pe.wait_ge(read_done, n + 1)
                            for s in range(2):
                                last = nc.tensor.matmul(dst_p[r][:, s, 0:DROW], onehot[q % DEPTH][:, s * P:(s + 1) * P],
                                                        flat[:, bass.ds(tiles[2 * q + s] * HCOL + HEADS, DROW)], start=True, stop=True)
                            last.then_inc(dst_done, 1)


def softmax_phase(nc, sb, ps, sem, pair, held, const, start_rows, score_rows, weight_rows):
    ident = const[5]
    COLS = ITERS * P
    J = 4
    TURNS = ITERS // J
    PIECE = 1024


    def backwards(t, hi, lo):
        return t[:, hi - 1:lo - 1:-1] if lo else t[:, hi - 1::-1]

    with ExitStack() as ctx:
        alpha = sb(ctx, "alpha", [P, COLS])
        start = sb(ctx, "start", [P, COLS + 1])
        top = sb(ctx, "top", [P, COLS])
        buf = [sb(ctx, f"sm_buf{u}", [P, J, P]) for u in range(2)]
        dump = [sb(ctx, f"sm_dump{u}", [P, PIECE]) for u in range(2)]
        weight = [sb(ctx, f"sm_weight{u}", [P, J * P]) for u in range(2)]
        any_start = sb(ctx, "any_start", [P, 2])
        carry = sb(ctx, "carry", [P, 1])
        line = sb(ctx, "line", [1, 3, P])
        turn = [ps(ctx, f"sm_turn{u}", [P, 512]) for u in range(2)]
        small = ps(ctx, "sm_small", [P, 3, P])
        s_flags, s_edge = sem("sm_flags"), sem("sm_edge")
        buf_in, buf_out = pair("sm_buf_in"), pair("sm_buf_out")
        turned, added = sem("sm_turned"), sem("sm_added")
        back, copied = sem("sm_back"), sem("sm_copied")
        s_dve, s_line, s_diff, s_exp = sem("sm_dve"), sem("sm_line"), sem("sm_diff"), sem("sm_exp")
        s_sum, s_pe, s_any = sem("sm_sum"), sem("sm_pe"), sem("sm_any")
        out_free = sem("sm_out_free")
        half = TURNS // 2
        with nc.Block() as block:
            @block.sync
            def _(sp):
                for u in range(2):
                    sp.dma_start(buf[u][:, :, :], score_rows[u * J:(u + 1) * J, :, :].rearrange("j e c -> e j c")).then_inc(buf_in[u], 16)
                with sp.Fori(0, half - 1) as i:
                    for u in range(2):
                        g = 2 * i + u
                        sp.wait_ge(turned, g + 1)
                        take_waits(sp, held)
                        sp.dma_start(buf[u][:, :, :], score_rows[bass.ds((g + 2) * J, J), :, :].rearrange("j e c -> e j c")).then_inc(buf_in[u], 16)
                sp.sem_inc(out_free, 2)
                with sp.Fori(0, half) as i:
                    for u in range(2):
                        g = 2 * i + u
                        sp.wait_ge(copied, g + 3)
                        take_waits(sp, held)
                        sp.dma_start(weight_rows[bass.ds(g * J, J), :, :].rearrange("j e c -> e j c"), buf[u][:, :, :]).then_inc(buf_out[u], 16)
                        sp.wait_ge(buf_out[u], 16 * (i + 1))
                        sp.sem_inc(out_free, 1)
                for u in range(2):
                    sp.wait_ge(buf_out[u], 16 * half)

            @block.scalar
            def _(act):
                act.wait_ge(s_edge, 1)
                for b in range(LANES):
                    w = COLS + (b < LANES - 1)
                    act.dma_start(start[b * HEADS:(b + 1) * HEADS, 0:w],
                                  AP(start_rows.tensor, b * COLS, [[0, HEADS], [1, w]])).then_inc(s_flags, 16)
                act.wait_ge(s_flags, 16 * LANES)
                for lo in range(2):
                    if lo:
                        act.wait_ge(s_any, lo)
                    nc.scalar.activation(top[:, :], start[:, lo:lo + COLS], ACT.Copy, accum_out=any_start[:, lo:lo + 1]).then_inc(s_any, 1)
                act.sem_inc(back, 2)
                act.wait_ge(s_diff, 1)
                with act.Fori(0, half) as i:
                    for u in range(2):
                        g = 2 * i + u
                        act.wait_ge(back, g + 1)
                        nc.scalar.activation(weight[u][:, :], alpha[:, bass.ds(g * (J * P), J * P)], ACT.Exp).then_inc(s_exp, 1)

            @block.gpsimd
            def _(pool):
                nc.gpsimd.memset(start[96:P, COLS:COLS + 1], -BIG).then_inc(s_edge, 1)

            @block.vector
            def _(dve):
                link = Link(dve, s_dve)
                dve.sem_inc(added, 2)
                dve.sem_inc(copied, 2)
                with dve.Fori(0, half) as i:
                    for u in range(2):
                        g = 2 * i + u
                        dve.wait_ge(turned, g + 1)
                        nc.vector.tensor_copy(alpha[:, bass.ds(g * (J * P), J * P)], turn[u][:, :]).then_inc(added, 1)
                dve.wait_ge(added, TURNS + 2)
                dve.wait_ge(s_flags, 16 * LANES)
                dve.wait_ge(s_any, 2)

                def across(first_in, first_out, step, lo):
                    dve.sem_inc(s_sum, 1)
                    k = lo
                    dve.wait_ge(s_pe, 2 * k + 1)
                    link(nc.vector.tensor_copy(line[0:1, 0:2, :], small[0:1, 0:2, :]))
                    link(nc.vector.memset(line[0:1, 2, :], -BIG))
                    def at(row, first, h):
                        one = line[0:1, row, first + h:first + h + 1]
                        return AP(one.tensor, one.offset, [list(one.ap[0]), [step, LANES - 1]])

                    for h in range(HEADS):
                        last = nc.vector.tensor_tensor_scan(out=at(2, first_out, h), data0=at(1, first_in, h), data1=at(0, first_in, h),
                                                            initial=-BIG, op0=ALU.add, op1=ALU.max)
                    link(last)
                    dve.sem_inc(s_line, 1)
                    dve.wait_ge(s_pe, 2 * k + 2)
                    link(nc.vector.tensor_copy(carry[:, :], small[:, 2, 0:1]))

                link(nc.vector.tensor_tensor_scan(out=top[:, :], data0=start[:, 0:COLS], data1=alpha[:, :], initial=-BIG, op0=ALU.add, op1=ALU.max))
                link(nc.vector.tensor_copy(dump[0][:, 0:1], top[:, COLS - 1:COLS]))
                across(0, HEADS, HEADS, 0)
                link(nc.vector.tensor_tensor_scan(out=top[:, :], data0=start[:, 0:COLS], data1=alpha[:, :], initial=carry[:, 0:1], op0=ALU.add, op1=ALU.max))
                prev = -BIG
                for k in range(COLS // PIECE):
                    hi = COLS - k * PIECE
                    lo = hi - PIECE
                    link(nc.vector.tensor_tensor_scan(out=dump[k % 2][:, :], data0=start[:, hi:lo:-1], data1=backwards(top, hi, lo),
                                                      initial=prev, op0=ALU.add, op1=ALU.max))
                    prev = dump[k % 2][:, PIECE - 1:PIECE]
                link(nc.vector.tensor_copy(dump[1][:, 0:1], prev))
                across(HEADS * (LANES - 1), HEADS * (LANES - 2), -HEADS, 1)
                link(nc.vector.tensor_tensor_scan(out=backwards(top, COLS, 0), data0=start[:, COLS:0:-1], data1=backwards(top, COLS, 0),
                                                  initial=carry[:, 0:1], op0=ALU.add, op1=ALU.max))
                nc.vector.tensor_tensor(alpha[:, :], alpha[:, :], top[:, :], ALU.subtract).then_inc(s_diff, 1)
                with dve.Fori(0, half) as i:
                    for u in range(2):
                        g = 2 * i + u
                        dve.wait_ge(back, g + 3)
                        dve.wait_ge(out_free, g + 1)
                        nc.vector.tensor_copy(buf[u][:, :, :], turn[u][:, :].rearrange("p (j c) -> p j c", c=P)).then_inc(copied, 1)

            @block.tensor
            def _(pe):
                with pe.Fori(0, half) as i:
                    for u in range(2):
                        g = 2 * i + u
                        pe.wait_ge(buf_in[u], 16 * (i + 1))
                        pe.wait_ge(added, g + 1)
                        for j in range(J):
                            last = nc.tensor.transpose(turn[u][:, j * P:(j + 1) * P], buf[u][:, j, :], ident[:, :])
                        last.then_inc(turned, 1)
                for k in range(2):
                    pe.wait_ge(s_sum, k + 1)
                    nc.tensor.transpose(small[0:1, 0, :], dump[k][:, 0:1], ident[:, :])
                    pe.wait_ge(s_any, k + 1)
                    nc.tensor.transpose(small[0:1, 1, :], any_start[:, k:k + 1], ident[:, :]).then_inc(s_pe, 1)
                    pe.wait_ge(s_line, k + 1)
                    nc.tensor.transpose(small[:, 2, 0:1], line[0:1, 2, :], ident[0:1, 0:1]).then_inc(s_pe, 1)
                with pe.Fori(0, half) as i:
                    for u in range(2):
                        g = 2 * i + u
                        pe.wait_ge(s_exp, g + 1)
                        pe.wait_ge(copied, g + 1)
                        for j in range(J):
                            last = nc.tensor.transpose(turn[u][:, j * P:(j + 1) * P], weight[u][:, j * P:(j + 1) * P], ident[:, :])
                        last.then_inc(back, 1)


def gat_sum_phase(nc, sb, ps, sem, pair, held, const, acc, S, gathered, weight_rows):
    src_col, dloc_col, tiles_row, iota_row, part_id, ident = const
    HALF, QUART = LANES // 2, LANES // 4
    R = 8
    MID = HROW // 2
    with ExitStack() as ctx:
        G = [sb(ctx, f"gs_g{u}", [P, LANES, HROW]) for u in range(2)]
        wt = [sb(ctx, f"gs_wt{u}", [P, LANES * HEADS]) for u in range(2)]
        dcol = [sb(ctx, f"gs_dcol{u}", [P, LANES]) for u in range(2)]
        sums = ps(ctx, "gs_sums", [P, R, 512])
        rows_in = [pair(f"gs_rows_in{u}_") for u in range(2)]
        wcopy_done, s_far = sem("gs_wcopy_done"), sem("gs_far")
        zeroed, dcol_ready = sem("gs_zeroed"), sem("gs_dcol_ready")
        onehot_done, sum_done = sem("gs_onehot_done"), sem("gs_sum_done")
        mul_done, add_done = sem("gs_mul_done"), sem("gs_add_done")
        half = ITERS // 2
        with nc.Block() as block:
            @block.sync
            def _(sp):
                with sp.Fori(0, half) as i:
                    for u in range(2):
                        m = 2 * i + u
                        for k in range(2):
                            sp.wait_ge(sum_done, LANES * m + HALF * (k + 1))
                            take_waits(sp, held)
                            b = slice(k * HALF, (k + 1) * HALF)
                            sp.dma_start(G[u][:, b, :].rearrange("p b c -> p (b c)"),
                                         gathered[bass.ds(m, 1), :, k * HALF * HROW:(k + 1) * HALF * HROW].rearrange("o p c -> (o p) c")).then_inc(rows_in[u][k], 16)
                            w = slice(k * HALF * HEADS, (k + 1) * HALF * HEADS)
                            sp.dma_start(wt[u][:, w], weight_rows[bass.ds(m, 1), :, w].rearrange("o p c -> (o p) c")).then_inc(rows_in[u][k], 16)

            @block.scalar
            def _(act):
                act.sem_inc(s_far, 1)
                one = iota_row[:, 1:2]

                def places(m, u):
                    act.wait_ge(onehot_done, LANES * (m + 1))
                    nc.scalar.copy(dcol[u][:, :], dloc_col[:, bass.ds(m * LANES, LANES)]).then_inc(dcol_ready, 1)
                    act.wait_ge(dcol_ready, m + 1)

                def distances(m, u, b):
                    act.wait_ge(sum_done, m * LANES + b + QUART)
                    for c in range(b, b + QUART):
                        last = nc.scalar.activation(S[:, u * LANES + c, :], iota_row[:, :], ACT.Abs, scale=-1.0, bias=dcol[u][:, c:c + 1])
                    last.then_inc(s_far, 1)

                def onehots(m, u, b):
                    act.wait_ge(s_far, 4 * m + b // QUART + 2)
                    four = S[:, u * LANES + b:u * LANES + b + QUART, :]
                    nc.scalar.activation(four, four, ACT.Relu, scale=-1.0, bias=one).then_inc(onehot_done, QUART)

                def weights(m, u, i, k):
                    act.wait_ge(rows_in[u][k], 32 * (i + 1))
                    w = wt[u][:, k * HALF * HEADS:(k + 1) * HALF * HEADS]
                    nc.scalar.copy(G[u][:, k * HALF:(k + 1) * HALF, 0:HEADS], w.rearrange("p (b h) -> p b h", h=HEADS)).then_inc(wcopy_done, 1)

                def iteration(m, u, i, more):
                    if more:
                        places(m + 1, 1 - u)
                    for b in range(0, LANES, QUART):
                        if more:
                            distances(m + 1, 1 - u, b)
                            if b:
                                onehots(m + 1, 1 - u, b - QUART)
                        if b % HALF == 0:
                            weights(m, u, i, b // HALF)
                    if more:
                        onehots(m + 1, 1 - u, LANES - QUART)

                act.sem_inc(onehot_done, 2 * LANES)
                places(0, 0)
                for b in range(0, LANES, QUART):
                    distances(0, 0, b)
                    onehots(0, 0, b)
                with act.Fori(0, half - 1) as i:
                    for u in range(2):
                        iteration(2 * i + u, u, i, True)
                for u in range(2):
                    iteration(ITERS - 2 + u, u, half - 1, u == 0)

            @block.gpsimd
            def _(pool):
                nc.gpsimd.memset(acc[:, 0:TILES // 2, :], 0.0).then_inc(zeroed, 1)
                with pool.Fori(0, half) as i:
                    for u in range(2):
                        for q in range(4):
                            if q % 2 == 0:
                                pool.wait_ge(rows_in[u][q // 2], 32 * (i + 1))
                                take_waits(pool, held)
                            w = wt[u][:, q * QUART * HEADS:(q + 1) * QUART * HEADS]
                            h = G[u][:, q * QUART:(q + 1) * QUART, H0:H1].rearrange("p b (h d) -> p b h d", d=HDIM)
                            nc.gpsimd.tensor_tensor(h, h, spread(w, [[HEADS, QUART], [1, HEADS], [0, HDIM]]), ALU.mult).then_inc(mul_done, 1)

            @block.vector
            def _(dve):
                dve.sem_inc(add_done, 2 * R)
                nc.vector.memset(acc[:, TILES // 2:TILES, :], 0.0).then_inc(zeroed, 1)
                dve.wait_ge(zeroed, 2)
                flat = acc[:, :, :].rearrange("p t c -> p (t c)")

                def iteration(m):
                    _, tiles = nc.values_load_multi_w_load_instructions(
                        tiles_row[0:1, bass.ds(m * LANES, LANES)], engines=[mybir.EngineType.DVE], min_val=0, max_val=TILES - 1,
                        skip_runtime_bounds_check_because="tile numbers are clamped where they are worked out")
                    for b in range(LANES):
                        n = m * LANES + b
                        if b % QUART == 0:
                            dve.wait_ge(sum_done, n + QUART + 2 * LANES)
                        for k, c in enumerate((slice(0, MID), slice(MID, HROW))):
                            dve.wait_ge(add_done, 2 * n + k + 2 * R - 1)
                            t = flat[:, bass.ds(tiles[b] * HROW + c.start, c.stop - c.start)]
                            nc.vector.tensor_tensor(t, t, sums[:, b % R, c], ALU.add).then_inc(add_done, 1)

                with dve.Fori(0, half) as i:
                    for u in range(2):
                        iteration(2 * i + u)

            @block.tensor
            def _(pe):
                pe.sem_inc(sum_done, 2 * LANES)
                with pe.Fori(0, half) as i:
                    for u in range(2):
                        m = 2 * i + u
                        for b in range(LANES):
                            n = m * LANES + b
                            if b % QUART == 0:
                                pe.wait_ge(onehot_done, n + QUART + 2 * LANES)
                                pe.wait_ge(add_done, 2 * (n + QUART))
                                pe.wait_ge(mul_done, 4 * m + b // QUART + 1)
                            if b % HALF == 0:
                                pe.wait_ge(wcopy_done, 2 * m + b // HALF + 1)
                            nc.tensor.matmul(sums[:, b % R, 0:HROW], S[:, u * LANES + b, :], G[u][:, b, :], start=True, stop=True).then_inc(sum_done, 1)


def mid_phase(nc, sb, ps, sem, pair, held, A, const, acc, acc1, dinv, x1_rows, conv1_table):
    with ExitStack() as ctx:
        w1 = sb(ctx, "w1", [P, 2, F1])
        bias = sb(ctx, "gat_bias", [P, FEAT])
        den = sb(ctx, "den", [P, GT, HEADS])
        deg = [sb(ctx, f"deg{u}", [P, GT]) for u in range(2)]
        s_w, deg_ready, root_ready = sem("md_w"), sem("md_deg_ready"), sem("md_root_ready")
        x1_out = pair("md_x1_out")

        def sync_before(sp):
            sp.dma_start(w1[:, :, :], A["L1_gnn_W1"].rearrange("(c p) k -> p c k", p=P)).then_inc(s_w, 16)
            sp.dma_start(bias[:, :], A["L0_gnn_bias"].partition_broadcast(P)).then_inc(s_w, 16)

        def pre(dve, link, g, u, xg, finish_done):
            if not (isinstance(g, int) and g == 0):
                dve.wait_ge(finish_done, (g - 1) * GT + 2)
            nc.vector.tensor_scalar(deg[u][:, :], acc[:, bass.ds(g * GT, GT), H1:HROW].rearrange("p t o -> p (t o)"), 1.0, None, ALU.add).then_inc(deg_ready, 1)
            link(nc.vector.tensor_scalar(den[:, :, :], acc[:, bass.ds(g * GT, GT), 0:HEADS], 1e-10, None, ALU.max))
            link(nc.vector.reciprocal(den[:, :, :], den[:, :, :]))
            h = acc[:, bass.ds(g * GT, GT), H0:H1].rearrange("p t (h d) -> p t h d", d=HDIM)
            link(nc.vector.tensor_tensor(h, h, spread(den[:, :, :], [[HEADS, GT], [1, HEADS], [0, HDIM]]), ALU.mult))
            link(nc.vector.tensor_tensor(xg[u][:, :, :], xg[u][:, :, :], acc[:, bass.ds(g * GT, GT), H0:H1], ALU.add))
            link(nc.vector.tensor_tensor(xg[u][:, :, :], xg[u][:, :, :], spread(bias[:, :], [[0, GT], [1, FEAT]]), ALU.add))

        def pre_late(dve, link, g, u):
            dve.wait_ge(root_ready, g + 1)
            link(nc.vector.reciprocal(deg[u][:, :], deg[u][:, :]))
            nc.vector.tensor_copy(dinv[:, bass.ds(g * GT, GT)], deg[u][:, :])

        def act_root(act, g, u):
            act.wait_ge(deg_ready, g + 1)
            nc.scalar.activation(deg[u][:, :], deg[u][:, :], ACT.Sqrt).then_inc(root_ready, 1)

        def hold(sp, g, u, i, xg, finish_done, stored):
            sp.dma_start(x1_rows[bass.ds(g * (GT * P), GT * P), :].rearrange("(a p) c -> p a c", p=P), xg[u][:, :, :]).then_inc(x1_out[u], 16)
            sp.wait_ge(x1_out[u], 16 * (i + 1))
            take_waits(sp, held)

        def finish_act(act, g, u, a, op, done):
            nc.scalar.activation(acc1[:, bass.ds(g * GT + a, 1), :].rearrange("p o c -> p (o c)"), op[:, 0:F1], ACT.Copy, scale=deg[u][:, a:a + 1]).then_inc(done, 1)

        def act_store(act, g, u, stored):
            act.dma_start(conv1_table[bass.ds(g * (GT * P), GT * P), :].rearrange("(a p) c -> p a c", p=P),
                          acc1[:, bass.ds(g * GT, GT), :]).then_inc(stored[u], 16)

        dense_phase(nc, sb, ps, sem, pair, held, const, "md", ctx, A["x"], NODES, [w1[:, 0, :], w1[:, 1, :]], F1,
                    lambda pe: pe.wait_ge(s_w, 32), pre=pre, pre_late=pre_late, pre_links=6, finish_act=finish_act, act_store=act_store,
                    hold=hold, act_first=act_root, sync_before=sync_before, dve_before=lambda dve, link: dve.wait_ge(s_w, 32))


def conv_phase(nc, sb, ps, sem, pair, held, const, name, width, acc, table):
    src_col, dloc_col, tiles_row, iota_row, part_id, ident = const
    R = 4
    with ExitStack() as ctx:
        idx = [sb(ctx, f"{name}_idx{u}", [P, LANES], I32) for u in range(2)]
        dcol = [sb(ctx, f"{name}_dcol{u}", [P, LANES]) for u in range(2)]
        G = [sb(ctx, f"{name}_g{u}", [P, LANES, width]) for u in range(2)]
        S = sb(ctx, f"{name}_S", [P, 2 * LANES, P])
        sums = ps(ctx, f"{name}_sums", [P, R, 512])
        idx_ready, dcol_ready, rows_in = sem(f"{name}_idx_ready"), sem(f"{name}_dcol_ready"), pair(f"{name}_rows_in")
        onehot_done = sem(f"{name}_onehot_done")
        sum_done, add_done = sem(f"{name}_sum_done"), sem(f"{name}_add_done")
        half = ITERS // 2
        with nc.Block() as block:
            @block.scalar
            def _(act):
                act.sem_inc(onehot_done, 2 * LANES)
                with act.Fori(0, half) as i:
                    for u in range(2):
                        m = 2 * i + u
                        act.wait_ge(sum_done, LANES * (m + 1))
                        nc.scalar.copy(idx[u][:, :], src_col[:, bass.ds(m * LANES, LANES)]).then_inc(idx_ready, 1)
                        act.wait_ge(onehot_done, LANES * (m + 1))
                        nc.scalar.copy(dcol[u][:, :], dloc_col[:, bass.ds(m * LANES, LANES)]).then_inc(dcol_ready, 1)

            @block.gpsimd
            def _(pool):
                with pool.Fori(0, half) as i:
                    for u in range(2):
                        pool.wait_ge(idx_ready, 2 * i + u + 1)
                        take_waits(pool, held)
                        for b in range(LANES):
                            pool.indirect_dma_start(G[u][:, b, :], None, table,
                                                    bass.IndirectOffsetOnAxis(idx[u][:, b:b + 1], 0)).then_inc(rows_in[u], 16)

            @block.vector
            def _(dve):
                dve.sem_inc(add_done, R)
                flat = acc[:, :, :].rearrange("p t c -> p (t c)")
                with dve.Fori(0, half) as i:
                    for u in range(2):
                        m = 2 * i + u
                        _, tiles = nc.values_load_multi_w_load_instructions(
                            tiles_row[0:1, bass.ds(m * LANES, LANES)], engines=[mybir.EngineType.DVE], min_val=0, max_val=TILES - 1,
                            skip_runtime_bounds_check_because="tile numbers are clamped where they are worked out")
                        dve.wait_ge(dcol_ready, m + 1)
                        for b in range(LANES):
                            dve.wait_ge(sum_done, m * LANES + b + 1)
                            nc.vector.tensor_scalar(S[:, u * LANES + b, :], iota_row[:, :], dcol[u][:, b:b + 1], None, ALU.is_equal).then_inc(onehot_done, 1)
                        for b in range(LANES):
                            n = m * LANES + b
                            dve.wait_ge(sum_done, n + 1 + 2 * LANES)
                            dve.wait_ge(add_done, n + R)
                            t = flat[:, bass.ds(tiles[b] * width, width)]
                            nc.vector.tensor_tensor(t, t, sums[:, b % R, 0:width], ALU.add).then_inc(add_done, 1)

            @block.tensor
            def _(pe):
                pe.sem_inc(sum_done, 2 * LANES)
                with pe.Fori(0, half) as i:
                    for u in range(2):
                        m = 2 * i + u
                        pe.wait_ge(rows_in[u], 16 * LANES * (i + 1))
                        for b in range(LANES):
                            n = m * LANES + b
                            pe.wait_ge(onehot_done, n + 1 + 2 * LANES)
                            pe.wait_ge(add_done, n + 1)
                            nc.tensor.matmul(sums[:, b % R, 0:width], S[:, u * LANES + b, :], G[u][:, b, :], start=True, stop=True).then_inc(sum_done, 1)


def norm_phase(nc, sb, ps, sem, A, const, name, width, acc, dinv, bias, gamma, beta):
    with ExitStack() as ctx:
        square = sb(ctx, f"{name}_square", [P, TILES, width])
        rows = sb(ctx, f"{name}_rows", [P, 3, width])
        ones = sb(ctx, f"{name}_ones", [P, 2, P])
        part_ok = sb(ctx, f"{name}_part_ok", [P, 1])
        mean = sb(ctx, f"{name}_mean", [P, width])
        var = sb(ctx, f"{name}_var", [P, width])
        root = sb(ctx, f"{name}_root", [P, width])
        total = [ps(ctx, f"{name}_total{k}", [P, 512]) for k in range(2)]
        s_rows, s_ones, s_dve = sem(f"{name}_rows_in"), sem(f"{name}_ones_ready"), sem(f"{name}_dve")
        s_vals, s_total, s_var, s_root, s_dev = (sem(f"{name}_{x}") for x in ("vals", "totals", "var_ready", "root_ready", "dev"))
        per = 512 // width
        whole = (TILES - 1) // per
        flat = acc[:, :, :].rearrange("p t c -> p (t c)")
        with nc.Block() as block:
            @block.sync
            def _(sp):
                for n, a in enumerate((bias, gamma, beta)):
                    sp.dma_start(rows[:, n, :], a.partition_broadcast(P)).then_inc(s_rows, 16)

            @block.vector
            def _(dve):
                link = Link(dve, s_dve)
                part_id = const[4]
                link(nc.vector.tensor_scalar(part_ok[:, :], part_id[:, :], float(LAST), None, ALU.is_lt))
                nc.vector.memset(ones[:, 0, :], 1.0)
                nc.vector.tensor_copy(ones[:, 1, :], spread(part_ok[:, :], [[0, P]])).then_inc(s_ones, 1)
                dve.wait_ge(s_rows, 48)

                def each(row):
                    return spread(row, [[0, TILES], [1, width]])

                link(nc.vector.tensor_tensor(acc[:, :, :], acc[:, :, :], spread(dinv[:, :], [[1, TILES], [0, width]]), ALU.mult))
                nc.vector.tensor_tensor(acc[:, :, :], acc[:, :, :], each(rows[:, 0, :]), ALU.add).then_inc(s_vals, 1)
                dve.wait_ge(s_total, 1)
                link(nc.vector.reduce_sum(mean[:, :], total[0][:, :].rearrange("p (a c) -> p c a", c=width), AXX))
                link(nc.vector.tensor_scalar(mean[:, :], mean[:, :], 1.0 / NODES, None, ALU.mult))
                nc.vector.tensor_tensor(acc[:, :, :], acc[:, :, :], each(mean[:, :]), ALU.subtract).then_inc(s_dev, 1)
                dve.wait_ge(s_total, 2)
                link(nc.vector.reduce_sum(var[:, :], total[1][:, :].rearrange("p (a c) -> p c a", c=width), AXX))
                nc.vector.tensor_scalar(var[:, :], var[:, :], 1.0 / NODES, EPS, ALU.mult, ALU.add).then_inc(s_var, 1)
                dve.wait_ge(s_root, 1)
                link(nc.vector.reciprocal(root[:, :], root[:, :]))
                link(nc.vector.tensor_tensor(root[:, :], root[:, :], rows[:, 1, :], ALU.mult))
                link(nc.vector.tensor_tensor(acc[:, :, :], acc[:, :, :], each(root[:, :]), ALU.mult))
                link(nc.vector.tensor_tensor(acc[:, :, :], acc[:, :, :], each(rows[:, 2, :]), ALU.add))

            @block.scalar
            def _(act):
                act.wait_ge(s_dev, 1)
                nc.scalar.activation(square[:, :, :], acc[:, :, :], ACT.Square).then_inc(s_dev, 1)
                act.wait_ge(s_var, 1)
                nc.scalar.activation(root[:, :], var[:, :], ACT.Sqrt).then_inc(s_root, 1)

            @block.tensor
            def _(pe):
                pe.wait_ge(s_ones, 1)
                for k, (src, ready, count) in enumerate(((flat, s_vals, 1), (square[:, :, :].rearrange("p t c -> p (t c)"), s_dev, 2))):
                    pe.wait_ge(ready, count)
                    for n in range(whole):
                        nc.tensor.matmul(total[k][:, :], ones[:, 0, :], src[:, n * 512:(n + 1) * 512], start=n == 0, stop=False)
                    for t in range(whole * per, TILES):
                        last = nc.tensor.matmul(total[k][:, 0:width], ones[:, int(t == TILES - 1), :], src[:, t * width:(t + 1) * width],
                                                start=False, stop=t == TILES - 1)
                    last.then_inc(s_total, 1)


def project_phase(nc, sb, ps, sem, pair, A, const, acc1, acc2, dinv, conv2_table):
    ident = const[5]
    with ExitStack() as ctx:
        w2 = sb(ctx, "w2", [P, F2])
        y = [sb(ctx, f"pj_y{r}", [P, F1]) for r in range(2)]
        yT = [sb(ctx, f"pj_yT{r}", [P, P]) for r in range(2)]
        tp = [ps(ctx, f"pj_tp{r}", [P, P]) for r in range(2)]
        op = [ps(ctx, f"pj_op{r}", [P, F2]) for r in range(2)]
        s_w, s_out = sem("pj_w"), sem("pj_out")
        relu_done, turn_done, copy_done = sem("pj_relu_done"), sem("pj_turn_done"), sem("pj_copy_done")
        product_done, finish_done = sem("pj_product_done"), sem("pj_finish_done")
        with nc.Block() as block:
            @block.sync
            def _(sp):
                sp.dma_start(w2[:, :], A["L1_gnn_W2"]).then_inc(s_w, 16)
                sp.wait_ge(finish_done, TILES + 2)
                sp.dma_start(conv2_table.rearrange("(t p) c -> p t c", p=P), acc2[:, :, :]).then_inc(s_out, 16)
                sp.wait_ge(s_out, 16)

            @block.scalar
            def _(act):
                for s in (turn_done, copy_done, product_done, finish_done):
                    act.sem_inc(s, 2)
                flat = acc1[:, :, :].rearrange("p t c -> p (t c)")
                with act.Fori(0, TILES // 2) as i:
                    for r in range(2):
                        t = 2 * i + r
                        act.wait_ge(turn_done, t + 1)
                        nc.scalar.activation(y[r][:, :], flat[:, bass.ds(t * F1, F1)], ACT.Relu).then_inc(relu_done, 1)

            @block.vector
            def _(dve):
                flat = acc2[:, :, :].rearrange("p t c -> p (t c)")

                def copy(t, r):
                    dve.wait_ge(turn_done, t + 3)
                    dve.wait_ge(product_done, t + 1)
                    nc.vector.tensor_copy(yT[r][:, :], tp[r][:, :]).then_inc(copy_done, 1)

                def finish(t, r):
                    dve.wait_ge(product_done, t + 3)
                    nc.vector.tensor_scalar(flat[:, bass.ds(t * F2, F2)], op[r][:, :], dinv[:, bass.ds(t, 1)], None, ALU.mult).then_inc(finish_done, 1)

                copy(0, 0)
                with dve.Fori(0, TILES // 2 - 1) as i:
                    for r in range(2):
                        copy(2 * i + r + 1, 1 - r)
                        finish(2 * i + r, r)
                copy(TILES - 1, 1)
                finish(TILES - 2, 0)
                finish(TILES - 1, 1)

            @block.tensor
            def _(pe):
                def turn(t, r):
                    pe.wait_ge(relu_done, t + 1)
                    pe.wait_ge(copy_done, t + 1)
                    nc.tensor.transpose(tp[r][:, :], y[r][:, :], ident[:, :]).then_inc(turn_done, 1)

                def product(t, r):
                    pe.wait_ge(copy_done, t + 3)
                    pe.wait_ge(finish_done, t + 1)
                    nc.tensor.matmul(op[r][:, :], yT[r][:, :], w2[:, :], start=True, stop=True).then_inc(product_done, 1)

                pe.wait_ge(s_w, 16)
                turn(0, 0)
                with pe.Fori(0, TILES // 2 - 1) as i:
                    for r in range(2):
                        turn(2 * i + r + 1, 1 - r)
                        product(2 * i + r, r)
                turn(TILES - 1, 1)
                product(TILES - 2, 0)
                product(TILES - 1, 1)


def final_phase(nc, sb, ps, sem, pair, held, A, const, acc1, acc2, x1_rows, out):
    with ExitStack() as ctx:
        wfc = sb(ctx, "wfc", [P, 4, FEAT])
        bias = sb(ctx, "fc_bias", [P, FEAT])
        res = [sb(ctx, f"fc_res{u}", [P, GT, FEAT]) for u in range(2)]
        s_w, out_done, res_free = sem("fn_w"), pair("fn_out_done"), sem("fn_res_free")

        def sync_before(sp):
            w = A["L1_gnn_Wfc"]
            sp.dma_start(wfc[:, 0:3, :], w[0:3 * P, :].rearrange("(c p) k -> p c k", p=P)).then_inc(s_w, 16)
            sp.dma_start(wfc[0:F2, 3, :], w[3 * P:3 * P + F2, :]).then_inc(s_w, 16)
            sp.dma_start(bias[:, :], A["L1_gnn_bfc"].partition_broadcast(P)).then_inc(s_w, 16)
            sp.sem_inc(res_free, 2)

        def finish_dve(dve, link, g, u, a, op, xg, done):
            if a == 0:
                dve.wait_ge(res_free, g + 1)
            link(nc.vector.tensor_tensor(res[u][:, a, :], op[:, 0:FEAT], bias[:, :], ALU.add))
            nc.vector.scalar_tensor_tensor(res[u][:, a, :], res[u][:, a, :], 0.0, xg[u][:, a, :], ALU.max, ALU.add).then_inc(done, 1)

        def hold(sp, g, u, i, xg, finish_done, stored):
            sp.wait_ge(finish_done, GT * (g + 1) + 2)
            take_waits(sp, held)
            r = g * (GT * P)
            full = GT - 1
            n = P if not isinstance(g, int) else min(P, NODES - g * GT * P - full * P)
            sp.dma_start(out[bass.ds(r, full * P), :].rearrange("(a p) c -> p a c", p=P), res[u][:, 0:full, :]).then_inc(out_done[u], 16)
            sp.dma_start(out[bass.ds(r + full * P, n), :], res[u][0:n, full, :]).then_inc(out_done[u], 16)

        def after(sp, g, u, i):
            sp.wait_ge(out_done[u], 32 * (i + 1))
            sp.sem_inc(res_free, 1)

        dense_phase(nc, sb, ps, sem, pair, held, const, "fn", ctx, x1_rows, TILES * P,
                    [wfc[:, 0, :], wfc[:, 1, :], wfc[:, 2, :], wfc[0:F2, 3, :]], FEAT,
                    lambda pe: pe.wait_ge(s_w, 48), extra=((acc1, F1), (acc2, F2)), finish_dve=finish_dve, hold=hold, after=after,
                    sync_before=sync_before, dve_before=lambda dve, link: dve.wait_ge(s_w, 48))


_INS = ["x", "src", "dst", "edge_attr_3", "L0_gnn_W", "L0_gnn_a_src", "L0_gnn_a_dst", "L0_gnn_edge_W",
        "L0_gnn_edge_b", "L0_gnn_bias", "L1_gnn_W1", "L1_gnn_b1", "L1_gnn_g1", "L1_gnn_be1", "L1_gnn_W2",
        "L1_gnn_b2", "L1_gnn_g2", "L1_gnn_be2", "L1_gnn_Wfc", "L1_gnn_bfc"]


def kernel(**inputs):
    import concourse.bacc as _bacc
    from concourse.bass_utils import run_bass_kernel_spmd as _run

    nc = _bacc.Bacc("TRN2", target_bir_lowering=False, num_devices=1)
    arrays, A = {}, {}
    for name in _INS:
        a = np.ascontiguousarray(inputs[name])
        arrays[f"in_{name}"] = a
        A[name] = nc.dram_tensor(f"in_{name}", a.shape, mybir.dt.from_np(a.dtype), kind="ExternalInput").ap()
    out = nc.dram_tensor("out", (NODES, FEAT), F32, kind="ExternalOutput").ap()
    gnn(nc, A, out)
    return _run(nc, [arrays], core_ids=[0]).results[0]["out"]
```

```python
from contextlib import ExitStack, contextmanager

import numpy as np

import concourse.bass as bass
from concourse import mybir
from concourse.bass import AP

F32 = mybir.dt.float32
BF16 = mybir.dt.bfloat16
I32 = mybir.dt.int32
ALU = mybir.AluOpType
ACT = mybir.ActivationFunctionType
AXX = mybir.AxisListType.X

P = 128
NODES, FEAT, EDGES = 12500, 256, 200000
HEADS, HDIM = 8, 32
F1, F2 = 128, 64
CHUNKS = -(-EDGES // P)
TILES = -(-NODES // P)
LAST = NODES - (TILES - 1) * P
Q = -(-(CHUNKS + TILES - 1) // P)
STEPS = Q * P
LANES = 16
ITERS = STEPS // LANES
PL = P // LANES
PARTS = 3
AROW = PARTS * 3 * P
EROW = 3 * P + AROW // 2
ENC = PARTS * PARTS * 3 + PARTS
HROW = HEADS + FEAT + 1
HCOL = HROW + HEADS
DROW = HCOL - HEADS
H0, H1 = HEADS, HEADS + FEAT
GT = 7
GROUPS = TILES // GT
BIG = 1.0e30
EPS = 1.0e-5
PAD_DST = 20000
EPP = Q * P
FULL_P = EDGES // EPP
REST = EDGES - FULL_P * EPP


class Link:

    def __init__(self, eng, sem):
        self.eng, self.sem, self.base, self.n = eng, sem, 0, 0

    def __call__(self, ins):
        self.n += 1
        ins.then_inc(self.sem, 1)
        self.eng.wait_ge(self.sem, self.base + self.n)

    @contextmanager
    def loop(self, trips, links):
        start = self.base + self.n
        with self.eng.Fori(0, trips) as i:
            self.base, self.n = i * links + start, 0
            yield i
            assert self.n == links, (self.n, links)
        self.base, self.n = start + trips * links, 0


def take_waits(eng, held):
    eng.sem_inc(held, 1)


def spread(ap, dims):
    return AP(ap.tensor, ap.offset, [list(ap.ap[0])] + [list(d) for d in dims])


def gnn(nc, A, out):
    held = nc.alloc_semaphore(name="held")
    top = ExitStack()
    in_phase = []

    def sem(name):
        in_phase.append(nc.alloc_semaphore(name=name))
        return in_phase[-1]

    def end_phase():
        nc.clear_and_free_semaphores(in_phase)
        nc.all_engine_barrier()
        in_phase.clear()

    def pair(name):
        return [sem(name + "0"), sem(name + "1")]

    def dram(name, shape, dt=F32):
        return nc.dram_tensor(name, shape, dt, kind="Internal").ap()

    edge_rows = dram("edge_rows", (STEPS, EROW))
    chunk_end = dram("chunk_end", (STEPS,))
    tile_of = dram("tile_of", (STEPS,), I32)
    dloc_rows = dram("dloc_rows", (ITERS, LANES, P), BF16)
    attr_rows = dram("attr_rows", (ITERS, LANES, AROW), BF16)
    enc_parts = dram("enc_parts", (PARTS, 4, FEAT), BF16)
    start_rows = dram("start_rows", (STEPS, P))
    gat_table = dram("gat_table", (TILES * P, HROW))
    gathered = dram("gathered", (ITERS, P, LANES * HROW))
    score_rows = dram("score_rows", (ITERS, P, LANES * HEADS))
    weight_rows = dram("weight_rows", (ITERS, P, LANES * HEADS))
    x1_rows = dram("x1_rows", (TILES * P, FEAT))
    z_rows = dram("z_rows", (TILES * P, FEAT))
    conv1_table = dram("conv1_table", (TILES * P, F1))
    conv2_table = dram("conv2_table", (TILES * P, F2))

    def sb(ctx, name, shape, dt=F32):
        return ctx.enter_context(nc.sbuf_tensor(name, shape, dt))

    def ps(ctx, name, shape, dt=F32):
        return ctx.enter_context(nc.psum_tensor(name, shape, dt))

    with top:
        src_col = sb(top, "src_col", [P, STEPS], I32)
        dloc_col = sb(top, "dloc_col", [P, STEPS])
        tiles_row = sb(top, "tiles_row", [1, STEPS], I32)
        iota_row = sb(top, "iota_row", [P, P])
        part_id = sb(top, "part_id", [P, 1])
        ident = sb(top, "ident", [P, P])
        const = (src_col, dloc_col, tiles_row, iota_row, part_id, ident)

        steps_phase(nc, sb, ps, sem, A, const, edge_rows, chunk_end, tile_of, dloc_rows, attr_rows,
                    start_rows)
        end_phase()
        with ExitStack() as ctx:
            h_all = sb(ctx, "h_all", [P, TILES, HCOL])
            node_phase(nc, sb, ps, sem, pair, held, A, const, h_all, gat_table)
            end_phase()
            score_phase(nc, sb, ps, sem, pair, held, A, const, h_all, gat_table, gathered, dloc_rows,
                        attr_rows, enc_parts, score_rows)
            end_phase()
        softmax_phase(nc, sb, ps, sem, pair, held, const, start_rows, score_rows, weight_rows)
        end_phase()
        with ExitStack() as ctx:
            acc1 = sb(ctx, "acc1", [P, TILES, F1])
            dinv = sb(ctx, "dinv", [P, TILES])
            x1_norm = [sb(ctx, f"x1_{n}", [P, TILES]) for n in ("scale", "shift")]
            with ExitStack() as ctx2:
                acc = sb(ctx2, "acc", [P, TILES, HROW])
                gat_sum_phase(nc, sb, ps, sem, pair, held, const, acc, acc1[:, 0:2 * LANES, :], gathered, weight_rows)
                end_phase()
                mid_phase(nc, sb, ps, sem, pair, held, A, const, acc, acc1, dinv, x1_norm, x1_rows, conv1_table)
                end_phase()
            conv_phase(nc, sb, ps, sem, pair, held, const, "c1", F1, acc1, conv1_table)
            end_phase()
            acc2 = sb(ctx, "acc2", [P, TILES, F2])
            norm_phase(nc, sb, ps, sem, A, const, "n1", F1, acc1, dinv,
                       A["L1_gnn_b1"], A["L1_gnn_g1"], A["L1_gnn_be1"])
            end_phase()
            project_phase(nc, sb, ps, sem, held, A, const, acc1, acc2, dinv, conv2_table)
            end_phase()
            with ExitStack() as ctx2:
                fc = FirstColumns(nc, sb, ps, sem, pair, held, A, const, ctx2, acc1, x1_norm, x1_rows, z_rows)
                conv_phase(nc, sb, ps, sem, pair, held, const, "c2", F2, acc2, conv2_table, fc)
            end_phase()
            norm_phase(nc, sb, ps, sem, A, const, "n2", F2, acc2, dinv,
                       A["L1_gnn_b2"], A["L1_gnn_g2"], A["L1_gnn_be2"])
            end_phase()
            final_phase(nc, sb, ps, sem, pair, held, A, const, acc2, x1_rows, z_rows, out)
            end_phase()


def steps_phase(nc, sb, ps, sem, A, const, edge_rows, chunk_end, tile_of, dloc_rows, attr_rows,
                start_rows):
    src_col, dloc_col, tiles_row, iota_row, part_id, ident = const
    with ExitStack() as ctx:
        dst_i = sb(ctx, "dst_i", [P, EPP], I32)
        prev_i = sb(ctx, "prev_i", [P, EPP], I32)
        src_i = sb(ctx, "src_i", [P, EPP], I32)
        attr = sb(ctx, "attr", [P, EPP * 3])
        rows = sb(ctx, "rows", [P, Q, EROW])
        parts = rows[:, :, 3 * P:EROW].bitcast(BF16)
        left = sb(ctx, "left", [P, Q, 3, P])
        ends = sb(ctx, "ends", [P, STEPS])
        below = sb(ctx, "below", [P, STEPS])
        order_i = sb(ctx, "order_i", [P, Q], I32)
        order = sb(ctx, "order", [P, Q])
        last_i = sb(ctx, "last_i", [P, Q], I32)
        last = sb(ctx, "last", [P, Q])
        chunk = sb(ctx, "chunk", [P, Q])
        chunk_i = sb(ctx, "chunk_i", [P, Q], I32)
        tile = sb(ctx, "tile", [P, Q])
        tile_i = sb(ctx, "tile_i", [P, Q], I32)
        base = sb(ctx, "base", [P, Q])
        valid = sb(ctx, "valid", [P, Q, P])
        dclip = sb(ctx, "dclip", [P, Q, P])
        dclip16 = sb(ctx, "dclip16", [P, Q, P], BF16)
        iota_i = sb(ctx, "iota_i", [P, P], I32)
        part_i = sb(ctx, "part_i", [P, 1], I32)
        turn = ps(ctx, "turn_s", [P, 4, 512])
        s_pads, s_loads, s_rows, s_rows_out = sem("st_pads"), sem("st_loads"), sem("st_rows"), sem("st_rows_out")
        s_end, s_end_out, s_end_in = sem("st_end"), sem("st_end_out"), sem("st_end_in")
        s_chunk, s_step_rows, s_iota, s_ident = sem("st_chunk"), sem("st_step_rows"), sem("st_iota"), sem("st_ident")
        s_tile, s_tile_out, s_tile_in = sem("st_tile"), sem("st_tile_out"), sem("st_tile_in")
        s_clip, s_left = sem("st_clip"), sem("st_left")
        s_ready, s_out, s_turned, s_taken = sem("st_ready"), sem("st_out"), sem("st_turned"), sem("st_taken")
        s_dve = sem("st_dve")

        def part(n):
            return parts[:, :, n * 3 * P:(n + 1) * 3 * P].rearrange("p q (f e) -> p q f e", e=P)

        with nc.Block() as block:
            @block.sync
            def _(sp):
                sp.wait_ge(s_pads, 4)
                a3 = A["edge_attr_3"].rearrange("e f -> (e f)")
                for t, a, w in ((dst_i, A["dst"], 1), (src_i, A["src"], 1), (attr, a3, 3)):
                    sp.dma_start(t[0:FULL_P, :], a[0:FULL_P * EPP * w].rearrange("(p e) -> p e", e=EPP * w)).then_inc(s_loads, 16)
                    sp.dma_start(t[FULL_P:FULL_P + 1, 0:REST * w], a[FULL_P * EPP * w:].rearrange("(p e) -> p e", p=1)).then_inc(s_loads, 16)
                d = A["dst"]
                sp.dma_start(prev_i[0:1, 1:EPP], d[0:EPP - 1].rearrange("(p e) -> p e", p=1)).then_inc(s_loads, 16)
                sp.dma_start(prev_i[1:FULL_P, :], d[EPP - 1:FULL_P * EPP - 1].rearrange("(p e) -> p e", e=EPP)).then_inc(s_loads, 16)
                sp.dma_start(prev_i[FULL_P:FULL_P + 1, 0:REST], d[FULL_P * EPP - 1:EDGES - 1].rearrange("(p e) -> p e", p=1)).then_inc(s_loads, 16)
                sp.wait_ge(s_end, 1)
                sp.dma_start(chunk_end.rearrange("(p q) -> p q", q=Q), last[:, :]).then_inc(s_end_out, 16)
                sp.wait_ge(s_end_out, 16)
                sp.dma_start(ends[:, :], AP(chunk_end.tensor, 0, [[0, P], [1, STEPS]])).then_inc(s_end_in, 16)
                sp.wait_ge(s_rows, 2)
                sp.dma_start(edge_rows.rearrange("(p q) e -> p q e", q=Q), rows[:, :, :]).then_inc(s_rows_out, 16)
                sp.wait_ge(s_tile, 1)
                with nc.allow_non_contiguous_dma(reason="one small table"):
                    for b in range(LANES):
                        sp.dma_start(AP(tile_of.tensor, b, [[Q * LANES, PL], [LANES, Q], [1, 1]]),
                                     tile_i[b * PL:(b + 1) * PL, :].rearrange("p (q o) -> p q o", o=1)).then_inc(s_tile_out, 16)
                sp.wait_ge(s_tile_out, 16 * LANES)
                sp.dma_start(tiles_row[:, :], tile_of.rearrange("(o k) -> o k", o=1)).then_inc(s_tile_in, 16)
                sp.wait_ge(s_ready, 1)
                sp.dma_start(start_rows.rearrange("(p q) e -> p q e", q=Q), rows[:, :, 2 * P:3 * P]).then_inc(s_out, 16)
                for b in range(LANES):
                    p = slice(b * PL, (b + 1) * PL)
                    sp.dma_start(AP(dloc_rows.tensor, b * P, [[Q * LANES * P, PL], [LANES * P, Q], [1, P]]),
                                 dclip16[p, :, :]).then_inc(s_out, 16)
                    sp.dma_start(AP(attr_rows.tensor, b * AROW, [[Q * LANES * AROW, PL], [LANES * AROW, Q], [1, AROW]]),
                                 parts[p, :, :]).then_inc(s_out, 16)
                sp.wait_ge(s_tile_in, 16)
                sp.wait_ge(s_out, 16 * (1 + 2 * LANES))

            @block.gpsimd
            def _(pool):
                nc.gpsimd.memset(dst_i[:, :], PAD_DST).then_inc(s_pads, 1)
                nc.gpsimd.memset(src_i[:, :], 0).then_inc(s_pads, 1)
                nc.gpsimd.memset(attr[:, :], 0.0).then_inc(s_pads, 1)
                nc.gpsimd.memset(prev_i[:, :], -1).then_inc(s_pads, 1)
                nc.gpsimd.iota(order_i[:, :], pattern=[[1, Q]], base=0, channel_multiplier=Q).then_inc(s_iota, 1)
                nc.gpsimd.iota(iota_i[:, :], pattern=[[1, P]], base=0, channel_multiplier=0).then_inc(s_iota, 1)
                nc.gpsimd.iota(part_i[:, :], pattern=[[0, 1]], base=0, channel_multiplier=1).then_inc(s_iota, 1)
                nc.gpsimd.memset(ident[:, :], 0.0).then_inc(s_ident, 1)
                pool.wait_ge(s_ident, 1)
                nc.gpsimd.affine_select(out=ident[:, :], in_=ident[:, :], compare_op=ALU.not_equal, fill=1.0,
                                        base=0, pattern=[[-1, P]], channel_multiplier=1).then_inc(s_ident, 1)
                pool.wait_ge(s_rows_out, 16)
                pool.wait_ge(s_chunk, 1)
                for q in range(Q):
                    pool.indirect_dma_start(rows[:, q, :], None, edge_rows,
                                            bass.IndirectOffsetOnAxis(chunk_i[:, q:q + 1], 0)).then_inc(s_step_rows, 16)

            @block.vector
            def _(dve):
                link = Link(dve, s_dve)
                dve.wait_ge(s_iota, 3)
                nc.vector.tensor_copy(iota_row[:, :], iota_i[:, :])
                nc.vector.tensor_copy(part_id[:, :], part_i[:, :])
                nc.vector.tensor_copy(order[:, :], order_i[:, :])
                dve.wait_ge(s_loads, 16 * 9)
                link(nc.vector.tensor_scalar(last_i[:, :], dst_i[:, :].rearrange("p (q e) -> p q e", e=P)[:, :, P - 1],
                                             7, None, ALU.arith_shift_right))
                link(nc.vector.tensor_scalar(last[:, :], last_i[:, :], float(TILES - 1), None, ALU.min))
                nc.vector.tensor_tensor(last[:, :], last[:, :], order[:, :], ALU.add).then_inc(s_end, 1)
                for n, t in enumerate((src_i, dst_i, prev_i)):
                    i = nc.vector.tensor_copy(rows[:, :, n * P:(n + 1) * P], t[:, :].rearrange("p (q e) -> p q e", e=P))
                    if n == 2:
                        i.then_inc(s_rows, 1)
                dve.wait_ge(s_end_in, 16)
                for q in range(Q):
                    if q % 3 == 0 and q // 3 < PARTS - 1:
                        n = q // 3
                        dve.wait_ge(s_left, 2 * n + 2)
                        nc.vector.tensor_tensor(left[:, :, :, :], left[:, :, :, :], part(n), ALU.subtract).then_inc(s_left, 1)
                    link(nc.vector.tensor_scalar(below[:, :], ends[:, :], order[:, q:q + 1], None, ALU.is_lt))
                    link(nc.vector.reduce_sum(chunk[:, q:q + 1], below[:, :], AXX))
                nc.vector.tensor_copy(chunk_i[:, :], chunk[:, :]).then_inc(s_chunk, 1)
                link(nc.vector.tensor_tensor(tile[:, :], order[:, :], chunk[:, :], ALU.subtract))
                nc.vector.tensor_copy(tile_i[:, :], tile[:, :]).then_inc(s_tile, 1)
                link(nc.vector.tensor_scalar(base[:, :], tile[:, :], float(P), None, ALU.mult))
                dve.wait_ge(s_step_rows, 16 * Q)
                link(nc.vector.tensor_tensor(rows[:, :, P:2 * P], rows[:, :, P:2 * P], spread(base[:, :], [[1, Q], [0, P]]), ALU.subtract))
                link(nc.vector.tensor_tensor(rows[:, :, 2 * P:3 * P], rows[:, :, 2 * P:3 * P], spread(base[:, :], [[1, Q], [0, P]]), ALU.subtract))
                link(nc.vector.tensor_scalar(valid[:, :, :], rows[:, :, P:2 * P], float(P - 1), None, ALU.is_le))
                link(nc.vector.scalar_tensor_tensor(valid[:, :, :], rows[:, :, P:2 * P], 0.0, valid[:, :, :], ALU.is_ge, ALU.mult))
                link(nc.vector.tensor_scalar(dclip[:, :, :], rows[:, :, P:2 * P], -1.0, float(P), ALU.max, ALU.min))
                dve.sem_inc(s_clip, 1)
                link(nc.vector.tensor_copy(dclip16[:, :, :], dclip[:, :, :]))
                link(nc.vector.tensor_tensor(rows[:, :, 2 * P:3 * P], rows[:, :, P:2 * P], rows[:, :, 2 * P:3 * P], ALU.not_equal))
                nc.vector.scalar_tensor_tensor(rows[:, :, 2 * P:3 * P], rows[:, :, 2 * P:3 * P], -BIG, valid[:, :, :], ALU.mult, ALU.mult).then_inc(s_ready, 1)

            @block.tensor
            def _(pe):
                pe.wait_ge(s_ident, 2)
                pe.wait_ge(s_step_rows, 16 * Q)
                for n in range(2 * Q):
                    if n == Q:
                        pe.wait_ge(s_clip, 1)
                    if n >= 4:
                        pe.wait_ge(s_taken, n - 3)
                    rows_n = rows[:, n, 0:P] if n < Q else dclip[:, n - Q, :]
                    nc.tensor.transpose(turn[:, n % 4, 0:P], rows_n, ident[:, :]).then_inc(s_turned, 1)

            @block.scalar
            def _(act):
                act.wait_ge(s_loads, 16 * 9)
                nc.scalar.copy(left[:, :, :, :], attr[:, :].rearrange("p (q e f) -> p q f e", e=P, f=3)).then_inc(s_left, 1)
                for n in range(PARTS):
                    act.wait_ge(s_left, 2 * n + 1)
                    nc.scalar.copy(part(n), left[:, :, :, :]).then_inc(s_left if n < PARTS - 1 else s_rows, 1)
                views = [t[:, :].rearrange("e (pl q b) -> e q b pl", q=Q, b=LANES) for t in (src_col, dloc_col)]
                for n in range(2 * Q):
                    act.wait_ge(s_turned, n + 1)
                    nc.scalar.copy(views[n // Q][:, n % Q, :, :],
                                   turn[:, n % 4, 0:P].rearrange("e (b pl) -> e b pl", pl=PL)).then_inc(s_taken, 1)


def load_groups(sp, src, xg, s_in, waits, rows):
    def load(g, u):
        r = g * (GT * P)
        full = GT - 1
        sp.dma_start(xg[u][:, 0:full, :], src[bass.ds(r, full * P), :].rearrange("(a p) c -> p a c", p=P)).then_inc(s_in[u], 16)
        n = P if not isinstance(g, int) else min(P, rows - g * GT * P - full * P)
        sp.dma_start(xg[u][0:n, full, :], src[bass.ds(r + full * P, n), :]).then_inc(s_in[u], 16)

    load(0, 0)
    load(1, 1)
    half = GROUPS // 2
    with sp.Fori(0, half - 2) as i:
        for u in range(2):
            waits(2 * i + u, u, i)
            load(2 * i + u + 2, u)
    for g in range(GROUPS - 4, GROUPS):
        waits(g, g % 2, g // 2)
        if g + 2 < GROUPS:
            load(g + 2, g % 2)


def dense_phase(nc, sb, ps, sem, pair, held, const, name, ctx, src, rows, weights, nout, w_ready,
                pre=None, pre_links=0, keep=None, finish_act=None, act_store=None,
                hold=None, act_before=None, pool=None, tensor_before=None, dve_before=None, sync_before=None):
    ident = const[5]
    xg = [sb(ctx, f"{name}_x{u}", [P, GT, FEAT]) for u in range(2)]
    hn = sb(ctx, f"{name}_hn", [P, GT, FEAT])
    hT = [sb(ctx, f"{name}_hT{r}", [P, 2, P]) for r in range(2)]
    stats = sb(ctx, f"{name}_stats", [P, GT, 6])
    mv = sb(ctx, f"{name}_mv", [P, GT, 2])
    var = sb(ctx, f"{name}_var", [P, GT])
    sd = sb(ctx, f"{name}_sd", [P, GT])
    rstd = [sb(ctx, f"{name}_rstd{u}", [P, GT]) for u in range(2)]
    shift = [sb(ctx, f"{name}_shift{u}", [P, GT]) for u in range(2)]
    tp = [ps(ctx, f"{name}_tp{r}", [P, 4, P]) for r in range(2)]
    op = [ps(ctx, f"{name}_op{r}", [P, 512]) for r in range(2)]
    x_in = pair(f"{name}_x_in")
    s_var, s_sd, s_norm = sem(f"{name}_var_ready"), sem(f"{name}_sd_ready"), sem(f"{name}_norm_ready")
    relu_done, turn_done = sem(f"{name}_relu_done"), sem(f"{name}_turn_done")
    copy_done, product_done = sem(f"{name}_copy_done"), sem(f"{name}_product_done")
    finish_done = sem(f"{name}_finish_done")
    s_dve = sem(f"{name}_dve")
    stored = pair(f"{name}_stored")
    half = GROUPS // 2
    with nc.Block() as block:
        @block.sync
        def _(sp):
            if sync_before:
                sync_before(sp)

            def waits(g, u, i):
                sp.wait_ge(relu_done, GT * (g + 1) + 2 * GT)
                take_waits(sp, held)
                if hold:
                    hold(sp, g, u, i, xg, finish_done, stored)
            load_groups(sp, src, xg, x_in, waits, rows)

        if pool:
            @block.gpsimd
            def _(p):
                pool(p)

        @block.vector
        def _(dve):
            link = Link(dve, s_dve)
            dve.sem_inc(relu_done, 2 * GT)
            dve.sem_inc(turn_done, GT)
            for s in (copy_done, product_done, finish_done):
                dve.sem_inc(s, 2)
            for s in (s_sd, s_norm):
                dve.sem_inc(s, 1)
            if dve_before:
                dve_before(dve, link)

            def begin(g, u, i):
                dve.wait_ge(x_in[u], 32 * (i + 1))
                if pre:
                    pre(dve, link, g, u, xg)

            def statistics(g, u):
                take_waits(dve, held)
                for a in range(GT):
                    last = nc.vector.bn_aggr(mv[:, a, :], stats[:, a, :])
                link(last)
                dve.wait_ge(s_sd, g + 1)
                nc.vector.tensor_scalar(var[:, :], mv[:, :, 1], EPS, None, ALU.add).then_inc(s_var, 1)
                dve.wait_ge(s_sd, g + 2)
                dve.wait_ge(relu_done, GT * (g + 1))
                link(nc.vector.reciprocal(rstd[u][:, :], sd[:, :]))
                link(nc.vector.scalar_tensor_tensor(shift[u][:, :], mv[:, :, 0], -1.0, rstd[u][:, :], ALU.mult, ALU.mult))
                dve.sem_inc(s_norm, 1)
                if keep:
                    nc.vector.tensor_copy(keep[0][:, bass.ds(g * GT, GT)], rstd[u][:, :])
                    nc.vector.tensor_copy(keep[1][:, bass.ds(g * GT, GT)], shift[u][:, :])

            def sums(u, tiles):
                for a in tiles:
                    last = nc.vector.bn_stats(stats[:, a, :], xg[u][:, a, :])
                if GT - 1 in tiles:
                    link(last)

            def group(g, u, i, more):
                for a in range(GT):
                    n, r = g * GT + a, (u * GT + a) % 2
                    dve.wait_ge(turn_done, n + 1 + GT)
                    dve.wait_ge(product_done, n + 1)
                    nc.vector.tensor_copy(hT[r][:, :, :], tp[r][:, 0:2, :]).then_inc(copy_done, 1)
                    if more and a == 0:
                        begin(g + 1, 1 - u, i + u)
                        sums(1 - u, [0])
                    if more and a in (1, 2):
                        sums(1 - u, [3 * a - 2, 3 * a - 1, 3 * a])
                    if more and a == 3:
                        statistics(g + 1, 1 - u)

            begin(0, 0, 0)
            sums(0, range(GT))
            statistics(0, 0)
            with link.loop(half - 1, 2 * (4 + pre_links)) as i:
                for u in range(2):
                    group(2 * i + u, u, i, True)
            group(GROUPS - 2, 0, half - 1, True)
            group(GROUPS - 1, 1, half - 1, False)

        @block.scalar
        def _(act):
            def root(g, u):
                act.wait_ge(s_var, g + 1)
                act.wait_ge(s_norm, g + 1)
                nc.scalar.activation(sd[:, :], var[:, :], ACT.Sqrt).then_inc(s_sd, 1)

            def relu(g, u, tiles):
                for a in tiles:
                    n, r = g * GT + a, (u * GT + a) % 2
                    if a == 0:
                        act.wait_ge(s_norm, g + 2)
                    act.wait_ge(turn_done, n + 1)
                    nc.scalar.activation(hn[:, a, :], xg[u][:, a, :], ACT.Relu, bias=shift[u][:, a:a + 1],
                                         scale=rstd[u][:, a:a + 1]).then_inc(relu_done, 1)

            def group(g, u, more):
                for a in range(GT):
                    if more and a == 3:
                        root(g + 1, 1 - u)
                    act.wait_ge(product_done, g * GT + a + 3)
                    finish_act(act, g, u, a, op[(u * GT + a) % 2], finish_done)
                    if more and a == 4:
                        relu(g + 1, 1 - u, range(3))
                    if more and a == 5:
                        relu(g + 1, 1 - u, range(3, 5))
                if more:
                    relu(g + 1, 1 - u, range(5, GT))
                act.wait_ge(finish_done, (g + 1) * GT + 2)
                act_store(act, g, u, stored)

            if act_before:
                act_before(act)
            root(0, 0)
            relu(0, 0, range(GT))
            with act.Fori(0, half - 1) as i:
                for u in range(2):
                    group(2 * i + u, u, True)
            group(GROUPS - 2, 0, True)
            group(GROUPS - 1, 1, False)
            for u in range(2):
                act.wait_ge(stored[u], 16 * half)

        @block.tensor
        def _(pe):
            if tensor_before:
                tensor_before(pe)
            w_ready(pe)

            def turn(g, u, a):
                n, r = g * GT + a, (u * GT + a) % 2
                pe.wait_ge(relu_done, n + 1 + 2 * GT)
                pe.wait_ge(copy_done, n + 1)
                for c in range(2):
                    last = nc.tensor.transpose(tp[r][:, c, :], hn[:, a, c * P:(c + 1) * P], ident[:, :])
                last.then_inc(turn_done, 1)

            def product(g, u, a):
                n, r = g * GT + a, (u * GT + a) % 2
                pe.wait_ge(copy_done, n + 3)
                pe.wait_ge(finish_done, n + 1)
                for c in range(2):
                    last = nc.tensor.matmul(op[r][:, 0:nout], hT[r][:, c, :], weights[c], start=c == 0, stop=c == 1)
                last.then_inc(product_done, 1)

            with pe.Fori(0, half) as i:
                for u in range(2):
                    g = 2 * i + u
                    turn(g, u, 0)
                    for a in range(GT):
                        if a < GT - 1:
                            turn(g, u, a + 1)
                        product(g, u, a)


def node_phase(nc, sb, ps, sem, pair, held, A, const, h_all, gat_table):
    ident = const[5]
    with ExitStack() as ctx:
        w_sb = sb(ctx, "w_sb", [P, 2, FEAT])
        score = sb(ctx, "score", [P, 2, 2])
        heads = sb(ctx, "heads", [P, 2, 2 * HEADS])
        w_t = sb(ctx, "w_t", [P, 2, HCOL])
        wp = ps(ctx, "wp", [P, 4, 512])
        s_w, s_heads, s_zero = sem("nd_w"), sem("nd_heads"), sem("nd_zero")
        s_wturn, s_wcopy = sem("nd_wturn"), sem("nd_wcopy")

        def sync_before(sp):
            sp.dma_start(w_sb[:, :, :], A["L0_gnn_W"].rearrange("(c p) k -> p c k", p=P)).then_inc(s_w, 16)
            with nc.allow_non_contiguous_dma(reason="two vectors"):
                for n, a in enumerate((A["L0_gnn_a_src"], A["L0_gnn_a_dst"])):
                    sp.dma_start(score[:, n, :], a.rearrange("h d -> (h d)").rearrange("(c p) -> p c", p=P)).then_inc(s_w, 16)

        def dve_before(dve, link):
            nc.vector.memset(h_all[:, :, H1:H1 + 1], 1.0)
            nc.vector.memset(w_t[:, :, H1:H1 + 1], 0.0)
            link(nc.vector.memset(heads[:, :, :], 0.0))
            dve.wait_ge(s_w, 48)
            for n in range(2):
                for c in range(2):
                    for q in range(4):
                        col = n * HEADS + c * 4 + q
                        last = nc.vector.tensor_copy(heads[q * HDIM:(q + 1) * HDIM, c, col:col + 1],
                                                     score[q * HDIM:(q + 1) * HDIM, n, c:c + 1])
            last.then_inc(s_heads, 1)
            for n in range(4):
                dve.wait_ge(s_wturn, n + 1)
                last = nc.vector.tensor_copy(w_t[:, n % 2, H0 + n // 2 * P:H0 + (n // 2 + 1) * P], wp[:, n, 0:P])
            last.then_inc(s_wcopy, 1)
            for c in range(2):
                dve.wait_ge(s_wturn, 5 + c)
                nc.vector.tensor_copy(w_t[:, c, 0:HEADS], wp[:, c, P:P + HEADS])
                last = nc.vector.tensor_copy(w_t[:, c, HROW:HCOL], wp[:, c, P + HEADS:P + 2 * HEADS])
            last.then_inc(s_wcopy, 1)

        def tensor_before(pe):
            pe.wait_ge(s_w, 48)
            for n in range(4):
                nc.tensor.transpose(wp[:, n, 0:P], w_sb[:, n // 2, n % 2 * P:(n % 2 + 1) * P], ident[:, :]).then_inc(s_wturn, 1)
            pe.wait_ge(s_heads, 1)
            pe.wait_ge(s_wcopy, 1)
            for c in range(2):
                for k in range(2):
                    last = nc.tensor.matmul(wp[:, c, P:P + 2 * HEADS], w_sb[:, k, c * P:(c + 1) * P], heads[:, k, :],
                                            start=k == 0, stop=k == 1)
                last.then_inc(s_wturn, 1)

        def finish_act(act, g, u, a, op, done):
            nc.scalar.copy(h_all[:, :, :].rearrange("p t c -> p (t c)")[:, bass.ds((g * GT + a) * HCOL, H1)], op[:, 0:H1])
            nc.scalar.copy(h_all[:, :, :].rearrange("p t c -> p (t c)")[:, bass.ds((g * GT + a) * HCOL + HROW, HEADS)],
                           op[:, HROW:HCOL]).then_inc(done, 1)

        def act_store(act, g, u, stored):
            act.dma_start(gat_table[bass.ds(g * (GT * P), GT * P), :].rearrange("(a p) c -> p a c", p=P),
                          h_all[:, bass.ds(g * GT, GT), 0:HROW]).then_inc(stored[u], 16)

        dense_phase(nc, sb, ps, sem, pair, held, const, "nd", ctx, A["x"], NODES, [w_t[:, 0, :], w_t[:, 1, :]], HCOL,
                    lambda pe: pe.wait_ge(s_wcopy, 2), finish_act=finish_act, act_store=act_store,
                    tensor_before=tensor_before, dve_before=dve_before, sync_before=sync_before)


def score_phase(nc, sb, ps, sem, pair, held, A, const, h_all, gat_table, gathered, dloc_rows, attr_rows, enc_parts,
                score_rows):
    src_col, dloc_col, tiles_row, iota_row, part_id, ident = const
    PAIRS, HALF = LANES // 2, LANES // 2
    DEPTH = 4
    with ExitStack() as ctx:
        idx = [sb(ctx, f"sc_idx{v}", [P, LANES], I32) for v in range(4)]
        G = [sb(ctx, f"sc_g{u}", [P, LANES, HROW]) for u in range(2)]
        dl = [sb(ctx, f"sc_dl{u}", [P, LANES * P], BF16) for u in range(2)]
        att = [sb(ctx, f"sc_att{u}", [ENC, LANES * P], BF16) for u in range(2)]
        ew_left = sb(ctx, "sc_ew_left", [4, FEAT])
        ew_parts = sb(ctx, "sc_ew_parts", [4, PARTS, FEAT], BF16)
        ew = sb(ctx, "sc_ew", [ENC, FEAT], BF16)
        onehot = [sb(ctx, f"sc_onehot{r}", [P, 2 * P]) for r in range(DEPTH)]
        enc = [sb(ctx, f"sc_enc{r}", [P, 2, FEAT]) for r in range(2)]
        prod = [sb(ctx, f"sc_prod{r}", [P, 2, FEAT]) for r in range(2)]
        dots = sb(ctx, "sc_dots", [P, LANES * HEADS])
        dsts = sb(ctx, "sc_dsts", [P, LANES, 1 + HEADS])
        score = [sb(ctx, f"sc_score{u}", [P, LANES * HEADS]) for u in range(2)]
        enc_p = [ps(ctx, f"sc_encp{r}", [P, 2, FEAT]) for r in range(2)]
        dst_p = [ps(ctx, f"sc_dstp{r}", [P, 2, 512]) for r in range(2)]
        s_w, s_ones, s_parts, s_parts_out, s_ew = (sem("sc_" + x) for x in ("w", "ones", "parts", "parts_out", "ew"))
        rows_in, rows_out = ([pair(f"sc_{x}{u}_") for u in range(2)] for x in ("rows_in", "rows_out"))
        score_out = pair("sc_score_out")
        dl_in, att_in = pair("sc_dl_in"), pair("sc_att_in")
        idx_ready, onehot_done = sem("sc_idx_ready"), sem("sc_onehot_done")
        enc_done = sem("sc_enc_done")
        relu_done, dst_done = sem("sc_relu_done"), sem("sc_dst_done")
        prod_done, read_done = sem("sc_prod_done"), sem("sc_read_done")
        dots_done, s_part = sem("sc_dots_done"), sem("sc_part")
        added_done = sem("sc_added_done")
        score_done = sem("sc_score_done")
        s_dve = sem("sc_dve")
        half = ITERS // 2
        with nc.Block() as block:
            @block.sync
            def _(sp):
                with nc.allow_non_contiguous_dma(reason="a small matrix"):
                    sp.dma_start(ew_left[0:3, :], A["L0_gnn_edge_W"].rearrange("k f -> f k")).then_inc(s_w, 16)
                sp.dma_start(ew_left[3:4, :], A["L0_gnn_edge_b"].rearrange("(o k) -> o k", o=1)).then_inc(s_w, 16)
                for u in range(2):
                    sp.sem_inc(score_out[u], 16)
                    for k in range(2):
                        sp.sem_inc(rows_out[u][k], 16)

                def load(m, u):
                    sp.dma_start(dl[u][:, :], AP(dloc_rows.tensor, m * (LANES * P), [[0, P], [1, LANES * P]])).then_inc(dl_in[u], 16)
                    n = PARTS * 3
                    for r in range(PARTS):
                        sp.dma_start(att[u][r * n:(r + 1) * n, :].rearrange("n (b l) -> n b l", l=P),
                                     AP(attr_rows.tensor, m * (LANES * AROW), [[P, n], [AROW, LANES], [1, P]])).then_inc(att_in[u], 16)

                def store(m, u, i):
                    for k in range(2):
                        sp.wait_ge(rows_in[u][k], 16 * HALF * (i + 1))
                        take_waits(sp, held)
                        sp.dma_start(gathered[bass.ds(m, 1), :, k * HALF * HROW:(k + 1) * HALF * HROW].rearrange("o p c -> (o p) c"),
                                     G[u][:, k * HALF:(k + 1) * HALF, :].rearrange("p b c -> p (b c)")).then_inc(rows_out[u][k], 16)
                    sp.wait_ge(score_done, m + 1)
                    take_waits(sp, held)
                    sp.dma_start(score_rows[bass.ds(m, 1), :, :].rearrange("o p c -> (o p) c"), score[u][:, :]).then_inc(score_out[u], 16)

                sp.wait_ge(s_ones, 2)
                load(0, 0)
                load(1, 1)
                sp.wait_ge(s_parts, 3 * PARTS - 2)
                sp.dma_start(enc_parts.rearrange("r f k -> f r k"), ew_parts[:, :, :]).then_inc(s_parts_out, 16)
                sp.wait_ge(s_parts_out, 16)
                for r in range(PARTS):
                    for n in range(PARTS):
                        k = (r * PARTS + n) * 3
                        sp.dma_start(ew[k:k + 3, :], enc_parts[r, 0:3, :]).then_inc(s_ew, 16)
                    sp.dma_start(ew[ENC - PARTS + r:ENC - PARTS + r + 1, :], enc_parts[r, 3:4, :]).then_inc(s_ew, 16)
                with sp.Fori(0, half - 1) as i:
                    for u in range(2):
                        m = 2 * i + u
                        store(m, u, i)
                        sp.wait_ge(onehot_done, PAIRS * (m + 1))
                        take_waits(sp, held)
                        sp.wait_ge(dst_done, PAIRS * (m + 1) + DEPTH)
                        take_waits(sp, held)
                        load(m + 2, u)
                for u in range(2):
                    store(ITERS - 2 + u, u, half - 1)
                for u in range(2):
                    for k in range(2):
                        sp.wait_ge(rows_out[u][k], 16 * (half + 1))
                    sp.wait_ge(score_out[u], 16 * (half + 1))

            @block.gpsimd
            def _(pool):
                for u in range(2):
                    nc.gpsimd.memset(att[u][:, :], 1.0).then_inc(s_ones, 1)
                with pool.Fori(0, half // 2) as i:
                    for v in range(4):
                        m, u = 4 * i + v, v % 2
                        pool.wait_ge(idx_ready, m + 1)
                        take_waits(pool, held)
                        pool.wait_ge(added_done, m + 1)
                        take_waits(pool, held)
                        for k in range(2):
                            pool.wait_ge(rows_out[u][k], 16 * (2 * i + v // 2 + 1))
                            take_waits(pool, held)
                            for b in range(k * HALF, (k + 1) * HALF):
                                pool.indirect_dma_start(G[u][:, b, :], None, gat_table,
                                                        bass.IndirectOffsetOnAxis(idx[v][:, b:b + 1], 0)).then_inc(rows_in[u][k], 16)

            @block.scalar
            def _(act):
                act.sem_inc(prod_done, 2)
                act.sem_inc(relu_done, 2)
                def indices(m, v):
                    nc.scalar.copy(idx[v][:, :], src_col[:, bass.ds(m * LANES, LANES)]).then_inc(idx_ready, 1)

                def relus(m):
                    for q in range(PAIRS):
                        n, r = m * PAIRS + q, q % 2
                        act.wait_ge(enc_done, n + 1)
                        act.wait_ge(prod_done, n + 1)
                        nc.scalar.activation(enc[r][:, :, :], enc_p[r][:, :, :], ACT.Relu).then_inc(relu_done, 1)

                def four(i, steps_ahead):
                    for v in range(4):
                        m = 4 * i + v
                        if v < steps_ahead:
                            act.wait_ge(added_done, m + 1)
                            indices(m + 2, (v + 2) % 4)
                        relus(m)

                indices(0, 0)
                indices(1, 1)
                with act.Fori(0, half // 2 - 1) as i:
                    four(i, 4)
                four(half // 2 - 1, 2)

            @block.vector
            def _(dve):
                link = Link(dve, s_dve)
                dve.sem_inc(dst_done, DEPTH)
                dve.sem_inc(read_done, 2)
                dve.sem_inc(added_done, 2)
                dve.wait_ge(s_w, 32)
                for r in range(PARTS):
                    nc.vector.tensor_copy(ew_parts[:, r, :], ew_left[:, :]).then_inc(s_parts, 1)
                    dve.wait_ge(s_parts, 3 * r + 1)
                    if r < PARTS - 1:
                        nc.vector.tensor_tensor(ew_left[:, :], ew_left[:, :], ew_parts[:, r, :], ALU.subtract).then_inc(s_parts, 2)
                        dve.wait_ge(s_parts, 3 * r + 3)

                def onehots(m, u, q, i):
                    if q == 0:
                        dve.wait_ge(dl_in[u], 16 * (i + 1))
                    dve.wait_ge(dst_done, m * PAIRS + q + 1)
                    nc.vector.tensor_scalar(onehot[q % DEPTH][:, :], dl[u][:, 2 * q * P:2 * (q + 1) * P], part_id[:, 0:1], None,
                                            ALU.is_equal).then_inc(onehot_done, 1)

                def iteration(m, u, i, more):
                    def product(q):
                        n, r = m * PAIRS + q, q % 2
                        dve.wait_ge(relu_done, n + 3)
                        dve.wait_ge(dst_done, n + 3 + DEPTH - 2)
                        if q >= 2:
                            dve.wait_ge(dots_done, n - 1)
                        nc.vector.tensor_tensor(prod[r][:, :, :], enc[r][:, :, :], dst_p[r][:, :, 0:FEAT], ALU.mult).then_inc(prod_done, 1)
                        nc.vector.tensor_copy(dsts[:, 2 * q:2 * q + 2, :], dst_p[r][:, :, FEAT:DROW]).then_inc(read_done, 1)
                        dve.wait_ge(prod_done, n + 3)
                        nc.vector.reduce_sum(dots[:, 2 * q * HEADS:2 * (q + 1) * HEADS],
                                             prod[r][:, :, :].rearrange("p s (h d) -> p (s h) d", d=HDIM), AXX).then_inc(dots_done, 1)

                    for q in range(PAIRS):
                        ahead = q + DEPTH - 2
                        if ahead < PAIRS:
                            onehots(m, u, ahead, i)
                        elif more:
                            onehots(m + 1, 1 - u, ahead - PAIRS, i + u)
                        product(q)
                    by_head = dots[:, :].rearrange("p (b h) -> p b h", h=HEADS)
                    dve.wait_ge(read_done, PAIRS * (m + 1) + 2)
                    dve.wait_ge(dots_done, PAIRS * (m + 1))
                    nc.vector.tensor_tensor(by_head, by_head, dsts[:, :, 1:1 + HEADS], ALU.add).then_inc(s_part, 1)
                    nc.vector.tensor_scalar(dsts[:, :, 0], dsts[:, :, 0], BIG, -BIG, ALU.mult, ALU.add).then_inc(s_part, 1)
                    dve.wait_ge(s_part, 2 * m + 2)
                    link(nc.vector.tensor_tensor(by_head, by_head, spread(dsts[:, :, :], [[1 + HEADS, LANES], [0, HEADS]]), ALU.add))
                    for k in range(2):
                        dve.wait_ge(rows_in[u][k], 16 * HALF * (i + 1))
                    link(nc.vector.tensor_tensor(by_head, by_head, G[u][:, :, 0:HEADS], ALU.add))
                    dve.sem_inc(added_done, 1)
                    dve.wait_ge(score_out[u], 16 * (i + 1))
                    link(nc.vector.scalar_tensor_tensor(score[u][:, :], dots[:, :], 0.2, dots[:, :], ALU.mult, ALU.max))
                    dve.sem_inc(score_done, 1)

                for q in range(DEPTH - 2):
                    onehots(0, 0, q, 0)
                with link.loop(half - 1, 2 * 3) as i:
                    for u in range(2):
                        iteration(2 * i + u, u, i, True)
                for u in range(2):
                    iteration(ITERS - 2 + u, u, half - 1, u == 0)

            @block.tensor
            def _(pe):
                pe.wait_ge(s_ew, 16 * (PARTS * PARTS + PARTS))
                flat = h_all[:, :, :].rearrange("p t c -> p (t c)")
                with pe.Fori(0, half) as i:
                    for u in range(2):
                        m = 2 * i + u
                        _, tiles = nc.values_load_multi_w_load_instructions(
                            tiles_row[0:1, bass.ds(m * LANES, LANES)], engines=[mybir.EngineType.PE], min_val=0, max_val=TILES - 1,
                            skip_runtime_bounds_check_because="tile numbers are clamped where they are worked out")
                        pe.wait_ge(att_in[u], 16 * PARTS * (i + 1))
                        for q in range(PAIRS):
                            n, r = m * PAIRS + q, q % 2
                            pe.wait_ge(relu_done, n + 1)
                            for s in range(2):
                                b = 2 * q + s
                                last = nc.tensor.matmul(enc_p[r][:, s, :], att[u][:, b * P:(b + 1) * P], ew[:, :], start=True, stop=True)
                            last.then_inc(enc_done, 1)
                            pe.wait_ge(onehot_done, n + 1)
                            pe.wait_ge(read_done, n + 1)
                            for s in range(2):
                                last = nc.tensor.matmul(dst_p[r][:, s, 0:DROW], onehot[q % DEPTH][:, s * P:(s + 1) * P],
                                                        flat[:, bass.ds(tiles[2 * q + s] * HCOL + HEADS, DROW)], start=True, stop=True)
                            last.then_inc(dst_done, 1)


def softmax_phase(nc, sb, ps, sem, pair, held, const, start_rows, score_rows, weight_rows):
    ident = const[5]
    COLS = ITERS * P
    J = 4
    TURNS = ITERS // J
    PIECE = 1024


    def backwards(t, hi, lo):
        return t[:, hi - 1:lo - 1:-1] if lo else t[:, hi - 1::-1]

    with ExitStack() as ctx:
        alpha = sb(ctx, "alpha", [P, COLS])
        start = sb(ctx, "start", [P, COLS + 1])
        top = sb(ctx, "top", [P, COLS])
        by_edge = top[:, :].rearrange("e (j c) -> e j c", c=P)
        dump = [sb(ctx, f"sm_dump{u}", [P, PIECE]) for u in range(2)]
        weight = [sb(ctx, f"sm_weight{u}", [P, J * P]) for u in range(2)]
        any_start = sb(ctx, "any_start", [P, 2])
        carry = sb(ctx, "carry", [P, 1])
        line = sb(ctx, "line", [1, 3, P])
        turn = [ps(ctx, f"sm_turn{u}", [P, 512]) for u in range(2)]
        small = ps(ctx, "sm_small", [P, 3, P])
        s_flags, s_edge = sem("sm_flags"), sem("sm_edge")
        cuts = [0, 7, 14, 20, TURNS]
        part_in, s_out = [sem(f"sm_part_in{k}") for k in range(4)], sem("sm_out")
        turned, added = sem("sm_turned"), sem("sm_added")
        back, copied = sem("sm_back"), sem("sm_copied")
        s_dve, s_line, s_diff, s_exp = sem("sm_dve"), sem("sm_line"), sem("sm_diff"), sem("sm_exp")
        s_sum, s_pe, s_any = sem("sm_sum"), sem("sm_pe"), sem("sm_any")
        half = TURNS // 2
        with nc.Block() as block:
            @block.sync
            def _(sp):
                def rows(k, t):
                    j = slice(cuts[k] * J, cuts[k + 1] * J)
                    return t[j, :, :].rearrange("j e c -> e j c"), by_edge[:, j, :]

                for k in range(4):
                    dram, here = rows(k, score_rows)
                    sp.dma_start(here, dram).then_inc(part_in[k], 16)
                for k in range(4):
                    sp.wait_ge(copied, cuts[k + 1] + 2)
                    dram, here = rows(k, weight_rows)
                    sp.dma_start(dram, here).then_inc(s_out, 16)
                sp.wait_ge(s_out, 16 * 4)

            @block.scalar
            def _(act):
                act.wait_ge(s_edge, 1)
                act.wait_ge(part_in[3], 16)
                for b in range(LANES):
                    w = COLS + (b < LANES - 1)
                    act.dma_start(start[b * HEADS:(b + 1) * HEADS, 0:w],
                                  AP(start_rows.tensor, b * COLS, [[0, HEADS], [1, w]])).then_inc(s_flags, 16)
                act.wait_ge(s_flags, 16 * LANES)
                for lo in range(2):
                    if lo:
                        act.wait_ge(s_any, lo)
                    nc.scalar.activation(start[:, lo:lo + COLS], start[:, lo:lo + COLS], ACT.Copy, accum_out=any_start[:, lo:lo + 1]).then_inc(s_any, 1)
                act.sem_inc(back, 2)
                act.wait_ge(s_diff, 1)
                with act.Fori(0, half) as i:
                    for u in range(2):
                        g = 2 * i + u
                        act.wait_ge(back, g + 1)
                        nc.scalar.activation(weight[u][:, :], alpha[:, bass.ds(g * (J * P), J * P)], ACT.Exp).then_inc(s_exp, 1)

            @block.gpsimd
            def _(pool):
                nc.gpsimd.memset(start[96:P, COLS:COLS + 1], -BIG).then_inc(s_edge, 1)

            @block.vector
            def _(dve):
                link = Link(dve, s_dve)
                dve.sem_inc(added, 2)
                dve.sem_inc(copied, 2)
                with dve.Fori(0, half) as i:
                    for u in range(2):
                        g = 2 * i + u
                        dve.wait_ge(turned, g + 1)
                        nc.vector.tensor_copy(alpha[:, bass.ds(g * (J * P), J * P)], turn[u][:, :]).then_inc(added, 1)
                dve.wait_ge(added, TURNS + 2)
                dve.wait_ge(s_flags, 16 * LANES)
                dve.wait_ge(s_any, 2)

                def across(first_in, first_out, step, lo):
                    dve.sem_inc(s_sum, 1)
                    k = lo
                    dve.wait_ge(s_pe, 2 * k + 1)
                    link(nc.vector.tensor_copy(line[0:1, 0:2, :], small[0:1, 0:2, :]))
                    link(nc.vector.memset(line[0:1, 2, :], -BIG))
                    def at(row, first, h):
                        one = line[0:1, row, first + h:first + h + 1]
                        return AP(one.tensor, one.offset, [list(one.ap[0]), [step, LANES - 1]])

                    for h in range(HEADS):
                        last = nc.vector.tensor_tensor_scan(out=at(2, first_out, h), data0=at(1, first_in, h), data1=at(0, first_in, h),
                                                            initial=-BIG, op0=ALU.add, op1=ALU.max)
                    link(last)
                    dve.sem_inc(s_line, 1)
                    dve.wait_ge(s_pe, 2 * k + 2)
                    link(nc.vector.tensor_copy(carry[:, :], small[:, 2, 0:1]))

                link(nc.vector.tensor_tensor_scan(out=top[:, :], data0=start[:, 0:COLS], data1=alpha[:, :], initial=-BIG, op0=ALU.add, op1=ALU.max))
                link(nc.vector.tensor_copy(dump[0][:, 0:1], top[:, COLS - 1:COLS]))
                across(0, HEADS, HEADS, 0)
                link(nc.vector.tensor_tensor_scan(out=top[:, :], data0=start[:, 0:COLS], data1=alpha[:, :], initial=carry[:, 0:1], op0=ALU.add, op1=ALU.max))
                prev = -BIG
                for k in range(COLS // PIECE):
                    hi = COLS - k * PIECE
                    lo = hi - PIECE
                    link(nc.vector.tensor_tensor_scan(out=dump[k % 2][:, :], data0=start[:, hi:lo:-1], data1=backwards(top, hi, lo),
                                                      initial=prev, op0=ALU.add, op1=ALU.max))
                    prev = dump[k % 2][:, PIECE - 1:PIECE]
                link(nc.vector.tensor_copy(dump[1][:, 0:1], prev))
                across(HEADS * (LANES - 1), HEADS * (LANES - 2), -HEADS, 1)
                link(nc.vector.tensor_tensor_scan(out=backwards(top, COLS, 0), data0=start[:, COLS:0:-1], data1=backwards(top, COLS, 0),
                                                  initial=carry[:, 0:1], op0=ALU.add, op1=ALU.max))
                nc.vector.tensor_tensor(alpha[:, :], alpha[:, :], top[:, :], ALU.subtract).then_inc(s_diff, 1)
                with dve.Fori(0, half) as i:
                    for u in range(2):
                        g = 2 * i + u
                        dve.wait_ge(back, g + 3)
                        nc.vector.tensor_copy(top[:, bass.ds(g * (J * P), J * P)], turn[u][:, :]).then_inc(copied, 1)

            @block.tensor
            def _(pe):
                for g in range(TURNS):
                    if g in cuts:
                        pe.wait_ge(part_in[cuts.index(g)], 16)
                    pe.wait_ge(added, g + 1)
                    for j in range(J):
                        last = nc.tensor.transpose(turn[g % 2][:, j * P:(j + 1) * P], by_edge[:, g * J + j, :], ident[:, :])
                    last.then_inc(turned, 1)
                for k in range(2):
                    pe.wait_ge(s_sum, k + 1)
                    nc.tensor.transpose(small[0:1, 0, :], dump[k][:, 0:1], ident[:, :])
                    pe.wait_ge(s_any, k + 1)
                    nc.tensor.transpose(small[0:1, 1, :], any_start[:, k:k + 1], ident[:, :]).then_inc(s_pe, 1)
                    pe.wait_ge(s_line, k + 1)
                    nc.tensor.transpose(small[:, 2, 0:1], line[0:1, 2, :], ident[0:1, 0:1]).then_inc(s_pe, 1)
                with pe.Fori(0, half) as i:
                    for u in range(2):
                        g = 2 * i + u
                        pe.wait_ge(s_exp, g + 1)
                        pe.wait_ge(copied, g + 1)
                        for j in range(J):
                            last = nc.tensor.transpose(turn[u][:, j * P:(j + 1) * P], weight[u][:, j * P:(j + 1) * P], ident[:, :])
                        last.then_inc(back, 1)


def gat_sum_phase(nc, sb, ps, sem, pair, held, const, acc, S, gathered, weight_rows):
    src_col, dloc_col, tiles_row, iota_row, part_id, ident = const
    HALF, QUART = LANES // 2, LANES // 4
    R = 8
    MID = HROW // 2
    with ExitStack() as ctx:
        G = [sb(ctx, f"gs_g{u}", [P, LANES, HROW]) for u in range(2)]
        wt = [sb(ctx, f"gs_wt{u}", [P, LANES * HEADS]) for u in range(2)]
        dcol = [sb(ctx, f"gs_dcol{u}", [P, LANES]) for u in range(2)]
        sums = ps(ctx, "gs_sums", [P, R, 512])
        rows_in = [pair(f"gs_rows_in{u}_") for u in range(2)]
        wcopy_done, s_far = sem("gs_wcopy_done"), sem("gs_far")
        zeroed, dcol_ready = sem("gs_zeroed"), sem("gs_dcol_ready")
        onehot_done, sum_done = sem("gs_onehot_done"), sem("gs_sum_done")
        mul_done, add_done = sem("gs_mul_done"), sem("gs_add_done")
        half = ITERS // 2
        with nc.Block() as block:
            @block.sync
            def _(sp):
                with sp.Fori(0, half) as i:
                    for u in range(2):
                        m = 2 * i + u
                        for k in range(2):
                            sp.wait_ge(sum_done, LANES * m + HALF * (k + 1))
                            take_waits(sp, held)
                            b = slice(k * HALF, (k + 1) * HALF)
                            sp.dma_start(G[u][:, b, :].rearrange("p b c -> p (b c)"),
                                         gathered[bass.ds(m, 1), :, k * HALF * HROW:(k + 1) * HALF * HROW].rearrange("o p c -> (o p) c")).then_inc(rows_in[u][k], 16)
                            w = slice(k * HALF * HEADS, (k + 1) * HALF * HEADS)
                            sp.dma_start(wt[u][:, w], weight_rows[bass.ds(m, 1), :, w].rearrange("o p c -> (o p) c")).then_inc(rows_in[u][k], 16)

            @block.scalar
            def _(act):
                act.sem_inc(s_far, 1)
                one = iota_row[:, 1:2]

                def places(m, u):
                    act.wait_ge(onehot_done, LANES * (m + 1))
                    nc.scalar.copy(dcol[u][:, :], dloc_col[:, bass.ds(m * LANES, LANES)]).then_inc(dcol_ready, 1)
                    act.wait_ge(dcol_ready, m + 1)

                def distances(m, u, b):
                    act.wait_ge(sum_done, m * LANES + b + QUART)
                    for c in range(b, b + QUART):
                        last = nc.scalar.activation(S[:, u * LANES + c, :], iota_row[:, :], ACT.Abs, scale=-1.0, bias=dcol[u][:, c:c + 1])
                    last.then_inc(s_far, 1)

                def onehots(m, u, b):
                    act.wait_ge(s_far, 4 * m + b // QUART + 2)
                    four = S[:, u * LANES + b:u * LANES + b + QUART, :]
                    nc.scalar.activation(four, four, ACT.Relu, scale=-1.0, bias=one).then_inc(onehot_done, QUART)

                def weights(m, u, i, k):
                    act.wait_ge(rows_in[u][k], 32 * (i + 1))
                    w = wt[u][:, k * HALF * HEADS:(k + 1) * HALF * HEADS]
                    nc.scalar.copy(G[u][:, k * HALF:(k + 1) * HALF, 0:HEADS], w.rearrange("p (b h) -> p b h", h=HEADS)).then_inc(wcopy_done, 1)

                def iteration(m, u, i, more):
                    if more:
                        places(m + 1, 1 - u)
                    for b in range(0, LANES, QUART):
                        if more:
                            distances(m + 1, 1 - u, b)
                            if b:
                                onehots(m + 1, 1 - u, b - QUART)
                        if b % HALF == 0:
                            weights(m, u, i, b // HALF)
                    if more:
                        onehots(m + 1, 1 - u, LANES - QUART)

                act.sem_inc(onehot_done, 2 * LANES)
                places(0, 0)
                for b in range(0, LANES, QUART):
                    distances(0, 0, b)
                    onehots(0, 0, b)
                with act.Fori(0, half - 1) as i:
                    for u in range(2):
                        iteration(2 * i + u, u, i, True)
                for u in range(2):
                    iteration(ITERS - 2 + u, u, half - 1, u == 0)

            @block.gpsimd
            def _(pool):
                nc.gpsimd.memset(acc[:, 0:TILES // 2, :], 0.0).then_inc(zeroed, 1)
                with pool.Fori(0, half) as i:
                    for u in range(2):
                        for q in range(4):
                            if q % 2 == 0:
                                pool.wait_ge(rows_in[u][q // 2], 32 * (i + 1))
                                take_waits(pool, held)
                            w = wt[u][:, q * QUART * HEADS:(q + 1) * QUART * HEADS]
                            h = G[u][:, q * QUART:(q + 1) * QUART, H0:H1].rearrange("p b (h d) -> p b h d", d=HDIM)
                            nc.gpsimd.tensor_tensor(h, h, spread(w, [[HEADS, QUART], [1, HEADS], [0, HDIM]]), ALU.mult).then_inc(mul_done, 1)

            @block.vector
            def _(dve):
                dve.sem_inc(add_done, 2 * R)
                nc.vector.memset(acc[:, TILES // 2:TILES, :], 0.0).then_inc(zeroed, 1)
                dve.wait_ge(zeroed, 2)
                flat = acc[:, :, :].rearrange("p t c -> p (t c)")

                def iteration(m):
                    _, tiles = nc.values_load_multi_w_load_instructions(
                        tiles_row[0:1, bass.ds(m * LANES, LANES)], engines=[mybir.EngineType.DVE], min_val=0, max_val=TILES - 1,
                        skip_runtime_bounds_check_because="tile numbers are clamped where they are worked out")
                    for b in range(LANES):
                        n = m * LANES + b
                        if b % QUART == 0:
                            dve.wait_ge(sum_done, n + QUART + 2 * LANES)
                        for k, c in enumerate((slice(0, MID), slice(MID, HROW))):
                            dve.wait_ge(add_done, 2 * n + k + 2 * R - 1)
                            t = flat[:, bass.ds(tiles[b] * HROW + c.start, c.stop - c.start)]
                            nc.vector.tensor_tensor(t, t, sums[:, b % R, c], ALU.add).then_inc(add_done, 1)

                with dve.Fori(0, half) as i:
                    for u in range(2):
                        iteration(2 * i + u)

            @block.tensor
            def _(pe):
                pe.sem_inc(sum_done, 2 * LANES)
                with pe.Fori(0, half) as i:
                    for u in range(2):
                        m = 2 * i + u
                        for b in range(LANES):
                            n = m * LANES + b
                            if b % QUART == 0:
                                pe.wait_ge(onehot_done, n + QUART + 2 * LANES)
                                pe.wait_ge(mul_done, 4 * m + b // QUART + 1)
                            if b % HALF == 0:
                                pe.wait_ge(wcopy_done, 2 * m + b // HALF + 1)
                            if b % 2 == 0:
                                pe.wait_ge(add_done, 2 * n + 4)
                            nc.tensor.matmul(sums[:, b % R, 0:HROW], S[:, u * LANES + b, :], G[u][:, b, :], start=True, stop=True).then_inc(sum_done, 1)


def mid_phase(nc, sb, ps, sem, pair, held, A, const, acc, acc1, dinv, x1_norm, x1_rows, conv1_table):
    with ExitStack() as ctx:
        w1 = sb(ctx, "w1", [P, 2, F1])
        bias = sb(ctx, "gat_bias", [P, FEAT])
        s_w, deg_ready, root_ready = sem("md_w"), sem("md_deg_ready"), sem("md_root_ready")
        den_ready, attended = sem("md_den_ready"), sem("md_attended")
        scaled = sem("md_scaled")
        x1_out = pair("md_x1_out")

        def sync_before(sp):
            sp.dma_start(w1[:, :, :], A["L1_gnn_W1"].rearrange("(c p) k -> p c k", p=P)).then_inc(s_w, 16)
            sp.dma_start(bias[:, :], A["L0_gnn_bias"].partition_broadcast(P)).then_inc(s_w, 16)

        def dve_before(dve, link):
            nc.vector.tensor_scalar(dinv[:, :], acc[:, :, H1], 1.0, None, ALU.add).then_inc(deg_ready, 1)
            link(nc.vector.tensor_scalar(acc[:, :, 0:HEADS], acc[:, :, 0:HEADS], 1e-10, None, ALU.max))
            nc.vector.reciprocal(acc[:, :, 0:HEADS], acc[:, :, 0:HEADS]).then_inc(den_ready, 1)
            dve.wait_ge(root_ready, 1)
            link(nc.vector.reciprocal(dinv[:, :], dinv[:, :]))

        def act_before(act):
            act.wait_ge(deg_ready, 1)
            nc.scalar.activation(dinv[:, :], dinv[:, :], ACT.Sqrt).then_inc(root_ready, 1)

        def attend(pool):
            pool.wait_ge(s_w, 32)
            pool.wait_ge(den_ready, 1)
            with pool.Fori(0, GROUPS) as g:
                h = acc[:, bass.ds(g * GT, GT), H0:H1]
                heads = h.rearrange("p t (h d) -> p t h d", d=HDIM)
                den = acc[:, bass.ds(g * GT, GT), 0:HEADS]
                nc.gpsimd.tensor_tensor(heads, heads, spread(den, [[HROW, GT], [1, HEADS], [0, HDIM]]), ALU.mult).then_inc(scaled, 1)
                pool.wait_ge(scaled, g + 1)
                take_waits(pool, held)
                nc.gpsimd.tensor_tensor(h, h, spread(bias[:, :], [[0, GT], [1, FEAT]]), ALU.add).then_inc(attended, 1)

        def pre(dve, link, g, u, xg):
            dve.wait_ge(attended, g + 1)
            link(nc.vector.tensor_tensor(xg[u][:, :, :], xg[u][:, :, :], acc[:, bass.ds(g * GT, GT), H0:H1], ALU.add))

        def hold(sp, g, u, i, xg, finish_done, stored):
            sp.dma_start(x1_rows[bass.ds(g * (GT * P), GT * P), :].rearrange("(a p) c -> p a c", p=P), xg[u][:, :, :]).then_inc(x1_out[u], 16)
            sp.wait_ge(x1_out[u], 16 * (i + 1))
            take_waits(sp, held)

        def finish_act(act, g, u, a, op, done):
            nc.scalar.activation(acc1[:, bass.ds(g * GT + a, 1), :].rearrange("p o c -> p (o c)"), op[:, 0:F1], ACT.Copy, scale=dinv[:, bass.ds(g * GT + a, 1)]).then_inc(done, 1)

        def act_store(act, g, u, stored):
            act.dma_start(conv1_table[bass.ds(g * (GT * P), GT * P), :].rearrange("(a p) c -> p a c", p=P),
                          acc1[:, bass.ds(g * GT, GT), :]).then_inc(stored[u], 16)

        dense_phase(nc, sb, ps, sem, pair, held, const, "md", ctx, A["x"], NODES, [w1[:, 0, :], w1[:, 1, :]], F1,
                    lambda pe: pe.wait_ge(s_w, 32), pre=pre, pre_links=1, keep=x1_norm, finish_act=finish_act, act_store=act_store,
                    hold=hold, act_before=act_before, sync_before=sync_before, dve_before=dve_before, pool=attend)


class FirstColumns:

    def __init__(self, nc, sb, ps, sem, pair, held, A, const, ctx, acc1, x1_norm, x1_rows, z_rows):
        self.nc, self.A, self.held, self.ident, self.norm = nc, A, held, const[5], x1_norm
        self.x1_rows, self.z_rows, self.y1 = x1_rows, z_rows, acc1[:, :, :].rearrange("p t c -> p (t c)")
        self.w = sb(ctx, "fc_w", [P, 3, FEAT])
        self.bias = sb(ctx, "fc_bias", [P, FEAT])
        self.x1 = [sb(ctx, f"fc_x1{r}", [P, FEAT]) for r in range(2)]
        self.rows = [sb(ctx, f"fc_rows{r}", [P, 3 * P]) for r in range(2)]
        self.turned = [sb(ctx, f"fc_turned{r}", [P, 3, P]) for r in range(2)]
        self.z = [sb(ctx, f"fc_z{r}", [P, FEAT]) for r in range(2)]
        self.tp = [ps(ctx, f"fc_tp{r}", [P, 4, P]) for r in range(2)]
        self.op = [ps(ctx, f"fc_op{r}", [P, 512]) for r in range(2)]
        self.s_w, self.x1_in, self.z_out = sem("fc_w_in"), pair("fc_x1_in"), pair("fc_z_out")
        self.relu_done, self.turn_done, self.copy_done = (sem("fc_" + n) for n in ("relu_done", "turn_done", "copy_done"))
        self.product_done, self.z_done = sem("fc_product_done"), sem("fc_z_done")

    def start(self, sp):
        for s in (self.relu_done, self.turn_done, self.copy_done, self.product_done):
            sp.sem_inc(s, 2)
        for r in range(2):
            sp.sem_inc(self.z_out[r], 16)
        sp.dma_start(self.w[:, :, :], self.A["L1_gnn_Wfc"][0:3 * P, :].rearrange("(c p) k -> p c k", p=P)).then_inc(self.s_w, 16)
        sp.dma_start(self.bias[:, :], self.A["L1_gnn_bfc"].partition_broadcast(P)).then_inc(self.s_w, 16)
        self.load(sp, 0, 0)

    def load(self, sp, t, r):
        sp.wait_ge(self.relu_done, t + 1)
        take_waits(sp, self.held)
        sp.dma_start(self.x1[r][:, :], self.x1_rows[bass.ds(t * P, P), :]).then_inc(self.x1_in[r], 16)

    def store(self, sp, t, r):
        sp.wait_ge(self.z_done, t + 1)
        take_waits(sp, self.held)
        sp.dma_start(self.z_rows[bass.ds(t * P, P), :], self.z[r][:, :]).then_inc(self.z_out[r], 16)

    def stored(self, sp):
        for r in range(2):
            sp.wait_ge(self.z_out[r], 16 * (TILES // 2 + 1))

    def relus(self, act, t, r, i):
        act.wait_ge(self.x1_in[r], 16 * (i + 1))
        act.wait_ge(self.turn_done, t + 1)
        self.nc.scalar.activation(self.rows[r][:, 0:FEAT], self.x1[r][:, :], ACT.Relu, scale=self.norm[0][:, bass.ds(t, 1)],
                                  bias=self.norm[1][:, bass.ds(t, 1)])
        self.nc.scalar.activation(self.rows[r][:, FEAT:3 * P], self.y1[:, bass.ds(t * F1, F1)], ACT.Relu).then_inc(self.relu_done, 1)

    def turn(self, pe, t, r):
        pe.wait_ge(self.relu_done, t + 3)
        pe.wait_ge(self.copy_done, t + 1)
        for c in range(3):
            last = self.nc.tensor.transpose(self.tp[r][:, c, :], self.rows[r][:, c * P:(c + 1) * P], self.ident[:, :])
        last.then_inc(self.turn_done, 1)

    def copy(self, dve, t, r):
        dve.wait_ge(self.turn_done, t + 3)
        dve.wait_ge(self.product_done, t + 1)
        self.nc.vector.tensor_copy(self.turned[r][:, :, :], self.tp[r][:, 0:3, :]).then_inc(self.copy_done, 1)

    def product(self, pe, t, r):
        pe.wait_ge(self.copy_done, t + 3)
        for c in range(3):
            last = self.nc.tensor.matmul(self.op[r][:, 0:FEAT], self.turned[r][:, c, :], self.w[:, c, :], start=c == 0, stop=c == 2)
        last.then_inc(self.product_done, 1)

    def finish(self, dve, t, r, i):
        dve.wait_ge(self.product_done, t + 3)
        dve.wait_ge(self.z_out[r], 16 * (i + 1))
        self.nc.vector.tensor_tensor(self.z[r][:, :], self.op[r][:, 0:FEAT], self.bias[:, :], ALU.add).then_inc(self.z_done, 1)


def conv_phase(nc, sb, ps, sem, pair, held, const, name, width, acc, table, fc=None):
    src_col, dloc_col, tiles_row, iota_row, part_id, ident = const
    R = 4
    QUART = LANES // 4
    with ExitStack() as ctx:
        idx = [sb(ctx, f"{name}_idx{u}", [P, LANES], I32) for u in range(2)]
        dcol = [sb(ctx, f"{name}_dcol{u}", [P, LANES]) for u in range(2)]
        G = [sb(ctx, f"{name}_g{u}", [P, LANES, width]) for u in range(2)]
        S = sb(ctx, f"{name}_S", [P, 2 * LANES, P])
        sums = ps(ctx, f"{name}_sums", [P, R, 512])
        idx_ready, dcol_ready, rows_in = sem(f"{name}_idx_ready"), sem(f"{name}_dcol_ready"), pair(f"{name}_rows_in")
        onehot_done = sem(f"{name}_onehot_done")
        sum_done, add_done = sem(f"{name}_sum_done"), sem(f"{name}_add_done")
        half = ITERS // 2

        def loop(eng, body):
            many = TILES // 2 if fc else half
            with eng.Fori(0, many) as i:
                for u in range(2):
                    body(2 * i + u, u, i, fc)
            for i in range(many, half):
                for u in range(2):
                    body(2 * i + u, u, i, None)

        with nc.Block() as block:
            if fc:
                @block.sync
                def _(sp):
                    fc.start(sp)
                    with sp.Fori(0, TILES // 2 - 1) as i:
                        for u in range(2):
                            fc.load(sp, 2 * i + u + 1, 1 - u)
                            fc.store(sp, 2 * i + u, u)
                    fc.load(sp, TILES - 1, 1)
                    for u in range(2):
                        fc.store(sp, TILES - 2 + u, u)
                    fc.stored(sp)

            @block.scalar
            def _(act):
                def iteration(m, u, i, fc):
                    act.wait_ge(sum_done, LANES * (m + 1))
                    nc.scalar.copy(idx[u][:, :], src_col[:, bass.ds(m * LANES, LANES)]).then_inc(idx_ready, 1)
                    act.wait_ge(onehot_done, LANES * (m + 1))
                    nc.scalar.copy(dcol[u][:, :], dloc_col[:, bass.ds(m * LANES, LANES)]).then_inc(dcol_ready, 1)
                    if fc:
                        fc.relus(act, m, u, i)

                act.sem_inc(onehot_done, 2 * LANES)
                loop(act, iteration)

            @block.gpsimd
            def _(pool):
                with pool.Fori(0, half) as i:
                    for u in range(2):
                        pool.wait_ge(idx_ready, 2 * i + u + 1)
                        take_waits(pool, held)
                        for b in range(LANES):
                            pool.indirect_dma_start(G[u][:, b, :], None, table,
                                                    bass.IndirectOffsetOnAxis(idx[u][:, b:b + 1], 0)).then_inc(rows_in[u], 16)

            @block.vector
            def _(dve):
                flat = acc[:, :, :].rearrange("p t c -> p (t c)")

                def iteration(m, u, i, fc):
                    _, tiles = nc.values_load_multi_w_load_instructions(
                        tiles_row[0:1, bass.ds(m * LANES, LANES)], engines=[mybir.EngineType.DVE], min_val=0, max_val=TILES - 1,
                        skip_runtime_bounds_check_because="tile numbers are clamped where they are worked out")
                    dve.wait_ge(dcol_ready, m + 1)
                    for b in range(0, LANES, QUART):
                        dve.wait_ge(sum_done, m * LANES + b + QUART)
                        nc.vector.tensor_tensor(S[:, u * LANES + b:u * LANES + b + QUART, :], spread(iota_row[:, :], [[0, QUART], [1, P]]),
                                                spread(dcol[u][:, b:b + QUART], [[1, QUART], [0, P]]), ALU.is_equal).then_inc(onehot_done, QUART)
                    if fc:
                        fc.copy(dve, m, u)
                    for b in range(LANES):
                        n = m * LANES + b
                        dve.wait_ge(sum_done, n + 1 + 2 * LANES)
                        dve.wait_ge(add_done, n + R)
                        t = flat[:, bass.ds(tiles[b] * width, width)]
                        nc.vector.tensor_tensor(t, t, sums[:, b % R, 0:width], ALU.add).then_inc(add_done, 1)
                    if fc:
                        fc.finish(dve, m, u, i)

                dve.sem_inc(add_done, R)
                if fc:
                    dve.wait_ge(fc.s_w, 32)
                loop(dve, iteration)

            @block.tensor
            def _(pe):
                def iteration(m, u, i, fc):
                    if fc:
                        fc.turn(pe, m, u)
                    pe.wait_ge(rows_in[u], 16 * LANES * (i + 1))
                    for b in range(LANES):
                        n = m * LANES + b
                        pe.wait_ge(onehot_done, n + 1 + 2 * LANES)
                        pe.wait_ge(add_done, n + 1)
                        nc.tensor.matmul(sums[:, b % R, 0:width], S[:, u * LANES + b, :], G[u][:, b, :], start=True, stop=True).then_inc(sum_done, 1)
                    if fc:
                        fc.product(pe, m, u)

                pe.sem_inc(sum_done, 2 * LANES)
                if fc:
                    pe.wait_ge(fc.s_w, 32)
                loop(pe, iteration)


def norm_phase(nc, sb, ps, sem, A, const, name, width, acc, dinv, bias, gamma, beta):
    with ExitStack() as ctx:
        square = sb(ctx, f"{name}_square", [P, TILES, width])
        rows = sb(ctx, f"{name}_rows", [P, 3, width])
        ones = sb(ctx, f"{name}_ones", [P, 2, P])
        part_ok = sb(ctx, f"{name}_part_ok", [P, 1])
        mean = sb(ctx, f"{name}_mean", [P, width])
        var = sb(ctx, f"{name}_var", [P, width])
        root = sb(ctx, f"{name}_root", [P, width])
        total = [ps(ctx, f"{name}_total{k}", [P, 512]) for k in range(2)]
        s_rows, s_ones, s_dve = sem(f"{name}_rows_in"), sem(f"{name}_ones_ready"), sem(f"{name}_dve")
        s_vals, s_total, s_var, s_root, s_dev = (sem(f"{name}_{x}") for x in ("vals", "totals", "var_ready", "root_ready", "dev"))
        s_square, s_scale = sem(f"{name}_square"), sem(f"{name}_scale")
        PIECE = 16
        PIECES = -(-TILES // PIECE)
        pieces = [slice(n * PIECE, min((n + 1) * PIECE, TILES)) for n in range(PIECES)]
        SHARE = TILES * 2 // 3
        per = 512 // width
        whole = (TILES - 1) // per
        flat = acc[:, :, :].rearrange("p t c -> p (t c)")
        with nc.Block() as block:
            @block.sync
            def _(sp):
                for n, a in enumerate((bias, gamma, beta)):
                    sp.dma_start(rows[:, n, :], a.partition_broadcast(P)).then_inc(s_rows, 16)

            @block.vector
            def _(dve):
                link = Link(dve, s_dve)
                part_id = const[4]
                link(nc.vector.tensor_scalar(part_ok[:, :], part_id[:, :], float(LAST), None, ALU.is_lt))
                nc.vector.memset(ones[:, 0, :], 1.0)
                nc.vector.tensor_copy(ones[:, 1, :], spread(part_ok[:, :], [[0, P]])).then_inc(s_ones, 1)
                dve.wait_ge(s_rows, 48)

                def each(row, tiles=TILES):
                    return spread(row, [[0, tiles], [1, width]])

                for t in range(TILES):
                    i = nc.vector.scalar_tensor_tensor(acc[:, t, :], acc[:, t, :], dinv[:, t:t + 1], rows[:, 0, :], ALU.mult, ALU.add)
                    if t % PIECE == PIECE - 1 or t == TILES - 1:
                        i.then_inc(s_vals, 1)
                dve.wait_ge(s_vals, PIECES)
                dve.wait_ge(s_total, 1)
                link(nc.vector.reduce_sum(mean[:, :], total[0][:, :].rearrange("p (a c) -> p c a", c=width), AXX))
                link(nc.vector.tensor_scalar(mean[:, :], mean[:, :], 1.0 / NODES, None, ALU.mult))
                for piece in pieces:
                    a = acc[:, piece, :]
                    nc.vector.tensor_tensor(a, a, each(mean[:, :], piece.stop - piece.start), ALU.subtract).then_inc(s_dev, 1)
                dve.wait_ge(s_total, 2)
                link(nc.vector.reduce_sum(var[:, :], total[1][:, :].rearrange("p (a c) -> p c a", c=width), AXX))
                nc.vector.tensor_scalar(var[:, :], var[:, :], 1.0 / NODES, EPS, ALU.mult, ALU.add).then_inc(s_var, 1)
                dve.wait_ge(s_root, 1)
                link(nc.vector.reciprocal(root[:, :], root[:, :]))
                link(nc.vector.tensor_tensor(root[:, :], root[:, :], rows[:, 1, :], ALU.mult))
                dve.sem_inc(s_scale, 1)
                a = acc[:, 0:SHARE, :]
                link(nc.vector.tensor_tensor(a, a, each(root[:, :], SHARE), ALU.mult))
                link(nc.vector.tensor_tensor(a, a, each(rows[:, 2, :], SHARE), ALU.add))

            @block.gpsimd
            def _(pool):
                pool.wait_ge(s_scale, 1)
                pool.wait_ge(s_rows, 48)
                a = acc[:, SHARE:TILES, :]
                nc.gpsimd.tensor_tensor(a, a, spread(root[:, :], [[0, TILES - SHARE], [1, width]]), ALU.mult).then_inc(s_scale, 1)
                pool.wait_ge(s_scale, 2)
                nc.gpsimd.tensor_tensor(a, a, spread(rows[:, 2, :], [[0, TILES - SHARE], [1, width]]), ALU.add)

            @block.scalar
            def _(act):
                for n, piece in enumerate(pieces):
                    act.wait_ge(s_dev, n + 1)
                    nc.scalar.activation(square[:, piece, :], acc[:, piece, :], ACT.Square).then_inc(s_square, 1)
                act.wait_ge(s_var, 1)
                nc.scalar.activation(root[:, :], var[:, :], ACT.Sqrt).then_inc(s_root, 1)

            @block.tensor
            def _(pe):
                pe.wait_ge(s_ones, 1)
                for k, (src, ready) in enumerate(((flat, s_vals), (square[:, :, :].rearrange("p t c -> p (t c)"), s_square))):
                    for n in range(whole):
                        if n % (PIECE // per) == 0:
                            pe.wait_ge(ready, n // (PIECE // per) + 1)
                        nc.tensor.matmul(total[k][:, :], ones[:, 0, :], src[:, n * 512:(n + 1) * 512], start=n == 0, stop=False)
                    pe.wait_ge(ready, PIECES)
                    for t in range(whole * per, TILES):
                        last = nc.tensor.matmul(total[k][:, 0:width], ones[:, int(t == TILES - 1), :], src[:, t * width:(t + 1) * width],
                                                start=False, stop=t == TILES - 1)
                    last.then_inc(s_total, 1)


def project_phase(nc, sb, ps, sem, held, A, const, acc1, acc2, dinv, conv2_table):
    ident = const[5]
    FIRST = 4
    with ExitStack() as ctx:
        w2 = sb(ctx, "w2", [P, F2])
        y = [sb(ctx, f"pj_y{r}", [P, GT, F1]) for r in range(2)]
        yT = [sb(ctx, f"pj_yT{r}", [P, GT, P]) for r in range(2)]
        tp = [ps(ctx, f"pj_tp{r}", [P, 2, FIRST, P]) for r in range(2)]
        op = [ps(ctx, f"pj_op{r}", [P, 512]) for r in range(2)]
        s_w, s_out = sem("pj_w"), sem("pj_out")
        relu_done, turn_done, copy_done = sem("pj_relu_done"), sem("pj_turn_done"), sem("pj_copy_done")
        product_done, finish_done = sem("pj_product_done"), sem("pj_finish_done")
        with nc.Block() as block:
            @block.sync
            def _(sp):
                sp.dma_start(w2[:, :], A["L1_gnn_W2"]).then_inc(s_w, 16)
                with sp.Fori(0, GROUPS) as g:
                    sp.wait_ge(finish_done, g + 3)
                    take_waits(sp, held)
                    sp.dma_start(conv2_table[bass.ds(g * (GT * P), GT * P), :].rearrange("(t p) c -> p t c", p=P),
                                 acc2[:, bass.ds(g * GT, GT), :]).then_inc(s_out, 16)
                sp.wait_ge(s_out, 16 * GROUPS)

            @block.scalar
            def _(act):
                for s in (turn_done, copy_done, product_done, finish_done):
                    act.sem_inc(s, 2)
                flat = acc1[:, :, :].rearrange("p t c -> p (t c)")
                with act.Fori(0, GROUPS // 2) as i:
                    for r in range(2):
                        g = 2 * i + r
                        act.wait_ge(turn_done, g + 1)
                        nc.scalar.activation(y[r][:, :, :].rearrange("p t c -> p (t c)"), flat[:, bass.ds(g * (GT * F1), GT * F1)],
                                             ACT.Relu).then_inc(relu_done, 1)

            @block.vector
            def _(dve):
                flat = acc2[:, :, :].rearrange("p t c -> p (t c)")

                def copy(g, r):
                    dve.wait_ge(turn_done, g + 3)
                    dve.wait_ge(product_done, g + 1)
                    nc.vector.tensor_copy(yT[r][:, 0:FIRST, :], tp[r][:, 0, :, :])
                    nc.vector.tensor_copy(yT[r][:, FIRST:GT, :], tp[r][:, 1, 0:GT - FIRST, :]).then_inc(copy_done, 1)

                def finish(g, r):
                    dve.wait_ge(product_done, g + 3)
                    nc.vector.tensor_tensor(flat[:, bass.ds(g * (GT * F2), GT * F2)].rearrange("p (t c) -> p t c", c=F2),
                                            op[r][:, 0:GT * F2].rearrange("p (t c) -> p t c", c=F2),
                                            spread(dinv[:, bass.ds(g * GT, GT)], [[1, GT], [0, F2]]), ALU.mult).then_inc(finish_done, 1)

                copy(0, 0)
                with dve.Fori(0, GROUPS // 2 - 1) as i:
                    for r in range(2):
                        copy(2 * i + r + 1, 1 - r)
                        finish(2 * i + r, r)
                copy(GROUPS - 1, 1)
                finish(GROUPS - 2, 0)
                finish(GROUPS - 1, 1)

            @block.tensor
            def _(pe):
                def turn(g, r):
                    pe.wait_ge(relu_done, g + 1)
                    pe.wait_ge(copy_done, g + 1)
                    for a in range(GT):
                        last = nc.tensor.transpose(tp[r][:, a // FIRST, a % FIRST, :], y[r][:, a, :], ident[:, :])
                    last.then_inc(turn_done, 1)

                def product(g, r):
                    pe.wait_ge(copy_done, g + 3)
                    pe.wait_ge(finish_done, g + 1)
                    for a in range(GT):
                        last = nc.tensor.matmul(op[r][:, a * F2:(a + 1) * F2], yT[r][:, a, :], w2[:, :], start=True, stop=True)
                    last.then_inc(product_done, 1)

                pe.wait_ge(s_w, 16)
                turn(0, 0)
                with pe.Fori(0, GROUPS // 2 - 1) as i:
                    for r in range(2):
                        turn(2 * i + r + 1, 1 - r)
                        product(2 * i + r, r)
                turn(GROUPS - 1, 1)
                product(GROUPS - 2, 0)
                product(GROUPS - 1, 1)


def final_phase(nc, sb, ps, sem, pair, held, A, const, acc2, x1_rows, z_rows, out):
    ident = const[5]
    PAIR = -(-GT // 2)
    FIRST = 4
    with ExitStack() as ctx:
        w = sb(ctx, "fn_w", [F2, FEAT])
        x1 = [sb(ctx, f"fn_x1{u}", [P, GT, FEAT]) for u in range(2)]
        z = [sb(ctx, f"fn_z{u}", [P, GT, FEAT]) for u in range(2)]
        res = [sb(ctx, f"fn_res{u}", [P, GT, FEAT]) for u in range(2)]
        y = [sb(ctx, f"fn_y{u}", [P, GT, F2]) for u in range(2)]
        yT = [sb(ctx, f"fn_yT{u}", [F2, GT, P]) for u in range(2)]
        tp = ps(ctx, "fn_tp", [F2, 2, FIRST, P])
        op = ps(ctx, "fn_op", [P, PAIR, 512])
        s_w, rows_in, res_out = sem("fn_w_in"), pair("fn_rows_in"), pair("fn_res_out")
        relu_done, turn_done, copy_done = sem("fn_relu_done"), sem("fn_turn_done"), sem("fn_copy_done")
        product_done, add_done = sem("fn_product_done"), sem("fn_add_done")
        res_done = sem("fn_res_done")
        half = GROUPS // 2

        def loop(eng, body):
            with eng.Fori(0, half - 1) as i:
                for u in range(2):
                    body(2 * i + u, u, i, True)
            body(GROUPS - 2, 0, half - 1, True)
            body(GROUPS - 1, 1, half - 1, False)

        with nc.Block() as block:
            @block.sync
            def _(sp):
                def load(g, u):
                    for to, rows in ((x1, x1_rows), (z, z_rows)):
                        sp.dma_start(to[u][:, :, :], rows[bass.ds(g * (GT * P), GT * P), :].rearrange("(a p) c -> p a c", p=P)).then_inc(rows_in[u], 16)

                sp.dma_start(w[:, :], A["L1_gnn_Wfc"][3 * P:3 * P + F2, :]).then_inc(s_w, 16)
                load(0, 0)
                load(1, 1)
                for u in range(2):
                    sp.sem_inc(res_out[u], 32)
                with sp.Fori(0, half - 1) as i:
                    for u in range(2):
                        sp.wait_ge(res_done, 2 * i + u + 1)
                        take_waits(sp, held)
                        load(2 * i + u + 2, u)

            @block.scalar
            def _(act):
                flat = acc2[:, :, :].rearrange("p t c -> p (t c)")

                def relu(g, u):
                    act.wait_ge(turn_done, g + 1)
                    nc.scalar.activation(y[u][:, :, :].rearrange("p t c -> p (t c)"), flat[:, bass.ds(g * (GT * F2), GT * F2)],
                                         ACT.Relu).then_inc(relu_done, 1)

                def store(g, u):
                    full = GT - 1
                    act.wait_ge(res_done, g + 1)
                    r = g * (GT * P)
                    n = P if not isinstance(g, int) else min(P, NODES - g * GT * P - full * P)
                    take_waits(act, held)
                    act.dma_start(out[bass.ds(r, full * P), :].rearrange("(a p) c -> p a c", p=P), res[u][:, 0:full, :]).then_inc(res_out[u], 16)
                    act.dma_start(out[bass.ds(r + full * P, n), :], res[u][0:n, full, :]).then_inc(res_out[u], 16)

                def copy(g, u):
                    act.wait_ge(turn_done, g + 3)
                    act.wait_ge(product_done, PAIR * (g + 1))
                    nc.scalar.copy(yT[u][:, 0:FIRST, :], tp[:, 0, :, :])
                    nc.scalar.copy(yT[u][:, FIRST:GT, :], tp[:, 1, 0:GT - FIRST, :]).then_inc(copy_done, 1)

                act.sem_inc(turn_done, 2)
                act.sem_inc(product_done, 2 * PAIR)
                relu(0, 0)
                relu(1, 1)
                copy(0, 0)
                with act.Fori(0, half - 1) as i:
                    for v in range(2):
                        g = 2 * i + v + 1
                        relu(g + 1, v)
                        copy(g, 1 - v)
                        store(g - 1, v)
                copy(GROUPS - 1, 1)
                for u in range(2):
                    store(GROUPS - 2 + u, u)
                for u in range(2):
                    act.wait_ge(res_out[u], 32 * (half + 1))

            @block.vector
            def _(dve):
                def group(g, u, i, more):
                    dve.wait_ge(rows_in[u], 32 * (i + 1))
                    for k in range(PAIR):
                        dve.wait_ge(product_done, PAIR * g + k + 1 + 2 * PAIR)
                        tiles = z[u][:, 2 * k:min(2 * k + 2, GT), :].rearrange("p a c -> p (a c)")
                        nc.vector.tensor_tensor(tiles, tiles, op[:, k, 0:tiles.shape[1]], ALU.add).then_inc(add_done, 1)
                    dve.wait_ge(add_done, PAIR * (g + 2))
                    dve.wait_ge(res_out[u], 32 * (i + 1))
                    nc.vector.scalar_tensor_tensor(res[u][:, :, :], z[u][:, :, :], 0.0, x1[u][:, :, :], ALU.max, ALU.add).then_inc(res_done, 1)

                dve.sem_inc(add_done, PAIR)
                loop(dve, group)

            @block.tensor
            def _(pe):
                def turn(g, u):
                    pe.wait_ge(relu_done, g + 1)
                    pe.wait_ge(copy_done, g + 1)
                    take_waits(pe, held)
                    for a in range(GT):
                        last = nc.tensor.transpose(tp[:, a // FIRST, a % FIRST, :], y[u][:, a, :], ident[:, :])
                    last.then_inc(turn_done, 1)

                def group(g, u, i, more):
                    pe.wait_ge(copy_done, g + 2)
                    if more:
                        turn(g + 1, 1 - u)
                    for a in range(GT):
                        if a % 2 == 0:
                            pe.wait_ge(add_done, PAIR * g + a // 2 + 1)
                        last = nc.tensor.matmul(op[:, a // 2, a % 2 * FEAT:(a % 2 + 1) * FEAT], yT[u][:, a, :], w[:, :], start=True, stop=True)
                        if a % 2 or a == GT - 1:
                            last.then_inc(product_done, 1)

                pe.sem_inc(copy_done, 1)
                pe.wait_ge(s_w, 16)
                turn(0, 0)
                loop(pe, group)


_INS = ["x", "src", "dst", "edge_attr_3", "L0_gnn_W", "L0_gnn_a_src", "L0_gnn_a_dst", "L0_gnn_edge_W",
        "L0_gnn_edge_b", "L0_gnn_bias", "L1_gnn_W1", "L1_gnn_b1", "L1_gnn_g1", "L1_gnn_be1", "L1_gnn_W2",
        "L1_gnn_b2", "L1_gnn_g2", "L1_gnn_be2", "L1_gnn_Wfc", "L1_gnn_bfc"]


def kernel(**inputs):
    import concourse.bacc as _bacc
    from concourse.bass_utils import run_bass_kernel_spmd as _run

    nc = _bacc.Bacc("TRN2", target_bir_lowering=False, num_devices=1)
    arrays, A = {}, {}
    for name in _INS:
        a = np.ascontiguousarray(inputs[name])
        arrays[f"in_{name}"] = a
        A[name] = nc.dram_tensor(f"in_{name}", a.shape, mybir.dt.from_np(a.dtype), kind="ExternalInput").ap()
    out = nc.dram_tensor("out", (NODES, FEAT), F32, kind="ExternalOutput").ap()
    gnn(nc, A, out)
    return _run(nc, [arrays], core_ids=[0]).results[0]["out"]
```
